# Optimizing a Trainium2 kernel written in Bass

```python
import numpy as np
import jax
import jax.numpy as jnp

def _softmax(x, axis=-1):
    return jax.nn.softmax(x, axis=axis)

def _gelu(x):
    return jax.nn.gelu(x, approximate=True)

def _silu(x):
    return jax.nn.silu(x)

def _sigmoid(x):
    return jax.nn.sigmoid(x)

def _layernorm(x, axis=-1, eps=1e-05):
    m = jnp.mean(x, axis=axis, keepdims=True)
    v = jnp.var(x, axis=axis, keepdims=True)
    return (x - m) / jnp.sqrt(v + eps)

def _scatter_add(tgt, idx, src, axis=0):
    return tgt.at[idx].add(src)

def _segment_sum(src, seg, n):
    return jax.ops.segment_sum(src, seg, n)
kernel_name = 'mk_gnn_ffn_d1_gnn_r8_d37eb0'

def setup_inputs(seed: int=0):
    np.random.seed(seed)
    _w = jnp.asarray

    def _rec_inputs():
        import jax
        import jax.numpy as jnp
        _gk = jax.random.key(seed)
        x = -0.0006008 + 1.001 * jax.random.normal(jax.random.fold_in(_gk, 1), (6250, 256), jnp.float32)
        src = jax.random.randint(jax.random.fold_in(_gk, 2), (100000,), 0, 6250, jnp.int32)
        dst = jax.random.randint(jax.random.fold_in(_gk, 3), (100000,), 0, 6250, jnp.int32)
        _o = jnp.argsort(dst, stable=True)
        src = src[_o]
        dst = dst[_o]
        return (x, src, dst)
    x, src, dst = _rec_inputs()

    def _L0_gnn_setup():
        import jax, jax.numpy as jnp
        import numpy as np
        EPS = 1e-05

        def _gcn_conv(x, W, row, col, n_nodes):
            xl = x @ W.T
            ones = jnp.ones(row.shape[0], dtype=x.dtype)
            deg = jax.ops.segment_sum(ones, col, num_segments=n_nodes)
            dis = jnp.where(deg > 0, deg ** (-0.5), 0.0).astype(x.dtype)
            norm = dis[row] * dis[col]
            msg = xl[row] * norm[:, None]
            return jax.ops.segment_sum(msg, col, num_segments=n_nodes)

        def _batchnorm(x, gamma, beta):
            m = jnp.mean(x, axis=0)
            v = jnp.mean((x - m) ** 2, axis=0)
            return (x - m) * jax.lax.rsqrt(v + EPS) * gamma + beta
        key = jax.random.key(seed)
        k1, k2, k3, k4 = jax.random.split(key, 4)
        N, C, IC, E = (1250, 256, 512, 20000)
        x = jax.random.normal(k1, (N, C), dtype=jnp.float32)
        es = jax.random.randint(k2, (2, E), 0, N, dtype=jnp.int64)
        W1 = jax.random.normal(k3, (IC, C), dtype=jnp.float32) * (1.0 / np.sqrt(C))
        W2 = jax.random.normal(k4, (C, IC), dtype=jnp.float32) * (1.0 / np.sqrt(IC))
        g1 = jnp.ones((IC,), jnp.float32)
        b1 = jnp.zeros((IC,), jnp.float32)
        g2 = jnp.ones((C,), jnp.float32)
        b2 = jnp.zeros((C,), jnp.float32)
        return {'x': x, 'es': es, 'W1': W1, 'g1': g1, 'b1': b1, 'W2': W2, 'g2': g2, 'b2': b2}
    _L0_gnn_all = _L0_gnn_setup()
    _L0_gnn_in = {k: v for k, v in _L0_gnn_all.items() if k in ('W1', 'g1', 'b1', 'W2', 'g2', 'b2')}
    del _L0_gnn_all

    def _L0_ffn_setup():
        import jax, jax.numpy as jnp
        import numpy as np
        C = 256
        HID = 1024
        E = 8
        TEMP = 1.0
        key = jax.random.key(seed)
        ks = jax.random.split(key, 7)
        x = jax.random.normal(ks[0], (8, 2048, C), dtype=jnp.float32)
        W1 = jax.random.normal(ks[1], (C, HID), dtype=jnp.float32) * 0.02
        b1 = jnp.zeros((HID,), dtype=jnp.float32)
        Wg = jax.random.normal(ks[2], (HID, E), dtype=jnp.float32) * 0.02
        bg = jnp.zeros((E,), dtype=jnp.float32)
        Wd = jax.random.normal(ks[3], (E, HID, C), dtype=jnp.float32) * 0.02
        bd = jnp.zeros((E, C), dtype=jnp.float32)
        return {'x': x, 'W1': W1, 'b1': b1, 'Wg': Wg, 'bg': bg, 'Wd': Wd, 'bd': bd}
    _L0_ffn_all = _L0_ffn_setup()
    _L0_ffn_in = {k: v for k, v in _L0_ffn_all.items() if k in ('W1', 'b1', 'Wg', 'bg', 'Wd', 'bd')}
    del _L0_ffn_all
    return {'x': x, 'src': src, 'dst': dst, 'L0_gnn_W1': _L0_gnn_in['W1'], 'L0_gnn_g1': _L0_gnn_in['g1'], 'L0_gnn_b1': _L0_gnn_in['b1'], 'L0_gnn_W2': _L0_gnn_in['W2'], 'L0_gnn_g2': _L0_gnn_in['g2'], 'L0_gnn_b2': _L0_gnn_in['b2'], 'L0_ffn_W1': _L0_ffn_in['W1'], 'L0_ffn_b1': _L0_ffn_in['b1'], 'L0_ffn_Wg': _L0_ffn_in['Wg'], 'L0_ffn_bg': _L0_ffn_in['bg'], 'L0_ffn_Wd': _L0_ffn_in['Wd'], 'L0_ffn_bd': _L0_ffn_in['bd']}

def reference(x, src, dst, L0_gnn_W1, L0_gnn_g1, L0_gnn_b1, L0_gnn_W2, L0_gnn_g2, L0_gnn_b2, L0_ffn_W1, L0_ffn_b1, L0_ffn_Wg, L0_ffn_bg, L0_ffn_Wd, L0_ffn_bd):
    import jax
    import jax.numpy as jnp

    def _L0_gnn_ref(x, es, W1, g1, b1, W2, g2, b2):
        import jax, jax.numpy as jnp
        import numpy as np
        EPS = 1e-05

        def _gcn_conv(x, W, row, col, n_nodes):
            xl = x @ W.T
            ones = jnp.ones(row.shape[0], dtype=x.dtype)
            deg = jax.ops.segment_sum(ones, col, num_segments=n_nodes)
            dis = jnp.where(deg > 0, deg ** (-0.5), 0.0).astype(x.dtype)
            norm = dis[row] * dis[col]
            msg = xl[row] * norm[:, None]
            return jax.ops.segment_sum(msg, col, num_segments=n_nodes)

        def _batchnorm(x, gamma, beta):
            m = jnp.mean(x, axis=0)
            v = jnp.mean((x - m) ** 2, axis=0)
            return (x - m) * jax.lax.rsqrt(v + EPS) * gamma + beta
        n_nodes = x.shape[0]
        loops = jnp.arange(n_nodes, dtype=es.dtype)
        row = jnp.concatenate([es[0], loops])
        col = jnp.concatenate([es[1], loops])
        res = x
        h = _gcn_conv(x, W1, row, col, n_nodes)
        h = jax.nn.relu(_batchnorm(h, g1, b1))
        h = _gcn_conv(h, W2, row, col, n_nodes)
        h = _batchnorm(h, g2, b2)
        return jax.nn.relu(h + res)

    def _L0_ffn_ref(x, W1, b1, Wg, bg, Wd, bd):
        import jax, jax.numpy as jnp
        import numpy as np
        C = 256
        HID = 1024
        E = 8
        TEMP = 1.0
        orig_shape = x.shape
        xf = x.reshape(-1, orig_shape[-1])
        H = jax.nn.gelu(xf @ W1 + b1, approximate=False)
        probs = jax.nn.softmax((H @ Wg + bg) / TEMP, axis=-1)
        assign = jnp.argmax(probs, axis=-1)
        out = jnp.zeros_like(xf)
        for e in range(Wd.shape[0]):
            y = H @ Wd[e] + bd[e]
            sel = (assign == e)[:, None]
            out = out + jnp.where(sel, probs[:, e:e + 1] * y, 0.0)
        return out.reshape(orig_shape)
    edge_index = jnp.stack([src, dst])
    x = x + _L0_gnn_ref(_layernorm(x, axis=-1), edge_index, L0_gnn_W1, L0_gnn_g1, L0_gnn_b1, L0_gnn_W2, L0_gnn_g2, L0_gnn_b2)
    x = x + _L0_ffn_ref(_layernorm(x, axis=-1)[None], L0_ffn_W1, L0_ffn_b1, L0_ffn_Wg, L0_ffn_bg, L0_ffn_Wd, L0_ffn_bd)[0]
    return x

_drawn_inputs = setup_inputs


def setup_inputs(seed=0):
    import zlib

    import numpy as np

    out = dict(_drawn_inputs(seed))
    spreads = {'L0_gnn_g1': (1.0, 0.2),
     'L0_gnn_b1': (0.0, 0.1),
     'L0_gnn_g2': (1.0, 0.2),
     'L0_gnn_b2': (0.0, 0.1),
     'L0_ffn_b1': (0.0, 0.8),
     'L0_ffn_bg': (0.0, 0.68),
     'L0_ffn_bd': (0.0, 0.8)}
    factors = {'L0_ffn_W1': 4.618, 'L0_ffn_Wg': 4.942, 'L0_ffn_Wd': 5.668}
    for name, (base, spread) in spreads.items():
        noise = np.random.default_rng([zlib.crc32(name.encode()), seed]).standard_normal(out[name].shape)
        drawn = base * np.exp(spread * noise) if base else spread * noise
        out[name] = jnp.asarray(drawn.astype(out[name].dtype))
    for name, factor in factors.items():
        out[name] = (out[name] * factor).astype(out[name].dtype)
    return out
```

```python
from contextlib import ExitStack

import concourse.bass as bass
from concourse import mybir

F32, F16, I32, F32R = mybir.dt.float32, mybir.dt.float16, mybir.dt.int32, mybir.dt.float32r
ACT = mybir.ActivationFunctionType
ALU = mybir.AluOpType
AX = mybir.AxisListType

P = 128
N, C, IC, HID, NEXP, NE = 6250, 256, 512, 1024, 8, 100000
EPS = 1e-5
NT = -(-N // P)
NP_ = NT * P
LAST = N - (NT - 1) * P
KC, KI, KH = C // P, IC // P, HID // P
WIN = 5
NW = N // WIN
SB = 250
NSB = N // SB
WPS = SB // WIN
GRP = 2
GPS = WPS // GRP
WP, WJ = 125, 10
KEYS = WIN * NT
RING = 5
NTE = -(-NE // P)
ROW = 8
NROWS = 12512
EPAD = 783 * P
PADROW = NE // ROW
FAR = 1 << 20
T1SCALE = 2048.0


def gnn_ffn_kernel(nc, x, src, dst, w1t, g1, b1, w2t, g2, b2, fw1, fb1, fwg, fbg, fwd, fbd, out, upto=99):
    with ExitStack() as ctx:
        m = Names()
        m.sem = lambda name: ctx.enter_context(nc.semaphore(name))
        base = 16512

        def at(name, off, shape, dt):
            return nc.alloc_sbuf_tensor_at(name, shape, dt, offset=base + off)

        R1, R2, R3, R4, R5 = 0, 52224, 102400, 152576, 177664
        END = 229368 - base
        m.at = at
        m.r1, m.r2, m.r3, m.r4 = R1, R2, R3, R4
        m.x = at("x_sb", R3, [P, NT, C], F32)
        m.table1 = at("table1", R1, [P, NT, 2 * C], F16)
        m.table2 = at("table2", R2, [P, NT, 2 * C], F16)
        m.agg1 = at("agg1", R2, [P, KC, NP_], F32)
        m.agg2 = at("agg2", R1, [P, KC, NP_], F32)
        m.adj = at("adj", R3, [P, 2, NT, SB], F16)
        m.rows = at("rows", R1, [P, NT, RW], F32)
        m.disB = at("disB", R4, [P, NP_], F32)
        m.h01 = at("h01", R1, [P, 2, NP_], F32)
        m.h23 = at("h23", R3, [P, 2, NP_], F32)
        m.end = END
        take = Place(m, R5)

        def small(name, shape, dt):
            return take(name, [P, *shape], dt)

        m.key = small("key", [WJ, WP], F32)
        m.rem = small("rem", [WJ, WP], F32)
        m.id32 = small("id32", [P], F32)
        m.id16 = small("id16", [P], F16)
        m.iota_r = small("iota_r", [P], F16)
        m.iota_k = small("iota_k", [KEYS + 1], F16)
        m.ones = small("ones", [P], F32)
        m.disP = small("disP", [NT], F32)
        m.mean = small("mean", [NT], F32)
        m.rstd = small("rstd", [NT], F32)
        m.levels = small("levels", [1], I32)
        m.row0 = small("row0", [WJ], F32)
        m.w5 = small("w5", [WJ], F32)
        m.step16 = small("step16", [1], F32)
        m.bn_g1 = small("bn_g1", [KI], F32)
        m.bn_b1 = small("bn_b1", [KI], F32)
        m.bn_g2 = small("bn_g2", [KC], F32)
        m.bn_b2 = small("bn_b2", [KC], F32)
        m.aff_a1 = small("aff_a1", [KI], F32)
        m.aff_b1 = small("aff_b1", [KI], F32)
        m.scale2 = small("scale2", [1], F32)
        m.sc_col = small("sc_col", [8], F32)
        m.alpha = small("alpha", [KH], F32)
        m.beta = small("beta", [KH], F32)
        m.inv_g = small("inv_g", [1], F32)
        m.b1f = small("b1f", [KH], F32)
        m.reg_base = small("reg_base", [NEXP], F32)
        m.tile_row = small("tile_row", [64], I32)
        m.tile_exp = small("tile_exp", [64], I32)
        m.stats1 = small("stats1", [KI, NSB, 6], F32)
        m.work = take.next
        m.ps = ctx.enter_context(nc.psum_tensor("ps", [P, 8, 512], F32))
        m.src_pad = nc.dram_tensor("src_pad", [EPAD], I32, kind="Internal").ap()
        m.dst_pad = nc.dram_tensor("dst_pad", [EPAD], I32, kind="Internal").ap()
        m.edge_rows = nc.dram_tensor("edge_rows", [NROWS, 2 * P], I32, kind="Internal").ap()
        m.first_dram = nc.dram_tensor("first_dram", [(NT + 1) * P], F32, kind="Internal").ap()
        m.dis_dram = nc.dram_tensor("dis_dram", [NP_], F32, kind="Internal").ap()
        m.sorted_rows = nc.dram_tensor("sorted_rows", [(NEXP + 1) * REG, RW], F32, kind="Internal").ap()
        m.x1_dram = nc.dram_tensor("x1_dram", [NP_, C], F32, kind="Internal").ap()
        m.s_chain, m.chained = m.sem("chain"), 0
        args = Names()
        args.x, args.src, args.dst, args.out = x, src, dst, out
        args.w1t, args.g1, args.b1, args.w2t, args.g2, args.b2 = w1t, g1, b1, w2t, g2, b2
        args.fw1, args.fb1, args.fwg, args.fbg, args.fwd, args.fbd = fw1, fb1, fwg, fbg, fwd, fbd
        m.s_align = [m.sem(f"align_{n}") for n in ("dve", "rowi", "edges", "keyw", "keyt", "spare")]
        prepare(nc, m, args)
        if upto < 2: return m
        ffn_scales(nc, m, args)
        build_table1(nc, m, args)
        m.agg = aggregate_tensors(m)
        aggregate(nc, m, 0, m.table1, m.agg1)
        if upto < 3: return m
        linear1(nc, m, args)
        if upto < 4: return m
        linear2(nc, m, args)
        aggregate(nc, m, 1, m.table2, m.agg2)
        if upto < 5: return m
        finish_gnn(nc, m, args)
        if upto < 6: return m
        ffn(nc, m, args)
        return m


class Names:
    pass


class Place:

    def __init__(self, m, start):
        self.m, self.next = m, start

    def __call__(self, name, shape, dt):
        size = mybir.dt.size(dt)
        for n in shape[1:]:
            size *= n
        t = self.m.at(name, self.next, shape, dt)
        self.next += -(-size // 32) * 32
        assert self.next <= self.m.end, (name, self.next - self.m.end)
        return t


def align_edges(m, t, eng, name, runs, level0):
    if name == "vector":
        if level0:
            eng.tensor_copy(t.rowf[:, :], m.row0[:WP, :]).then_inc(t.s_dve, 1)
        else:
            eng.tensor_scalar(t.rowf[:, :], m.row0[:WP, :], m.step16[:WP, 0:1], float(PADROW), ALU.add, ALU.min).then_inc(t.s_dve, 1)
        eng.wait_ge(t.s_dve, runs * 6 + 1)
        eng.tensor_copy(t.rowi[:, :], t.rowf[:, :]).then_inc(t.s_rowi, 1)
        eng.wait_ge(t.s_edges, (runs + 1) * 16 * WJ)
        eng.wait_ge(t.s_spare, runs + 1)
        dstv = t.edges[:, :, P:2 * P]
        srcv = t.edges[:, :, 0:P]
        eng.tensor_tensor(t.dl[:, :, :], dstv, m.w5[:WP, :].unsqueeze(2).to_broadcast([WP, WJ, P]), ALU.subtract).then_inc(t.s_dve, 1)
        eng.tensor_scalar(t.chunk[:, :, :], srcv, 7, None, ALU.arith_shift_right).then_inc(t.s_dve, 1)
        eng.tensor_scalar(t.lowi[:, :, :], srcv, P - 1, None, ALU.bitwise_and).then_inc(t.s_dve, 1)
        eng.wait_ge(t.s_dve, runs * 6 + 4)
        eng.scalar_tensor_tensor(t.keyw[:, :, :], t.dl[:, :, :], float(NT), t.chunk[:, :, :], ALU.mult, ALU.add).then_inc(t.s_keyw, 1)
        eng.tensor_copy(t.lowf[:, :, :], t.lowi[:, :, :]).then_inc(t.s_keyw, 1)
        for b in range(5):
            eng.wait_ge(t.s_keyt, runs * 5 + b + 1)
            for q in range(4):
                k = 4 * b + q
                dest = (m.key if k < WJ else m.rem)[:, k % WJ, :]
                last = eng.tensor_copy(dest, m.ps[:, b, q * WP:(q + 1) * WP])
            if b == 4:
                last.then_inc(t.s_dve, 2)
        eng.wait_ge(t.s_dve, runs * 6 + 6)
    elif name == "gpsimd":
        eng.wait_ge(t.s_rowi, runs + 1)
        eng.tensor_tensor(t.spare[:, :], t.rowf[:, :], t.rowf[:, :], ALU.add).then_inc(t.s_spare, 1)
        for j in range(WJ):
            eng.indirect_dma_start(t.edges[:, j, :], None, m.edge_rows,
                                   bass.IndirectOffsetOnAxis(ap=t.rowi[:, j:j + 1], axis=0)).then_inc(t.s_edges, 16)
    elif name == "tensor":
        eng.wait_ge(t.s_keyw, runs * 2 + 2)
        for k in range(2 * WJ):
            b, q = divmod(k, 4)
            from_ = (t.keyw if k < WJ else t.lowf)[:, k % WJ, :]
            ins = eng.transpose(m.ps[:, b, q * WP:(q + 1) * WP], from_, m.id32[:WP, :WP])
            if q == 3:
                ins.then_inc(t.s_keyt, 1)


def align_tensors(m, tag, off):
    t = Names()
    t.s_dve, t.s_rowi, t.s_edges, t.s_keyw, t.s_keyt, t.s_spare = m.s_align
    t.edges = m.at(f"edges_{tag}", off, [WP, WJ, 2 * P], I32)
    t.dl = m.at(f"dl_{tag}", off + 10240, [WP, WJ, P], F32)
    t.chunk = m.at(f"chunk_{tag}", off + 15360, [WP, WJ, P], I32)
    t.lowi = m.at(f"lowi_{tag}", off + 20480, [WP, WJ, P], I32)
    t.keyw = m.at(f"keyw_{tag}", off + 25600, [WP, WJ, P], F32)
    t.lowf = m.at(f"lowf_{tag}", off + 30720, [WP, WJ, P], F32)
    t.rowf = m.at(f"rowf_{tag}", off + 35840, [WP, WJ], F32)
    t.spare = m.at(f"spare_{tag}", off + 35968, [WP, WJ], F32)
    t.rowi = m.at(f"rowi_{tag}", off + 35904, [WP, WJ], I32)
    return t


def prepare(nc, m, a):
    NHALF = NTE // 2
    off = m.r4
    head_i = m.at("head_i", off, [1, NTE], I32)
    head_f = m.at("head_f", off + 3136, [1, NTE], F32)
    heads = m.at("heads", off + 6272, [P, NTE], F32)
    junk = m.at("junk", off + 9408, [P, 2, NTE], F16)
    near = m.at("near", 0, [P, NT, P], I32)
    less = m.at("less", m.r2, [P, NT, P], F16)
    take = Place(m, m.work)
    padt = take("padt", [1, 2, EPAD - NE], I32)
    far_f = take("far_f", [1, P], F32)
    nodes, tcnt, rowf = take("nodes", [P, NT], F32), take("tcnt", [P, NT], F32), take("nrowf", [P, NT], F32)
    rowi = take("nrowi", [P, NT], I32)
    cnt, first = take("cnt", [P, NT], F32), take("first", [P, NT], F32)
    firstT, nextT = take("firstT", [NT, P], F32), take("nextT", [NT, P], F32)
    degT, disT = take("degT", [NT, P], F32), take("disT", [NT, P], F32)
    mhalfT = take("mhalfT", [P, P], F32)
    wa, wb = take("win_a", [WP, 5 * WJ], F32), take("win_b", [WP, 5 * WJ], F32)
    wi, wi8 = take("win_i", [WP, WJ], I32), take("win_i8", [WP, WJ], I32)
    wn, wm = take("win_n", [WP, WJ], F32), take("win_m", [WP, 1], F32)
    lv, lvi = take("lv", [1, 4], F32), take("lvi", [1, 4], I32)
    st, mv, vare = take("ln_st", [P, NT, 6], F32), take("ln_mv", [P, NT, 2], F32), take("vare", [P, NT], F32)
    t = align_tensors(m, "pa", m.r2 + 12544)
    S = m.sem
    s_x, s_heads, s_pads, s_pad_mem, s_copy, s_rows = S("a_x"), S("a_heads"), S("a_pads"), S("a_pad_mem"), S("a_copy"), S("a_rows")
    s_const, s_headf, s_headp, s_nrow, s_near, s_first, s_firstT = S("a_const"), S("a_headf"), S("a_headp"), S("a_nrow"), S("a_near"), S("a_first"), S("a_firstT")
    s_firstS, s_fd, s_next, s_deg, s_dis, s_disd, s_disB = S("a_firstS"), S("a_fd"), S("a_next"), S("a_deg"), S("a_dis"), S("a_disd"), S("a_disB")
    s_disT, s_wm, s_wmT, s_vare, s_rstd, s_par, s_xtail = S("a_disT"), S("a_wm"), S("a_wmT"), S("a_vare"), S("a_rstd"), S("a_par"), S("a_xtail")

    with nc.Block() as block:
        @block.sync
        def _(sp):
            with nc.allow_non_contiguous_dma("the first dst of each edge tile"):
                sp.dma_start(head_i[0:1, :], bass.AP(a.dst.tensor, 0, [[P, 1], [P, NTE]])).then_inc(s_heads, 16)
            sp.dma_start(m.dst_pad[0:NE], a.dst).then_inc(s_copy, 16)
            sp.dma_start(m.src_pad[0:NE], a.src).then_inc(s_copy, 16)
            sp.wait_ge(s_pad_mem, 1)
            sp.dma_start(m.src_pad[NE:EPAD].rearrange("(a n) -> a n", a=1), padt[0:1, 0, :]).then_inc(s_pads, 16)
            sp.dma_start(m.dst_pad[NE:EPAD].rearrange("(a n) -> a n", a=1), padt[0:1, 1, :]).then_inc(s_pads, 16)
            sp.dma_start(m.first_dram[NP_:NP_ + P].rearrange("(a n) -> a n", a=1), far_f[0:1, :]).then_inc(s_pads, 16)
            for i in range(6):
                sp.dma_start(m.x[:, 8 * i:8 * i + 8, :],
                             a.x[1024 * i:1024 * (i + 1), :].rearrange("(t p) c -> p t c", p=P)).then_inc(s_x, 16)
            sp.wait_ge(s_xtail, 1)
            sp.dma_start(m.x[:LAST, NT - 1, :], a.x[(NT - 1) * P:N, :]).then_inc(s_x, 16)
            sp.wait_ge(s_copy, 32)
            sp.wait_ge(s_pads, 48)
            for k, pad in enumerate((m.src_pad, m.dst_pad)):
                sp.dma_start(m.edge_rows[:, k * P:(k + 1) * P],
                             bass.AP(pad.tensor, 0, [[ROW, NROWS], [1, P]])).then_inc(s_rows, 16)
            with nc.allow_non_contiguous_dma("batch norm's parameters to partitions"):
                sp.dma_start(m.bn_g1[:, :], a.g1.rearrange("(f p) -> p f", p=P)).then_inc(s_par, 16)
                sp.dma_start(m.bn_b1[:, :], a.b1.rearrange("(f p) -> p f", p=P)).then_inc(s_par, 16)
                sp.dma_start(m.bn_g2[:, :], a.g2.rearrange("(f p) -> p f", p=P)).then_inc(s_par, 16)
                sp.dma_start(m.bn_b2[:, :], a.b2.rearrange("(f p) -> p f", p=P)).then_inc(s_par, 16)
            sp.wait_ge(s_firstS, 1)
            sp.dma_start(m.first_dram[0:NP_].rearrange("(t p) -> t p", p=P), firstT[:, :]).then_inc(s_fd, 16)
            sp.wait_ge(s_fd, 16)
            sp.dma_start(nextT[:, :], m.first_dram[1:NP_ + 1].rearrange("(t p) -> t p", p=P)).then_inc(s_next, 16)
            sp.dma_start(wa[:, :], m.first_dram[0:N].rearrange("(p w) -> p w", p=WP)).then_inc(s_next, 16)
            sp.dma_start(wb[:, :], m.first_dram[WIN:N + WIN].rearrange("(p w) -> p w", p=WP)).then_inc(s_next, 16)
            sp.wait_ge(s_dis, 1)
            sp.dma_start(m.dis_dram.rearrange("(t p) -> t p", p=P), disT[:, :]).then_inc(s_disd, 16)
            sp.wait_ge(s_disd, 16)
            sp.dma_start(m.disB[:, :], bass.AP(m.dis_dram.tensor, 0, [[0, P], [1, NP_]])).then_inc(s_disB, 16)
            sp.wait_ge(s_par, 64)
            sp.wait_ge(s_disB, 16)

        @block.gpsimd
        def _(pool):
            pool.iota(nodes[:, :], [[P, NT]], base=0, channel_multiplier=1, allow_small_or_imprecise_dtypes=True).then_inc(s_const, 1)
            pool.memset(m.id32[:, :], 0.0).then_inc(s_const, 1)
            pool.memset(m.id16[:, :], 0.0).then_inc(s_const, 1)
            pool.memset(mhalfT[:, :], -0.5).then_inc(s_const, 1)
            pool.wait_ge(s_const, 4)
            for mat in (m.id32, m.id16):
                pool.affine_select(out=mat[:, :], in_=mat[:, :], compare_op=ALU.not_equal, fill=1.0,
                                   base=0, pattern=[[-1, P]], channel_multiplier=1).then_inc(s_const, 1)
            pool.iota(m.iota_r[:, :], [[1, P]], base=0, channel_multiplier=0, allow_small_or_imprecise_dtypes=True).then_inc(s_const, 1)
            pool.iota(m.iota_k[:, :], [[1, KEYS + 1]], base=0, channel_multiplier=0, allow_small_or_imprecise_dtypes=True).then_inc(s_const, 1)
            pool.iota(m.w5[:WP, :], [[WIN, WJ]], base=0, channel_multiplier=WIN * WJ, allow_small_or_imprecise_dtypes=True).then_inc(s_const, 1)
            pool.wait_ge(s_nrow, 1)
            pool.wait_ge(s_copy, 32)
            pool.wait_ge(s_pads, 48)
            for i in range(NT):
                pool.indirect_dma_start(near[:, i, :], None, m.dst_pad.rearrange("(t p) -> t p", p=P),
                                        bass.IndirectOffsetOnAxis(ap=rowi[:, i:i + 1], axis=0)).then_inc(s_near, 16)
            pool.wait_ge(s_vare, 1)
            pool.tensor_tensor(m.rstd[:, :], vare[:, :], mhalfT[:, :NT], ALU.pow).then_inc(s_rstd, 1)
            pool.wait_ge(s_deg, 1)
            pool.tensor_tensor(disT[:, :], degT[:, :], mhalfT[:NT, :], ALU.pow).then_inc(s_dis, 1)
            pool.wait_ge(s_rows, 32)
            align_edges(m, t, pool, "gpsimd", 0, True)

        @block.tensor
        def _(pe):
            pe.wait_ge(s_headf, 2)
            for k in range(2):
                pe.matmul(m.ps[:, k, 0:NHALF], m.ones[0:1, :], head_f[0:1, k * NHALF:(k + 1) * NHALF],
                          start=True, stop=True).then_inc(s_headp, 1)
            pe.wait_ge(s_const, 6)
            pe.wait_ge(s_first, 1)
            pe.transpose(m.ps[:NT, 2, 0:P], first[:, :], m.id32[:, :]).then_inc(s_firstT, 1)
            pe.wait_ge(s_wm, 1)
            pe.transpose(m.ps[:1, 3, 0:WP], wm[:, :], m.id32[:WP, :WP]).then_inc(s_wmT, 1)
            pe.wait_ge(s_dis, 1)
            pe.transpose(m.ps[:, 4, 0:NT], disT[:, :], m.id32[:NT, :NT]).then_inc(s_disT, 1)
            align_edges(m, t, pe, "tensor", 0, True)

        @block.vector
        def _(dve):
            link = chain_on(m, dve)
            dve.memset(m.ones[:, :], 1.0).then_inc(s_headf, 1)
            link(dve.memset(far_f[:, :], float(NE)))
            link(dve.memset(padt[:, 0, :], 0))
            dve.memset(padt[:, 1, :], FAR).then_inc(s_pad_mem, 1)
            dve.memset(m.x[:, NT - 1, :], 0.0).then_inc(s_xtail, 1)
            link(dve.memset(m.step16[:, :], 0.0))
            dve.wait_ge(s_heads, 16)
            dve.tensor_copy(head_f[:, :], head_i[:, :]).then_inc(s_headf, 1)
            dve.wait_ge(s_headp, 2)
            link(dve.tensor_copy(heads[:, :].rearrange("p (k n) -> p k n", k=2), m.ps[:, 0:2, 0:NHALF]))
            dve.wait_ge(s_const, 1)
            for i in range(NT):
                if i >= 2:
                    dve.wait_ge(m.s_chain, m.chained - 1)
                m.chained += 1
                dve.tensor_scalar(junk[:, i % 2, :], heads[:, :], nodes[:, i:i + 1], None, ALU.is_lt, ALU.add,
                                  accum_out=tcnt[:, i:i + 1]).then_inc(m.s_chain, 1)
            dve.wait_ge(m.s_chain, m.chained)
            link(dve.tensor_scalar(rowf[:, :], tcnt[:, :], -1.0, 0.0, ALU.add, ALU.max))
            dve.tensor_copy(rowi[:, :], rowf[:, :]).then_inc(s_nrow, 1)
            dve.wait_ge(s_x, 16 * 7)
            for i in range(NT):
                last = dve.bn_stats(st[:, i, :], m.x[:, i, :])
            link(last)
            for i in range(NT):
                last = dve.bn_aggr(mv[:, i, :], st[:, i, :])
            link(last)
            dve.tensor_copy(m.mean[:, :], mv[:, :, 0])
            dve.tensor_scalar(vare[:, :], mv[:, :, 1], EPS, None, ALU.add).then_inc(s_vare, 1)
            dve.wait_ge(s_near, 16 * NT)
            link(dve.tensor_tensor(less[:, :, :], near[:, :, :], nodes[:, :].unsqueeze(2).to_broadcast([P, NT, P]), ALU.is_lt))
            link(dve.tensor_reduce(cnt[:, :], less[:, :, :], AX.X, ALU.add))
            dve.scalar_tensor_tensor(first[:, :], rowf[:, :], float(P), cnt[:, :], ALU.mult, ALU.add).then_inc(s_first, 1)
            dve.wait_ge(s_firstT, 1)
            dve.tensor_copy(firstT[:, :], m.ps[:NT, 2, 0:P]).then_inc(s_firstS, 1)
            dve.wait_ge(s_next, 48)
            link(dve.tensor_tensor(degT[:, :], nextT[:, :], firstT[:, :], ALU.subtract))
            dve.tensor_scalar(degT[:, :], degT[:, :], 1.0, None, ALU.add).then_inc(s_deg, 1)
            link(dve.tensor_copy(wi[:, :], wa[:, 0::WIN]))
            link(dve.tensor_scalar(wi8[:, :], wi[:, :], 3, None, ALU.arith_shift_right))
            link(dve.tensor_copy(m.row0[:WP, :], wi8[:, :]))
            link(dve.scalar_tensor_tensor(wn[:, :], m.row0[:WP, :], float(-ROW), wb[:, 0::WIN], ALU.mult, ALU.add))
            dve.tensor_reduce(wm[:, :], wn[:, :], AX.X, ALU.max).then_inc(s_wm, 1)
            dve.wait_ge(s_wmT, 1)
            link(dve.tensor_reduce(lv[:, 0:1], m.ps[:1, 3, 0:WP], AX.X, ALU.max))
            link(dve.tensor_scalar(lv[:, 1:2], lv[:, 0:1], float(P - 1), float(P), ALU.add, ALU.max))
            link(dve.tensor_copy(lvi[:, 0:1], lv[:, 1:2]))
            link(dve.tensor_scalar(m.levels[0:1, :], lvi[:, 0:1], 7, None, ALU.arith_shift_right))
            dve.wait_ge(s_disT, 1)
            link(dve.tensor_copy(m.disP[:, :], m.ps[:, 4, 0:NT]))
            dve.wait_ge(s_rstd, 1)
            align_edges(m, t, dve, "vector", 0, True)


def build_table1(nc, m, a):
    scale = m.at("t1_scale", m.work, [P, NT], F32)
    xs, xs32 = m.x, m.x
    s_scale, s_xs, s_hi, s_lo = m.sem("b_scale"), m.sem("b_xs"), m.sem("b_hi"), m.sem("b_lo")
    groups = [(4 * g, min(4, NT - 4 * g)) for g in range(-(-NT // 4))]
    def low_half(dve, g):
        t0, k = groups[g]
        dve.wait_ge(s_hi, g + 1)
        dve.tensor_tensor(m.table1[:, t0:t0 + k, C:], xs[:, t0:t0 + k, :], m.table1[:, t0:t0 + k, :C],
                          ALU.subtract).then_inc(s_lo, 1)

    with nc.Block() as block:
        @block.vector
        def _(dve):
            dve.scalar_tensor_tensor(scale[:, :], m.rstd[:, :], T1SCALE, m.disP[:, :], ALU.mult, ALU.mult).then_inc(s_scale, 1)
            dve.wait_ge(s_scale, 1)
            for g, (t0, k) in enumerate(groups):
                for i in range(t0, t0 + k):
                    last = dve.tensor_scalar(xs[:, i, :], m.x[:, i, :], m.mean[:, i:i + 1], scale[:, i:i + 1],
                                             ALU.subtract, ALU.mult)
                last.then_inc(s_xs, 1)
                if g >= 1:
                    low_half(dve, g - 1)
            low_half(dve, len(groups) - 1)

        @block.scalar
        def _(act):
            for g, (t0, k) in enumerate(groups):
                act.wait_ge(s_xs, g + 1)
                act.activation(m.table1[:, t0:t0 + k, :C], xs[:, t0:t0 + k, :], ACT.Copy).then_inc(s_hi, 1)
    self_loops(nc, m, "l1", m.table1, m.agg1)


def self_loops(nc, m, tag, table, agg):
    s_tr, s_ev = m.sem(f"{tag}_tr"), m.sem(f"{tag}_ev")
    groups = [(4 * g, min(4, NT - 4 * g)) for g in range(-(-NT // 4))]
    with nc.Block() as block:
        @block.tensor
        def _(pe):
            for g, (t0, k) in enumerate(groups):
                for h in range(KC):
                    n = g * KC + h
                    if n >= 8:
                        pe.wait_ge(s_ev, n - 7)
                    for i in range(k):
                        for half in range(2):
                            last = pe.matmul(m.ps[:, n % 8, i * P:(i + 1) * P],
                                             table[:, t0 + i, half * C + h * P:half * C + (h + 1) * P], m.id16[:, :],
                                             start=half == 0, stop=half == 1)
                    last.then_inc(s_tr, 1)

        @block.scalar
        def _(act):
            for g, (t0, k) in enumerate(groups):
                for h in range(KC):
                    n = g * KC + h
                    act.wait_ge(s_tr, n + 1)
                    act.activation(agg[:, h, t0 * P:(t0 + k) * P], m.ps[:, n % 8, 0:k * P], ACT.Copy).then_inc(s_ev, 1)


def aggregate_tensors(m):
    take = Place(m, m.work)
    g = Names()
    g.oh_r, g.oh_k = take("oh_r", [P, RING, GRP, P], F16), take("oh_k", [P, RING, GRP, KEYS + 1], F16)
    g.col_k, g.col_r = take("col_k", [P, 2, WPS], F32), take("col_r", [P, 2, WPS], F32)
    g.align = align_tensors(m, "agg", m.r3)
    g.s_col = m.sem("agg_col")
    g.s_oh = m.sem("agg_oh")
    g.s_used = m.sem("agg_used")
    g.s_adj = m.sem("agg_adj")
    g.s_half = m.sem("agg_half")
    g.s_evac = m.sem("agg_evac")
    g.s_go = m.sem("agg_go")
    g.s_step = m.sem("agg_step")
    return g


def aggregate(nc, m, second, table, agg):
    a = m.agg
    oh_r, oh_k, col_k, col_r, t = a.oh_r, a.oh_k, a.col_k, a.col_r, a.align
    s_col, s_oh, s_used, s_adj, s_half, s_evac = a.s_col, a.s_oh, a.s_used, a.s_adj, a.s_half, a.s_evac
    EVERY = 6

    def walk(eng, name, head, step, tail):
        nlev = eng.value_load(m.levels[0:1, 0:1], min_val=1, max_val=NTE + 1)
        with eng.Fori(0, nlev) as level:
            run = eng.snap(level + nlev) if second else level
            with eng.If(nlev > 1):
                between_levels(eng, name, run)
            b = eng.snap(run * NSB)
            head(eng, b)
            with eng.Fori(0, (NSB - 1) // 2) as k:
                bb = eng.snap(b + 2 * k)
                step(eng, bb, 2 * k, 0)
                step(eng, bb + 1, 2 * k + 1, 1)
            tail(eng, b)

    def between_levels(eng, name, run):
        align_edges(m, t, eng, name, run + 1, False)
        if name == "vector":
            eng.tensor_scalar(m.step16[:, :], m.step16[:, :], float(P // ROW), None, ALU.add).then_inc(a.s_step, 1)
            eng.wait_ge(a.s_step, run + 1)
            eng.sem_inc(a.s_go, 1)
        elif name == "tensor":
            eng.wait_ge(a.s_go, run + 1)

    def columns(dve, par, s):
        for col, whole in ((col_k, m.key), (col_r, m.rem)):
            last = dve.tensor_copy(col[:, par, :].rearrange("e (p j) -> e p j", j=WJ),
                                   whole[:, :, bass.ds(s * (WPS // WJ), WPS // WJ)].rearrange("e j p -> e p j"))
        last.then_inc(s_col, 1)

    def one_hots(dve, b, par, g):
        dve.wait_ge(s_used, b * GPS + (g + 1))
        for i in range(GRP):
            window = GRP * g + i
            dve.tensor_scalar(oh_r[:, g % RING, i, :], m.iota_r[:, :], col_r[:, par, window:window + 1], None, ALU.is_equal)
            last = dve.tensor_scalar(oh_k[:, g % RING, i, :], m.iota_k[:, :], col_k[:, par, window:window + 1], None, ALU.is_equal)
        last.then_inc(s_oh, 1)

    def add_half(dve, b, s, h):
        dve.wait_ge(s_half, b * KC + (KC + h + 1))
        dve.tensor_tensor(agg[:, h, bass.ds(s * SB, SB)], agg[:, h, bass.ds(s * SB, SB)],
                          m.ps[:, RING + h, 0:SB], ALU.add).then_inc(s_evac, 1)

    def v_head(dve, b):
        columns(dve, 0, 0)
        dve.wait_ge(s_col, b + 1)
        for g in range(GPS):
            one_hots(dve, b, 0, g)

    def v_step(dve, b, s, par):
        columns(dve, 1 - par, s + 1)
        dve.wait_ge(s_col, b + 2)
        for g in range(GPS):
            one_hots(dve, b + 1, 1 - par, g)
            if g == 16:
                add_half(dve, b, s, 0)
        add_half(dve, b, s, 1)

    def v_tail(dve, b):
        add_half(dve, b + (NSB - 1), NSB - 1, 0)
        add_half(dve, b + (NSB - 1), NSB - 1, 1)
        dve.wait_ge(s_evac, b * KC + (NSB + 1) * KC)

    def build_group(pe, b, g):
        pe.wait_ge(s_oh, b * GPS + (g + 1))
        pe.wait_ge(s_adj, b * GPS + (g + 1))
        for i in range(GRP):
            last = pe.matmul(m.ps[:, g % RING, i * KEYS:(i + 1) * KEYS], oh_r[:, g % RING, i, :],
                             oh_k[:, g % RING, i, 0:KEYS], start=True, stop=True)
        last.then_inc(s_used, 1)

    def t_head(pe, b):
        for g in range(GPS):
            build_group(pe, b, g)

    def dense(pe, b, par, build):
        pe.wait_ge(s_adj, b * GPS + (GPS + RING))
        g, n = 0, 0
        for h in range(KC):
            pe.wait_ge(s_evac, b * KC + (h + 1))
            for c in range(NT):
                for half in range(2):
                    if build and n % EVERY == 0 and g < GPS:
                        build_group(pe, b + 1, g)
                        g += 1
                    n += 1
                    last = pe.matmul(m.ps[:, RING + h, 0:SB], table[:, c, half * C + h * P:half * C + (h + 1) * P],
                                     m.adj[:, par, c, :], start=c == 0 and half == 0, stop=c == NT - 1 and half == 1)
            last.then_inc(s_half, 1)

    def t_step(pe, b, s, par):
        dense(pe, b, par, True)

    def t_tail(pe, b):
        dense(pe, b + (NSB - 1), 0, False)

    def evacuate(act, b, par, g):
        act.wait_ge(s_used, b * GPS + (RING + g + 1))
        act.activation(m.adj[:, par, :, GRP * WIN * g:GRP * WIN * (g + 1)].rearrange("r c w -> r w c"),
                       m.ps[:, g % RING, 0:GRP * KEYS].rearrange("r (w c) -> r w c", c=NT), ACT.Copy).then_inc(s_adj, 1)

    def a_head(act, b):
        for g in range(GPS):
            evacuate(act, b, 0, g)

    def a_step(act, b, s, par):
        act.wait_ge(s_half, b * KC + KC)
        for g in range(GPS):
            evacuate(act, b + 1, 1 - par, g)

    def a_tail(act, b):
        act.wait_ge(s_half, b * KC + (NSB + 1) * KC)

    with nc.Block() as block:
        @block.vector
        def _(dve):
            chain_on(m, dve)(dve.memset(m.step16[:, :], 0.0))
            if not second:
                dve.sem_inc(s_evac, KC)
            walk(dve, "vector", v_head, v_step, v_tail)

        @block.tensor
        def _(pe):
            if not second:
                pe.sem_inc(s_used, RING)
                pe.sem_inc(s_half, KC)
            walk(pe, "tensor", t_head, t_step, t_tail)

        @block.scalar
        def _(act):
            if not second:
                act.sem_inc(s_adj, RING)
            walk(act, "scalar", a_head, a_step, a_tail)

        @block.gpsimd
        def _(pool):
            nlev = pool.value_load(m.levels[0:1, 0:1], min_val=1, max_val=NTE + 1)
            with pool.Fori(0, nlev) as level:
                run = pool.snap(level + nlev) if second else level
                with pool.If(nlev > 1):
                    between_levels(pool, "gpsimd", run)


def f32r_halves(dve, act, raw, hi, lo, s_in, n_in, s_hi, n_hi, s_lo):
    if act is not None:
        act.wait_ge(s_in, n_in)
        act.activation(hi, raw, ACT.Copy).then_inc(s_hi, 1)
    if dve is not None:
        dve.wait_ge(s_hi, n_hi)
        dve.tensor_tensor(lo, raw, hi.bitcast(F32), ALU.subtract).then_inc(s_lo, 1)


def linear1(nc, m, a):
    take = Place(m, m.work)
    w_hi, w_lo = take("w1_hi", [P, KC, IC], F32R), take("w1_lo", [P, KC, IC], F32R)
    raw = m.at("w1_raw", m.r3, [P, KC, IC], F32)
    u_hi, u_lo = take("u_hi", [P, 2, KC, SB], F32R), take("u_lo", [P, 2, KC, SB], F32R)
    S = m.sem
    s_raw, s_whi, s_wlo = S("d_raw"), S("d_whi"), S("d_wlo")
    s_u, s_uhi, s_ulo = S("d_u"), S("d_uhi"), S("d_ulo")
    s_mm = S("d_mm")
    s_h = S("d_h")
    h_of = (m.h01, m.h23)
    cols = lambda s: bass.ds(s * SB, SB)

    with nc.Block() as block:
        @block.sync
        def _(sp):
            sp.dma_start(raw[:, :, :], a.w1t.rearrange("(k p) f -> p k f", p=P)).then_inc(s_raw, 16)

        def walk(step, flush):
            def run(eng):
                step(eng, 0, 0)
                with eng.Fori(0, (NSB - 1) // 2) as k:
                    step(eng, 2 * k + 1, 1)
                    step(eng, 2 * k + 2, 0)
                flush(eng)
            return run

        @block.vector
        def _(dve):
            for h in h_of:
                dve.memset(h[:, :, N:NP_], 0.0)
            f32r_halves(dve, None, raw[:, :, :], w_hi[:, :, :], w_lo[:, :, :], None, 0, s_whi, 1, s_wlo)

            def stats(dve, s):
                dve.wait_ge(s_h, 2 * s + (2 + 4))
                for f in range(KI):
                    last = dve.bn_stats(m.stats1[:, f, bass.ds(s, 1), :].rearrange("p a b -> p (a b)"), h_of[f // 2][:, f % 2, cols(s)])
                return last

            def step(dve, s, par):
                dis = m.disB[:, cols(s)].unsqueeze(1).to_broadcast([P, KC, SB])
                dve.scalar_tensor_tensor(m.agg1[:, :, cols(s)], m.agg1[:, :, cols(s)], 1.0 / T1SCALE, dis,
                                         ALU.mult, ALU.mult).then_inc(s_u, 1)
                if not (isinstance(s, int) and s == 0):
                    stats(dve, s - 1)
                dve.wait_ge(s_uhi, s + 1)
                dve.wait_ge(s_mm, 2 * s + 2)
                dve.tensor_tensor(u_lo[:, par, :, :], m.agg1[:, :, cols(s)], u_hi[:, par, :, :].bitcast(F32),
                                  ALU.subtract).then_inc(s_ulo, 1)
            walk(step, lambda dve: stats(dve, NSB - 1))(dve)

        @block.scalar
        def _(act):
            act.sem_inc(s_h, 4)
            f32r_halves(None, act, raw[:, :, :], w_hi[:, :, :], w_lo[:, :, :], s_raw, 16, s_whi, 1, s_wlo)

            def evacuate(act, s, par):
                for q in range(2):
                    act.wait_ge(s_mm, 2 * s + (q + 1 + 4))
                    act.activation(h_of[q][:, :, cols(s)], m.ps[:, 4 * par + 2 * q:4 * par + 2 * q + 2, 0:SB], ACT.Copy).then_inc(s_h, 1)

            def step(act, s, par):
                act.wait_ge(s_u, s + 1)
                act.wait_ge(s_mm, 2 * s + 2)
                act.activation(u_hi[:, par, :, :], m.agg1[:, :, cols(s)], ACT.Copy).then_inc(s_uhi, 1)
                if not (isinstance(s, int) and s == 0):
                    evacuate(act, s - 1, 1 - par)
            walk(step, lambda act: evacuate(act, NSB - 1, 0))(act)

        @block.tensor
        def _(pe):
            pe.sem_inc(s_mm, 4)
            pe.wait_ge(s_wlo, 1)

            def step(pe, s, par):
                pe.wait_ge(s_ulo, s + 1)
                for q in range(2):
                    pe.wait_ge(s_h, 2 * s + (q + 1))
                    for f in (2 * q, 2 * q + 1):
                        for n, (w, u) in enumerate(((w_hi, u_hi), (w_lo, u_hi), (w_hi, u_lo))):
                            for k in range(KC):
                                last = pe.matmul(m.ps[:, 4 * par + f, 0:SB], w[:, k, f * P:(f + 1) * P], u[:, par, k, :],
                                                 start=n == 0 and k == 0, stop=n == 2 and k == KC - 1)
                    last.then_inc(s_mm, 1)
            walk(step, lambda pe: None)(pe)


def chain_on(m, dve):
    def link(ins):
        m.chained += 1
        ins.then_inc(m.s_chain, 1)
        dve.wait_ge(m.s_chain, m.chained)
    return link


def norm1(nc, m, a):
    take = Place(m, m.work)
    m.w2_hi, m.w2_lo = take("w2_hi", [P, KI, C], F32R), take("w2_lo", [P, KI, C], F32R)
    m.work2 = take.next
    raw, wabs = take("w2_raw", [P, KI, C], F32), take("w2_abs", [P, KI, C], F32)
    take = Place(m, m.r3 - 2048)
    mv, ve, mh = take("n1_mv", [P, KI, 2], F32), take("n1_ve", [P, KI], F32), take("n1_mh", [P, KI], F32)
    rs, tmp = take("n1_rs", [P, KI], F32), take("n1_tmp", [P, KI], F32)
    bnd, babs = take("n1_bnd", [P, KI], F32), take("n1_babs", [P, KI], F32)
    top, one = take("n1_top", [P, 1], F32), take("n1_one", [1, 4], F32)
    S = m.sem
    s_raw, s_whi, s_wlo, s_ve, s_mh, s_rs = S("e_raw"), S("e_whi"), S("e_wlo"), S("e_ve"), S("e_mh"), S("e_rs")
    s_b, s_bp, s_top, s_topT, s_sc, s_scB = S("e_b"), S("e_bp"), S("e_top"), S("e_topT"), S("e_sc"), S("e_scB")
    with nc.Block() as block:
        @block.sync
        def _(sp):
            sp.dma_start(raw[:, :, :], a.w2t.rearrange("(k p) c -> p k c", p=P)).then_inc(s_raw, 16)

        @block.scalar
        def _(act):
            f32r_halves(None, act, raw[:, :, :], m.w2_hi[:, :, :], m.w2_lo[:, :, :], s_raw, 16, s_whi, 1, s_wlo)

        @block.gpsimd
        def _(pool):
            pool.memset(mh[:, :], -0.5).then_inc(s_mh, 1)
            pool.wait_ge(s_mh, 1)
            pool.wait_ge(s_ve, 1)
            pool.tensor_tensor(rs[:, :], ve[:, :], mh[:, :], ALU.pow).then_inc(s_rs, 1)

        @block.tensor
        def _(pe):
            pe.wait_ge(s_b, 1)
            for c in range(KC):
                for k in range(KI):
                    last = pe.matmul(m.ps[:, 0, c:c + 1], wabs[:, k, c * P:(c + 1) * P], bnd[:, k:k + 1],
                                     start=k == 0, stop=k == KI - 1)
            last.then_inc(s_bp, 1)
            pe.wait_ge(s_top, 1)
            pe.transpose(m.ps[:1, 1, 0:P], top[:, :], m.id32[:, :]).then_inc(s_topT, 1)
            pe.wait_ge(s_sc, 1)
            pe.matmul(m.ps[:, 2, 0:1], m.ones[0:1, :], one[0:1, 3:4], start=True, stop=True).then_inc(s_scB, 1)

        @block.vector
        def _(dve):
            link = chain_on(m, dve)
            for f in range(KI):
                last = dve.bn_aggr(mv[:, f, :], m.stats1[:, f, :, :].rearrange("p a b -> p (a b)"))
            link(last)
            dve.tensor_scalar(ve[:, :], mv[:, :, 1], EPS, None, ALU.add).then_inc(s_ve, 1)
            dve.wait_ge(s_raw, 16)
            link(dve.scalar_tensor_tensor(wabs[:, :, :], raw[:, :, :], -1.0, raw[:, :, :], ALU.mult, ALU.max))
            link(dve.scalar_tensor_tensor(babs[:, :], m.bn_b1[:, :], -1.0, m.bn_b1[:, :], ALU.mult, ALU.max))
            link(dve.scalar_tensor_tensor(bnd[:, :], m.bn_g1[:, :], -1.0, m.bn_g1[:, :], ALU.mult, ALU.max))
            dve.scalar_tensor_tensor(bnd[:, :], bnd[:, :], float(N) ** 0.5 + 1.0, babs[:, :], ALU.mult, ALU.add).then_inc(s_b, 1)
            dve.wait_ge(s_bp, 1)
            dve.tensor_reduce(top[:, :], m.ps[:, 0, 0:KC], AX.X, ALU.max).then_inc(s_top, 1)
            dve.wait_ge(s_topT, 1)
            link(dve.tensor_reduce(one[:, 0:1], m.ps[:1, 1, 0:P], AX.X, ALU.max))
            link(dve.tensor_scalar(one[:, 1:2], one[:, 0:1], 1e-6, 1.0 / 32768.0, ALU.max, ALU.mult))
            link(dve.reciprocal(one[:, 2:3], one[:, 1:2]))
            dve.tensor_scalar(one[:, 3:4].bitcast(I32), one[:, 2:3].bitcast(I32), 0x7F800000, None, ALU.bitwise_and).then_inc(s_sc, 1)
            dve.wait_ge(s_scB, 1)
            link(dve.tensor_copy(m.scale2[:, :], m.ps[:, 2, 0:1]))
            link(dve.tensor_scalar(m.disP[:, :], m.disP[:, :], m.scale2[:, 0:1], None, ALU.mult))
            dve.wait_ge(s_rs, 1)
            link(dve.tensor_tensor(m.aff_a1[:, :], m.bn_g1[:, :], rs[:, :], ALU.mult))
            link(dve.tensor_tensor(tmp[:, :], mv[:, :, 0], m.aff_a1[:, :], ALU.mult))
            link(dve.tensor_tensor(m.aff_b1[:, :], m.bn_b1[:, :], tmp[:, :], ALU.subtract))
            f32r_halves(dve, None, raw[:, :, :], m.w2_hi[:, :, :], m.w2_lo[:, :, :], None, 0, s_whi, 1, s_wlo)


def linear2(nc, m, a):
    norm1(nc, m, a)
    take = Place(m, m.work2)
    h_hi, h_lo = take("h_hi", [P, 2, KI, P], F32R), take("h_lo", [P, 2, KI, P], F32R)
    S = m.sem
    s_r, s_hhi, s_split = S("f_r"), S("f_hhi"), S("f_split")
    s_mm = S("f_mm")
    s_thi = S("f_thi")
    s_tlo = S("f_tlo")
    h_of = (m.h01, m.h23)
    rows = lambda i: bass.ds(i * P, P)

    def walk(eng, step, flush):
        step(eng, 0, 0)
        with eng.Fori(0, (NT - 1) // 2) as k:
            step(eng, 2 * k + 1, 1)
            step(eng, 2 * k + 2, 0)
        flush(eng)

    with nc.Block() as block:
        @block.vector
        def _(dve):
            dve.sem_inc(s_tlo, 2)

            def low(dve, i, par):
                dve.wait_ge(s_thi, i + 1)
                dve.scalar_tensor_tensor(m.table2[:, bass.ds(i, 1), C:].rearrange("p a c -> p (a c)"), m.ps[:, par, 0:C],
                                         m.disP[:, bass.ds(i, 1)], m.table2[:, bass.ds(i, 1), :C].rearrange("p a c -> p (a c)"),
                                         ALU.mult, ALU.subtract).then_inc(s_tlo, 1)

            def step(dve, i, par):
                dve.wait_ge(s_r, i + 1)
                dve.wait_ge(s_mm, i + 1)
                for q in range(2):
                    last = dve.tensor_copy(h_hi[:, par, 2 * q:2 * q + 2, :], h_of[q][:, :, rows(i)])
                last.then_inc(s_hhi, 1)
                if not (isinstance(i, int) and i == 0):
                    low(dve, i - 1, 1 - par)
                dve.wait_ge(s_hhi, i + 1)
                for q in range(2):
                    last = dve.tensor_tensor(h_lo[:, par, 2 * q:2 * q + 2, :], h_of[q][:, :, rows(i)],
                                             h_hi[:, par, 2 * q:2 * q + 2, :].bitcast(F32), ALU.subtract)
                last.then_inc(s_split, 1)
            walk(dve, step, lambda dve: low(dve, NT - 1, 0))

        @block.scalar
        def _(act):
            def high(act, i, par):
                act.wait_ge(s_mm, i + (1 + 2))
                act.activation(m.table2[:, bass.ds(i, 1), :C].rearrange("p a c -> p (a c)"), m.ps[:, par, 0:C], ACT.Copy,
                               scale=m.disP[:, bass.ds(i, 1)]).then_inc(s_thi, 1)

            def step(act, i, par):
                for f in range(KI):
                    h = h_of[f // 2][:, f % 2, rows(i)]
                    last = act.activation(h, h, ACT.Relu, bias=m.aff_b1[:, f:f + 1], scale=m.aff_a1[:, f:f + 1])
                last.then_inc(s_r, 1)
                if not (isinstance(i, int) and i == 0):
                    high(act, i - 1, 1 - par)
            walk(act, step, lambda act: high(act, NT - 1, 0))

        @block.tensor
        def _(pe):
            pe.sem_inc(s_mm, 2)

            def step(pe, i, par):
                pe.wait_ge(s_split, i + 1)
                pe.wait_ge(s_tlo, i + 1)
                for n, (h, w) in enumerate(((h_hi, m.w2_hi), (h_hi, m.w2_lo), (h_lo, m.w2_hi))):
                    for f in range(KI):
                        last = pe.matmul(m.ps[:, par, 0:C], h[:, par, f, :], w[:, f, :],
                                         start=n == 0 and f == 0, stop=n == 2 and f == KI - 1)
                last.then_inc(s_mm, 1)
            walk(pe, step, lambda pe: None)
    self_loops(nc, m, "l2", m.table2, m.agg2)


def finish_gnn(nc, m, a):
    x = m.x
    x1 = m.at("x1_sb", m.r2, [P, NT, C], F32)
    take = Place(m, m.work)
    st2, mv2 = take("st2", [P, KC, NSB, 6], F32), take("mv2", [P, KC, 2], F32)
    e2, ve2, mh, rs2 = take("e2", [P, 1], F32), take("ve2", [P, KC], F32), take("mh2", [P, NT], F32), take("rs2", [P, KC], F32)
    a2, b2, tmp = take("a2", [P, KC], F32), take("b2c", [P, KC], F32), take("tmp2", [P, KC], F32)
    xn = take("xn", [P, 2, 2, C], F32)
    st3, mv3 = take("st3", [P, NT, 6], F32), take("mv3", [P, NT, 2], F32)
    ve3, rs3 = take("ve3", [P, NT], F32), take("rs3", [P, NT], F32)
    S = m.sem
    s_x, s_xt, s_u, s_ve, s_mh, s_rs, s_aff, s_v, s_tr, s_sum = (S("g_" + n) for n in ("x", "xt", "u", "ve", "mh", "rs", "aff", "v", "tr", "sum"))
    s_x1, s_ve3, s_rs3, s_out = (S("g_" + n) for n in ("x1", "ve3", "rs3", "out"))
    pairs = [(2 * g, min(2, NT - 2 * g)) for g in range(-(-NT // 2))]
    eights = [(8 * g, min(8, NT - 8 * g)) for g in range(-(-NT // 8))]
    with nc.Block() as block:
        @block.sync
        def _(sp):
            for i in range(6):
                sp.dma_start(x[:, 8 * i:8 * i + 8, :],
                             a.x[1024 * i:1024 * (i + 1), :].rearrange("(t p) c -> p t c", p=P)).then_inc(s_x, 16)
            sp.wait_ge(s_xt, 1)
            sp.dma_start(x[:LAST, NT - 1, :], a.x[(NT - 1) * P:N, :]).then_inc(s_x, 16)
            for t0, k in eights:
                sp.wait_ge(s_x1, (t0 + k + 1) // 2)
                sp.dma_start(m.x1_dram[t0 * P:(t0 + k) * P, :].rearrange("(t p) c -> p t c", p=P), x1[:, t0:t0 + k, :]).then_inc(s_out, 16)
            sp.wait_ge(s_out, 16 * len(eights))

        @block.gpsimd
        def _(pool):
            pool.memset(mh[:, :], -0.5).then_inc(s_mh, 1)
            pool.wait_ge(s_mh, 1)
            pool.wait_ge(s_ve, 1)
            pool.tensor_tensor(rs2[:, :], ve2[:, :], mh[:, :KC], ALU.pow).then_inc(s_rs, 1)
            pool.wait_ge(s_ve3, 1)
            pool.tensor_tensor(rs3[:, :], ve3[:, :], mh[:, :], ALU.pow).then_inc(s_rs3, 1)

        @block.vector
        def _(dve):
            link = chain_on(m, dve)
            dve.memset(x[:, NT - 1, :], 0.0).then_inc(s_xt, 1)
            with dve.Fori(0, NSB) as s:
                c = bass.ds(s * SB, SB)
                dve.tensor_tensor(m.agg2[:, :, c], m.agg2[:, :, c], m.disB[:, c].unsqueeze(1).to_broadcast([P, KC, SB]),
                                  ALU.mult).then_inc(s_u, 1)
                dve.wait_ge(s_u, s + 1)
                for h in range(KC):
                    dve.bn_stats(st2[:, h, bass.ds(s, 1), :].rearrange("p a b -> p (a b)"), m.agg2[:, h, c])
            link(dve.tensor_tensor(e2[:, :], m.scale2[:, :], m.scale2[:, :], ALU.mult))
            for h in range(KC):
                last = dve.bn_aggr(mv2[:, h, :], st2[:, h, :, :].rearrange("p a b -> p (a b)"))
            link(last)
            dve.scalar_tensor_tensor(ve2[:, :], e2[:, 0:1].to_broadcast([P, KC]), EPS, mv2[:, :, 1], ALU.mult, ALU.add).then_inc(s_ve, 1)
            dve.wait_ge(s_rs, 1)
            link(dve.tensor_tensor(a2[:, :], m.bn_g2[:, :], rs2[:, :], ALU.mult))
            link(dve.tensor_tensor(tmp[:, :], mv2[:, :, 0], a2[:, :], ALU.mult))
            dve.tensor_tensor(b2[:, :], m.bn_b2[:, :], tmp[:, :], ALU.subtract).then_inc(s_aff, 1)
            dve.wait_ge(s_x, 16 * 7)
            for g, (t0, k) in enumerate(pairs):
                for i in range(k):
                    last = dve.tensor_scalar(xn[:, g % 2, i, :], x[:, t0 + i, :], m.mean[:, t0 + i:t0 + i + 1],
                                             m.rstd[:, t0 + i:t0 + i + 1], ALU.subtract, ALU.mult)
                link(last)
                dve.wait_ge(s_tr, g + 1)
                link(dve.tensor_tensor(xn[:, g % 2, 0:k, :], xn[:, g % 2, 0:k, :],
                                       m.ps[:, g % 4, 0:k * C].rearrange("p (t c) -> p t c", c=C), ALU.add))
                dve.scalar_tensor_tensor(x1[:, t0:t0 + k, :], xn[:, g % 2, 0:k, :], 0.0, x[:, t0:t0 + k, :],
                                         ALU.max, ALU.add).then_inc(s_x1, 1)
                dve.wait_ge(s_x1, g + 1)
                for i in range(t0, t0 + k):
                    dve.bn_stats(st3[:, i, :], x1[:, i, :]).then_inc(s_sum, 1)
            dve.wait_ge(s_sum, NT)
            for i in range(NT):
                last = dve.bn_aggr(mv3[:, i, :], st3[:, i, :])
            link(last)
            dve.tensor_scalar(ve3[:, :], mv3[:, :, 1], EPS, None, ALU.add).then_inc(s_ve3, 1)
            dve.wait_ge(s_rs3, 1)
            for i in range(NT):
                last = dve.tensor_scalar(m.rows[:, i, 0:C], x1[:, i, :], mv3[:, i, 0:1], rs3[:, i:i + 1], ALU.subtract, ALU.mult)
            link(last)

        @block.scalar
        def _(act):
            act.wait_ge(s_aff, 1)
            for g, (t0, k) in enumerate(pairs):
                for h in range(KC):
                    v = m.agg2[:, h, t0 * P:(t0 + k) * P]
                    last = act.activation(v, v, ACT.Identity, bias=b2[:, h:h + 1], scale=a2[:, h:h + 1])
                last.then_inc(s_v, 1)

        @block.tensor
        def _(pe):
            for g, (t0, k) in enumerate(pairs):
                pe.wait_ge(s_v, g + 1)
                if g >= 4:
                    pe.wait_ge(s_x1, g - 3)
                for i in range(k):
                    for h in range(KC):
                        last = pe.transpose(m.ps[:, g % 4, i * C + h * P:i * C + (h + 1) * P],
                                            m.agg2[:, h, (t0 + i) * P:(t0 + i + 1) * P], m.id32[:, :])
                last.then_inc(s_tr, 1)



def ffn_scales(nc, m, a):
    raw = m.at("w1f_abs", m.r1, [P, KC, HID], F32)
    wd_raw = m.at("wd_abs", m.r1 + 8192, [P, 2, NEXP, C], F32)
    take = Place(m, m.r1 + 8192 * 3)
    asum, bsum, babs = take("asum", [P, KH], F32), take("bsum", [P, KH], F32), take("babs", [P, KH], F32)
    rb, inv, prod, low = take("rb", [P, KH], F32), take("inv", [P, KH], F32), take("prod", [P, KH], F32), take("low", [P, 1], F32)
    one = take("one_f", [1, 1], F32)
    S = m.sem
    s_w1, s_b1, s_wd, s_abs, s_free, s_wabs, s_bp, s_low, s_lowT, s_one, s_G = (
        S("h_" + n) for n in ("w1", "b1", "wd", "abs", "free", "wabs", "bp", "low", "lowT", "one", "G"))
    s_wdp = [S("h_wd0"), S("h_wd1")]
    with nc.Block() as block:
        @block.sync
        def _(sp):
            sp.dma_start(raw[:, :, :], a.fw1.rearrange("(k p) h -> p k h", p=P)).then_inc(s_w1, 16)
            with nc.allow_non_contiguous_dma("the bias of the hidden units to partitions"):
                sp.dma_start(m.b1f[:, :], a.fb1.rearrange("(k p) -> p k", p=P)).then_inc(s_b1, 16)
            for k in range(KH):
                if k >= 2:
                    sp.wait_ge(s_free, k - 1)
                sp.dma_start(wd_raw[:, k % 2, :, :], a.fwd[:, k * P:(k + 1) * P, :].rearrange("e p c -> p e c")).then_inc(s_wdp[k % 2], 16)

        @block.scalar
        def _(act):
            for k in range(KH):
                act.wait_ge(s_wdp[k % 2], 16 * (k // 2 + 1))
                act.activation(wd_raw[:, k % 2, :, :], wd_raw[:, k % 2, :, :], ACT.Abs, accum_out=asum[:, k:k + 1]).then_inc(s_free, 1)

        @block.tensor
        def _(pe):
            pe.wait_ge(s_wabs, 1)
            for h in range(KH):
                for k in range(KC):
                    last = pe.matmul(m.ps[:, 0, h:h + 1], raw[:, k, h * P:(h + 1) * P], m.ones[:, 0:1], start=k == 0, stop=k == KC - 1)
            last.then_inc(s_bp, 1)
            pe.wait_ge(s_low, 1)
            pe.transpose(m.ps[:1, 1, 0:P], low[:, :], m.id32[:, :]).then_inc(s_lowT, 1)
            pe.wait_ge(s_one, 1)
            pe.matmul(m.ps[:, 2, 0:1], m.ones[0:1, :], one[0:1, 0:1], start=True, stop=True).then_inc(s_G, 1)

        @block.vector
        def _(dve):
            link = chain_on(m, dve)

            def power(out, bound):
                link(dve.tensor_scalar(out, bound, 1e-6, 1.0 / 32768.0, ALU.max, ALU.mult))
                link(dve.reciprocal(out, out))
                link(dve.tensor_scalar(out.bitcast(I32), out.bitcast(I32), 0x7F800000, None, ALU.bitwise_and))

            def inverse(out, x):
                link(dve.tensor_scalar(out.bitcast(I32), x.bitcast(I32), -1.0, float(254 << 23), ALU.mult, ALU.add))

            dve.wait_ge(s_w1, 16)
            dve.scalar_tensor_tensor(raw[:, :, :], raw[:, :, :], -1.0, raw[:, :, :], ALU.mult, ALU.max).then_inc(s_wabs, 1)
            dve.wait_ge(s_b1, 16)
            link(dve.scalar_tensor_tensor(babs[:, :], m.b1f[:, :], -1.0, m.b1f[:, :], ALU.mult, ALU.max))
            dve.wait_ge(s_bp, 1)
            link(dve.scalar_tensor_tensor(bsum[:, :], m.ps[:, 0, 0:KH], 16.25, babs[:, :], ALU.mult, ALU.add))
            power(rb[:, :], bsum[:, :])
            dve.wait_ge(s_free, KH)
            power(m.alpha[:, :], asum[:, :])
            link(dve.tensor_tensor(prod[:, :], rb[:, :], m.alpha[:, :], ALU.mult))
            dve.tensor_reduce(low[:, :], prod[:, :], AX.X, ALU.min).then_inc(s_low, 1)
            dve.wait_ge(s_lowT, 1)
            dve.tensor_reduce(one[:, :], m.ps[:1, 1, 0:P], AX.X, ALU.min).then_inc(s_one, 1)
            dve.wait_ge(s_G, 1)
            link(dve.tensor_copy(low[:, :], m.ps[:, 2, 0:1]))
            inverse(m.inv_g[:, :], low[:, :])
            inverse(inv[:, :], m.alpha[:, :])
            link(dve.tensor_scalar(m.beta[:, :], inv[:, :], low[:, 0:1], None, ALU.mult))


def ffn(nc, m, a):
    take = Place(m, m.r2)
    m.wd_hi, m.wd_lo = take("wd_hi", [P, NEXP, KH, C], F16), take("wd_lo", [P, NEXP, KH, C], F16)
    m.w1_hi, m.w1_lo = take("fw1_hi", [P, KC, HID], F32R), take("fw1_lo", [P, KC, HID], F32R)
    m.xt_hi, m.xt_lo = take("xt_hi", [P, 2, KC, 2 * P], F32R), take("xt_lo", [P, 2, KC, 2 * P], F32R)
    m.hf = take("hf", [P, KH, 2 * P], F32)
    m.work3 = take.next
    gate(nc, m, a)
    experts(nc, m, a)


def up_tensors(nc, m, tag):
    u = Names()
    u.tr = m.sem(f"{tag}_tr")
    u.xthi = m.sem(f"{tag}_xthi")
    u.xt = m.sem(f"{tag}_xt")
    u.up = m.sem(f"{tag}_up")
    u.gelu = m.sem(f"{tag}_gelu")
    u.split = m.sem(f"{tag}_split")
    return u


UB = 4
TBANK = 4


def pe_transpose(pe, m, u, i, rows, ntile):
    pe.wait_ge(u.xt, i + 1)
    for j in range(ntile):
        for k in range(KC):
            last = pe.transpose(m.ps[:, TBANK, k * 2 * P + j * P:k * 2 * P + (j + 1) * P], rows(j, k), m.id32[:, :])
    last.then_inc(u.tr, 1)


def pe_up(pe, m, u, i, par, ntile, h):
    n = ntile * P
    if h == 0:
        pe.wait_ge(u.xt, i + 2)
    pe.wait_ge(u.gelu, i * KH + (h + 1))
    for q, (w, x) in enumerate(((m.w1_hi, m.xt_hi), (m.w1_lo, m.xt_hi), (m.w1_hi, m.xt_lo))):
        for k in range(KC):
            last = pe.matmul(m.ps[:, h % UB, 0:n], w[:, k, h * P:(h + 1) * P], x[:, par, k, 0:n],
                             start=q == 0 and k == 0, stop=q == 2 and k == KC - 1)
    last.then_inc(u.up, 1)


def act_xt(act, m, u, i, par, ntile):
    act.wait_ge(u.tr, i + 1)
    act.wait_ge(u.up, i * KH + KH)
    act.activation(m.xt_hi[:, par, :, 0:ntile * P],
                   m.ps[:, TBANK, :].rearrange("p (k n) -> p k n", k=KC)[:, :, 0:ntile * P], ACT.Copy).then_inc(u.xthi, 1)


def dve_xt(dve, m, u, i, par, ntile):
    dve.wait_ge(u.xthi, i + 1)
    dve.tensor_tensor(m.xt_lo[:, par, :, 0:ntile * P],
                      m.ps[:, TBANK, :].rearrange("p (k n) -> p k n", k=KC)[:, :, 0:ntile * P],
                      m.xt_hi[:, par, :, 0:ntile * P].bitcast(F32), ALU.subtract).then_inc(u.xt, 1)


def act_gelu(act, m, u, i, ntile, h):
    act.wait_ge(u.up, i * KH + (h + 1 + 2 * KH))
    if h % 4 == 0:
        act.wait_ge(u.split, 2 * i + (h // 4 + 1))
    act.activation(m.hf[:, h, 0:ntile * P], m.ps[:, h % UB, 0:ntile * P], ACT.Gelu, bias=m.b1f[:, h:h + 1]).then_inc(u.gelu, 1)


REG = 6400
MAXT = 56
assert MAXT * P >= N + NEXP * (P - 1) - P + 1 and REG >= NP_ + P
RW = C + NEXP + 1


def gate(nc, m, a):
    rows = m.rows
    take = Place(m, m.work3)
    h_hi, h_lo = take("gh_hi", [P, KH, 2 * P], F32R), take("gh_lo", [P, KH, 2 * P], F32R)
    w1_raw = m.at("fw1_raw", take.next - 16384, [P, KC, HID], F32)
    take = Place(m, m.work)
    wd_raw = take("wd_raw", [P, 1, NEXP, C], F32)
    wg_raw, wg = take("wg_raw", [P, KH, NEXP], F32), take("wg", [P, KH, 2 * NEXP], F32R)
    bg = take("bgB", [P, NEXP], F32)
    tri, ones16 = take("tri", [P, P], F16), take("ones16", [P, P], F16)
    prio, run = take("prio", [P, NEXP], F32), take("run", [P, NEXP], F32)
    lg, mx = take("lg", [P, 2, NEXP], F32), take("mx", [P, 2], F32)
    sc, best = take("sc", [P, 2, NEXP], F32), take("best", [P, 2], F32)
    oh, ohf = take("oh", [P, 2, NEXP], F16), take("ohf", [P, 2, NEXP], F32)
    rk, slotf, slot = take("rk", [P, 2, NEXP], F32), take("slotf", [P, 2], F32), take("slot", [P, NT], I32)
    valid = take("valid", [P, 1], F32)
    padi, padf, prow = take("padi", [P, NEXP + 1], I32), take("padf", [P, NEXP + 1], F32), take("prow", [P, RW], F32)
    pcol = take("pcol", [P, 1], F32)
    stage = take("stage", [P, 2, 2, C], F32)
    tv, tb, nt, nti = take("tv", [1, 64], F32), take("tb", [1, NEXP + 1], F32), take("nt", [1, NEXP], F32), take("nti", [1, NEXP], I32)
    te, tr_, tq, tf = take("te", [1, 64], F32), take("tr_", [1, 64], F32), take("tq", [1, 64], F32), take("tf", [1, 64], F32)
    u = up_tensors(nc, m, "i")
    S = m.sem
    (s_w1, s_w1hi, s_w1lo, s_par, s_wd, s_wdhi, s_wdfree, s_const, s_lg, s_oh, s_rk, s_slot, s_scat, s_hi,
     s_init, s_last, s_lgfree, s_pads, s_stage) = (S("i_" + n) for n in (
         "w1", "w1hi", "w1lo", "par", "wd", "wdhi", "wdfree", "const", "lg", "oh", "rk", "slot", "scat", "hi",
         "init", "last", "lgfree", "pads", "stage"))
    NPAIR = NT // 2
    LB, RB = 5, 6

    with nc.Block() as block:
        @block.sync
        def _(sp):
            sp.dma_start(w1_raw[:, :, :], a.fw1.rearrange("(k p) h -> p k h", p=P)).then_inc(s_w1, 16)
            sp.dma_start(wg_raw[:, :, :], a.fwg.rearrange("(k p) e -> p k e", p=P)).then_inc(s_par, 16)
            sp.dma_start(bg[:, :], bass.AP(a.fbg.tensor, 0, [[0, P], [1, NEXP]])).then_inc(s_par, 16)
            for k in range(KH):
                if k:
                    sp.wait_ge(s_wdfree, k)
                sp.dma_start(wd_raw[:, 0, :, :], a.fwd[:, k * P:(k + 1) * P, :].rearrange("e p c -> p e c")).then_inc(s_wd, 16)

        @block.gpsimd
        def _(pool):
            pool.iota(rows[:, :, RW - 1].bitcast(I32), [[P, NT]], base=0, channel_multiplier=1).then_inc(s_const, 1)
            pool.memset(tri[:, :], 1.0).then_inc(s_init, 1)
            pool.memset(prow[:, :], 0.0).then_inc(s_init, 1)
            pool.memset(valid[:, :], 1.0).then_inc(s_init, 1)
            pool.wait_ge(s_init, 3)
            pool.affine_select(out=tri[:, :], in_=tri[:, :], compare_op=ALU.is_ge, fill=0.0,
                               base=-1, pattern=[[1, P]], channel_multiplier=-1).then_inc(s_const, 1)
            pool.affine_select(out=valid[:, :], in_=valid[:, :], compare_op=ALU.is_ge, fill=0.0,
                               base=LAST - 1, pattern=[[0, 1]], channel_multiplier=-1).then_inc(s_const, 1)
            pool.iota(prow[:, RW - 1:RW].bitcast(I32), [[0, 1]], base=N, channel_multiplier=0).then_inc(s_const, 1)
            pool.iota(prio[:, :], [[-1, NEXP]], base=NEXP, channel_multiplier=0, allow_small_or_imprecise_dtypes=True).then_inc(s_const, 1)
            pool.iota(run[:, :], [[REG, NEXP]], base=0, channel_multiplier=0, allow_small_or_imprecise_dtypes=True).then_inc(s_const, 1)
            pool.iota(padf[:, :], [[REG, NEXP + 1]], base=0, channel_multiplier=1, allow_small_or_imprecise_dtypes=True).then_inc(s_const, 1)
            pool.iota(m.reg_base[:, :], [[REG, NEXP]], base=0, channel_multiplier=0, allow_small_or_imprecise_dtypes=True).then_inc(s_const, 1)
            pool.iota(pcol[:, :], [[0, 1]], base=0, channel_multiplier=1, allow_small_or_imprecise_dtypes=True).then_inc(s_const, 1)
            pool.iota(tv[:, :], [[1, 64]], base=0, channel_multiplier=0, allow_small_or_imprecise_dtypes=True).then_inc(s_const, 1)
            for i in range(NPAIR + 3):
                if i <= NPAIR:
                    n = min(2, NT - 2 * i)
                    if i >= 2:
                        pool.wait_ge(u.tr, i - 1)
                    pool.tensor_copy(stage[:, i % 2, 0:n, :], rows[:, 2 * i:2 * i + n, 0:C]).then_inc(s_stage, 1)
                for k in range(2 * (i - 2), min(2 * (i - 2) + 2, NT)):
                    if k < 0:
                        continue
                    n = P if k < NT - 1 else LAST
                    if k % 2 == 0:
                        pool.wait_ge(s_slot, k // 2 + 1)
                    pool.indirect_dma_start(m.sorted_rows, bass.IndirectOffsetOnAxis(ap=slot[:n, k:k + 1], axis=0),
                                            rows[:n, k, :], None).then_inc(s_scat, 16)
            pool.wait_ge(s_pads, 1)
            pool.wait_ge(s_const, 10)
            for e in range(NEXP + 1):
                pool.indirect_dma_start(m.sorted_rows, bass.IndirectOffsetOnAxis(ap=padi[:, e:e + 1], axis=0),
                                        prow[:, :], None).then_inc(s_scat, 16)
            pool.wait_ge(s_scat, 16 * (NT + NEXP + 1))

        def steps(eng, step):
            step(eng, 0, 0, 2, True)
            step(eng, 1, 1, 2, False)
            with eng.Fori(1, NPAIR // 2) as k:
                step(eng, 2 * k, 0, 2, False)
                step(eng, 2 * k + 1, 1, 2, False)
            step(eng, NPAIR, 0, 1, False)

        @block.tensor
        def _(pe):
            pe.sem_inc(u.up, 2 * KH)
            pe.sem_inc(s_lg, 1)
            pe.wait_ge(s_w1lo, 1)
            pe.wait_ge(s_const, 10)

            def logits(pe, i, ntile):
                pe.wait_ge(u.split, 2 * i + (2 + 2))
                pe.wait_ge(s_lgfree, i + 1)
                for j in range(ntile):
                    for k in range(KH):
                        pe.matmul(m.ps[:, LB, j * 16:j * 16 + 2 * NEXP], h_hi[:, k, j * P:(j + 1) * P], wg[:, k, :],
                                  start=k == 0, stop=False)
                    for k in range(KH):
                        last = pe.matmul(m.ps[:, LB, j * 16:j * 16 + 2 * NEXP], h_lo[:, k, j * P:(j + 1) * P], wg[:, k, :],
                                         start=False, stop=k == KH - 1)
                last.then_inc(s_lg, 1)

            def ranks(pe, i, ntile):
                pe.wait_ge(s_oh, i + 1)
                pe.matmul(m.ps[:, RB, 0:NEXP], tri[:, :], oh[:, 0, :], start=True, stop=True)
                if ntile == 2:
                    pe.matmul(m.ps[:, RB, NEXP:2 * NEXP], tri[:, :], oh[:, 1, :], start=True, stop=False)
                    pe.matmul(m.ps[:, RB, NEXP:2 * NEXP], ones16[:, :], oh[:, 0, :], start=False, stop=True)
                for j in range(ntile):
                    last = pe.matmul(m.ps[:, RB, 2 * NEXP:3 * NEXP], ones16[:, :], oh[:, j, :], start=j == 0, stop=j == ntile - 1)
                last.then_inc(s_rk, 1)

            def step(pe, i, par, ntile, first):
                if first:
                    pe.wait_ge(s_stage, 1)
                    pe_transpose(pe, m, u, 0, lambda j, k: stage[:, 0, j, k * P:(k + 1) * P], 2)
                for h in range(KH):
                    pe_up(pe, m, u, i, par, ntile, h)
                    if h == 1 and not first:
                        logits(pe, i - 1, 2)
                    if h == 5 and not first:
                        ranks(pe, i - 1, 2)
                    if h == 3 and ntile == 2:
                        nxt = 2 if not (isinstance(i, int) and i == NPAIR - 1) else 1
                        pe.wait_ge(s_stage, i + 2)
                        pe_transpose(pe, m, u, i + 1, lambda j, k: stage[:, 1 - par, j, k * P:(k + 1) * P], nxt)

            step(pe, 0, 0, 2, True)
            step(pe, 1, 1, 2, False)
            with pe.Fori(1, NPAIR // 2 - 1) as k:
                step(pe, 2 * k, 0, 2, False)
                step(pe, 2 * k + 1, 1, 2, False)
            step(pe, NPAIR - 2, 0, 2, False)
            step(pe, NPAIR - 1, 1, 2, False)
            step(pe, NPAIR, 0, 1, False)
            logits(pe, NPAIR, 1)
            ranks(pe, NPAIR, 1)

        @block.scalar
        def _(act):
            act.sem_inc(u.gelu, UB)
            act.wait_ge(s_w1, 16)
            act.activation(m.w1_hi[:, :, :], w1_raw[:, :, :], ACT.Copy).then_inc(s_w1hi, 1)
            act.wait_ge(s_par, 32)
            act.activation(wg[:, :, 0:NEXP], wg_raw[:, :, :], ACT.Copy).then_inc(s_w1hi, 1)

            def step(act, i, par, ntile, first):
                act_xt(act, m, u, i, par, ntile)
                for h in range(KH):
                    act_gelu(act, m, u, i, ntile, h)
                if isinstance(i, int) and i < 2:
                    for k in range(4 * i, 4 * i + 4):
                        act.wait_ge(s_wd, 16 * (k + 1))
                        act.activation(m.wd_hi[:, :, k, :], wd_raw[:, 0, :, :], ACT.Copy, scale=m.alpha[:, k:k + 1]).then_inc(s_wdhi, 1)
            steps(act, step)

        @block.vector
        def _(dve):
            link = chain_on(m, dve)
            dve.sem_inc(u.xt, 1)
            dve.sem_inc(u.split, 2)
            dve.sem_inc(s_lgfree, 1)
            link(dve.memset(ones16[:, :], 1.0))
            dve.wait_ge(s_w1hi, 1)
            link(dve.tensor_tensor(m.w1_lo[:, :, :], w1_raw[:, :, :], m.w1_hi[:, :, :].bitcast(F32), ALU.subtract))
            dve.wait_ge(s_w1hi, 2)
            dve.tensor_tensor(wg[:, :, NEXP:], wg_raw[:, :, :], wg[:, :, 0:NEXP].bitcast(F32), ALU.subtract).then_inc(s_w1lo, 1)
            dve.wait_ge(s_const, 10)

            def split(dve, i, ntile, half):
                n = ntile * P
                q = slice(4 * half, 4 * half + 4)
                dve.wait_ge(u.gelu, i * KH + (4 * half + 4 + UB))
                if half == 0:
                    dve.wait_ge(s_lg, i + 1)
                dve.tensor_copy(h_hi[:, q, 0:n], m.hf[:, q, 0:n]).then_inc(s_hi, 1)
                dve.wait_ge(s_hi, 2 * i + (half + 1))
                dve.tensor_tensor(h_lo[:, q, 0:n], m.hf[:, q, 0:n], h_hi[:, q, 0:n].bitcast(F32), ALU.subtract).then_inc(u.split, 1)

            def choose(dve, i, ntile):
                t = slice(0, ntile)
                c0 = lambda n: base_of(i) + n

                def lk(ins, n):
                    ins.then_inc(s_last, 1)
                    dve.wait_ge(s_last, c0(n))
                dve.wait_ge(s_lg, i + 2)
                ps = m.ps[:, LB, 0:16 * ntile].rearrange("p (t e) -> p t e", e=16)
                lk(dve.tensor_tensor(lg[:, t, :], ps[:, :, 0:NEXP], bg[:, :].unsqueeze(1).to_broadcast([P, ntile, NEXP]), ALU.add), 1)
                lk(dve.tensor_tensor(lg[:, t, :], lg[:, t, :], ps[:, :, NEXP:], ALU.add), 2)
                dve.sem_inc(s_lgfree, 1)
                lk(dve.tensor_reduce(mx[:, t], lg[:, t, :], AX.X, ALU.max), 3)
                shifted = rows[:, bass.ds(2 * i, ntile), C:C + NEXP]
                lk(dve.tensor_tensor(lg[:, t, :], lg[:, t, :], mx[:, t].unsqueeze(2).to_broadcast([P, ntile, NEXP]), ALU.subtract), 4)
                dve.tensor_copy(shifted, lg[:, t, :])
                lk(dve.scalar_tensor_tensor(sc[:, t, :], lg[:, t, :], 0.0, prio[:, :].unsqueeze(1).to_broadcast([P, ntile, NEXP]), ALU.is_equal, ALU.mult), 5)
                lk(dve.tensor_reduce(best[:, t], sc[:, t, :], AX.X, ALU.max), 6)
                lk(dve.tensor_tensor(ohf[:, t, :], sc[:, t, :], best[:, t].unsqueeze(2).to_broadcast([P, ntile, NEXP]), ALU.is_equal), 7)
                if ntile == 1:
                    link(dve.tensor_scalar(ohf[:, 0, :], ohf[:, 0, :], valid[:, 0:1], None, ALU.mult))
                dve.tensor_copy(oh[:, t, :], ohf[:, t, :]).then_inc(s_oh, 1)

            def place(dve, i, ntile):
                t = slice(0, ntile)
                c0 = lambda n: base_of(i) + 7 + n

                def lk(ins, n):
                    ins.then_inc(s_last, 1)
                    dve.wait_ge(s_last, c0(n))
                dve.wait_ge(s_rk, i + 1)
                lk(dve.tensor_tensor(rk[:, t, :], m.ps[:, RB, 0:NEXP * ntile].rearrange("p (t e) -> p t e", e=NEXP),
                                     run[:, :].unsqueeze(1).to_broadcast([P, ntile, NEXP]), ALU.add), 1)
                lk(dve.tensor_tensor(rk[:, t, :], rk[:, t, :], ohf[:, t, :], ALU.mult), 2)
                lk(dve.tensor_tensor(run[:, :], run[:, :], m.ps[:, RB, 2 * NEXP:3 * NEXP], ALU.add), 3)
                lk(dve.tensor_reduce(slotf[:, t], rk[:, t, :], AX.X, ALU.add), 4)
                dve.tensor_copy(slot[:, bass.ds(2 * i, ntile)], slotf[:, t]).then_inc(s_slot, 1)

            def base_of(i):
                return i * 11

            def step(dve, i, par, ntile, first):
                dve_xt(dve, m, u, i, par, ntile)
                if not first:
                    choose(dve, i - 1, 2)
                split(dve, i, ntile, 0)
                if not first:
                    place(dve, i - 1, 2)
                split(dve, i, ntile, 1)
                if isinstance(i, int) and i < 2:
                    for k in range(4 * i, 4 * i + 4):
                        dve.wait_ge(s_wdhi, k + 1)
                        dve.scalar_tensor_tensor(m.wd_lo[:, :, k, :], wd_raw[:, 0, :, :], m.alpha[:, k:k + 1],
                                                 m.wd_hi[:, :, k, :], ALU.mult, ALU.subtract).then_inc(s_wdfree, 1)
            steps(dve, step)
            choose(dve, NPAIR, 1)
            place(dve, NPAIR, 1)
            link(dve.tensor_scalar(padf[:, 0:NEXP], run[:, :], pcol[:, 0:1], None, ALU.add))
            dve.tensor_copy(padi[:, :], padf[:, :]).then_inc(s_pads, 1)
            link(dve.tensor_tensor(nt[:, :], run[0:1, :], m.reg_base[0:1, :], ALU.subtract))
            link(dve.tensor_scalar(nt[:, :], nt[:, :], float(P - 1), None, ALU.add))
            link(dve.tensor_copy(nti[:, :], nt[:, :]))
            link(dve.tensor_scalar(nti[:, :], nti[:, :], 7, None, ALU.arith_shift_right))
            link(dve.tensor_copy(nt[:, :], nti[:, :]))
            link(dve.memset(tb[:, :], 0.0))
            link(dve.memset(te[:, :], 0.0))
            link(dve.memset(tr_[:, :], 0.0))
            for e in range(NEXP):
                link(dve.tensor_tensor(tb[:, e + 1:e + 2], tb[:, e:e + 1], nt[:, e:e + 1], ALU.add))
                link(dve.tensor_scalar(tq[:, :], tv[:, :], tb[0:1, e + 1:e + 2], None, ALU.is_ge))
                link(dve.tensor_tensor(te[:, :], te[:, :], tq[:, :], ALU.add))
                link(dve.scalar_tensor_tensor(tr_[:, :], tq[:, :], nt[0:1, e:e + 1], tr_[:, :], ALU.mult, ALU.add))
            link(dve.tensor_tensor(tr_[:, :], tv[:, :], tr_[:, :], ALU.subtract))
            link(dve.tensor_scalar(tf[:, :], te[:, :], float(REG), None, ALU.mult))
            link(dve.scalar_tensor_tensor(tr_[:, :], tr_[:, :], float(P), tf[:, :], ALU.mult, ALU.add))
            link(dve.tensor_scalar(tr_[:, :], tr_[:, :], float(NEXP * REG), None, ALU.min))
            link(dve.tensor_copy(m.tile_row[0:1, :], tr_[:, :]))
            link(dve.tensor_scalar(te[:, :], te[:, :], float(NEXP - 1), None, ALU.min))
            link(dve.tensor_copy(m.tile_exp[0:1, :], te[:, :]))


def experts(nc, m, a):
    take = Place(m, 0)
    r = take("in_rows", [P, 2, 2, RW], F32)
    x1t, outt = take("x1_rows", [P, 2, 2, C], F32), take("out_rows", [P, 2, 2, C], F32)
    bd = take("bdB", [P, NEXP, C], F32)
    h_hi, h_lo = take("eh_hi", [P, 2, KH, 2 * P], F16), take("eh_lo", [P, 2, KH, 2 * P], F16)
    ex, su, pr = take("ex", [P, 2, NEXP], F32), take("su", [P, 2], F32), take("pr", [P, 2], F32)
    y = take("y", [P, 2, C], F32)
    assert take.next <= 52224
    u = up_tensors(nc, m, "j")
    S = m.sem
    s_bd, s_hi, s_dn, s_dnfree, s_ex, s_pr, s_out, s_su, s_used = (S("j_" + n) for n in (
        "bd", "hi", "dn", "dnfree", "ex", "pr", "out", "su", "used"))
    s_row = [S("j_row0"), S("j_row1")]
    s_gx = [S("j_gx0"), S("j_gx1")]
    s_st = [S("j_st0"), S("j_st1")]
    NPAIR = MAXT // 2
    DB = 5

    def pairs(eng, step):
        with eng.Fori(0, NPAIR // 2) as k:
            step(eng, 2 * k, 0, k)
            step(eng, 2 * k + 1, 1, k)

    with nc.Block() as block:
        @block.sync
        def _(sp):
            sp.dma_start(bd[:, :, :].rearrange("p e c -> p (e c)"), bass.AP(a.fbd.tensor, 0, [[0, P], [1, NEXP * C]])).then_inc(s_bd, 16)

            def step(sp, i, par, k):
                sp.wait_ge(s_used, i + 1)
                for j in range(2):
                    at = sp.value_load(m.tile_row[0:1, bass.ds(2 * i + j, 1)], min_val=0, max_val=NEXP * REG)
                    sp.dma_start(r[:, par, j, :], m.sorted_rows[bass.ds(at, P), :]).then_inc(s_row[par], 16)
            pairs(sp, step)
            sp.wait_ge(s_bd, 16)

        @block.gpsimd
        def _(pool):
            def step(pool, i, par, k):
                pool.wait_ge(s_row[par], k * 32 + 32)
                pool.wait_ge(s_used, i + 1)
                for j in range(2):
                    pool.indirect_dma_start(x1t[:, par, j, :], None, m.x1_dram,
                                            bass.IndirectOffsetOnAxis(ap=r[:, par, j, RW - 1:RW].bitcast(I32), axis=0)).then_inc(s_gx[par], 16)
                if i:
                    store(pool, i - 1, 1 - par, k if par else k - 1)

            def store(pool, i, par, k):
                pool.wait_ge(s_out, i + 1)
                for j in range(2):
                    pool.indirect_dma_start(a.out, bass.IndirectOffsetOnAxis(ap=r[:, par, j, RW - 1:RW].bitcast(I32), axis=0),
                                            outt[:, par, j, :], None, bounds_check=N - 1, oob_is_err=False).then_inc(s_st[par], 16)
                pool.wait_ge(s_st[par], k * 32 + 32)
                pool.sem_inc(s_used, 1)
            pool.sem_inc(s_used, 2)
            for i in range(NPAIR):
                step(pool, i, i % 2, i // 2)
            store(pool, NPAIR - 1, 1, NPAIR // 2 - 1)

        @block.tensor
        def _(pe):
            pe.sem_inc(u.up, 2 * KH)

            def rows(par):
                return lambda j, k: r[:, par, j, k * P:(k + 1) * P]

            def down(pe, i, par):
                for j in range(2):
                    e = pe.value_load(m.tile_exp[0:1, bass.ds(2 * i + j, 1)], min_val=0, max_val=NEXP - 1)
                    if j == 0:
                        pe.wait_ge(u.split, KH * i + (KH + 2))
                    pe.wait_ge(s_dnfree, 2 * i + (j + 1))
                    for k in range(KH):
                        w_hi = m.wd_hi[:, bass.ds(e, 1), k, :].rearrange("p a c -> p (a c)")
                        w_lo = m.wd_lo[:, bass.ds(e, 1), k, :].rearrange("p a c -> p (a c)")
                        for q, (h, w) in enumerate(((h_hi, w_hi), (h_hi, w_lo), (h_lo, w_hi))):
                            last = pe.matmul(m.ps[:, DB + j, 0:C], h[:, par, k, j * P:(j + 1) * P], w,
                                             start=q == 0 and k == 0, stop=q == 2 and k == KH - 1)
                    last.then_inc(s_dn, 1)

            def up_all(pe, i, par):
                for h in range(KH):
                    pe_up(pe, m, u, i, par, 2, h)

            pe.wait_ge(s_row[0], 32)
            pe_transpose(pe, m, u, 0, rows(0), 2)
            up_all(pe, 0, 0)
            pe.wait_ge(s_row[1], 32)
            pe_transpose(pe, m, u, 1, rows(1), 2)

            def step(pe, i, par, k):
                up_all(pe, i + 1, 1 - par)
                down(pe, i, par)

            with pe.Fori(0, NPAIR // 2 - 1) as k:
                step(pe, 2 * k, 0, k)
                pe.wait_ge(s_row[0], k * 32 + 64)
                pe_transpose(pe, m, u, 2 * k + 2, rows(0), 2)
                step(pe, 2 * k + 1, 1, k)
                pe.wait_ge(s_row[1], k * 32 + 64)
                pe_transpose(pe, m, u, 2 * k + 3, rows(1), 2)
            step(pe, NPAIR - 2, 0, 0)
            down(pe, NPAIR - 1, 1)

        @block.scalar
        def _(act):
            act.sem_inc(u.gelu, UB)

            def step(act, i, par, k):
                act_xt(act, m, u, i, par, 2)
                act.wait_ge(s_su, i + 1)
                act.activation(ex[:, :, :], r[:, par, :, C:C + NEXP], ACT.Exp).then_inc(s_ex, 1)
                act.wait_ge(u.split, KH * i + 2)
                for h in range(KH):
                    act.wait_ge(u.up, i * KH + (h + 1 + 2 * KH))
                    act.activation(m.hf[:, h, :], m.ps[:, h % UB, 0:2 * P], ACT.Gelu, bias=m.b1f[:, h:h + 1]).then_inc(u.gelu, 1)
            pairs(act, step)

        @block.vector
        def _(dve):
            dve.sem_inc(u.xt, 1)
            dve.sem_inc(u.split, 2)
            dve.sem_inc(s_dnfree, 2)
            dve.sem_inc(s_su, 1)

            def halves(dve, i, par):
                for h in range(KH):
                    dve.wait_ge(u.gelu, i * KH + (h + 1 + UB))
                    dve.tensor_scalar(h_hi[:, par, h, :], m.hf[:, h, :], m.beta[:, h:h + 1], None, ALU.mult).then_inc(s_hi, 1)
                for h in range(KH):
                    dve.wait_ge(s_hi, i * KH + (h + 1))
                    dve.scalar_tensor_tensor(h_lo[:, par, h, :], m.hf[:, h, :], m.beta[:, h:h + 1], h_hi[:, par, h, :],
                                             ALU.mult, ALU.subtract).then_inc(u.split, 1)

            def probability(dve, i):
                dve.wait_ge(s_ex, i + 1)
                dve.tensor_reduce(su[:, :], ex[:, :, :], AX.X, ALU.add).then_inc(s_su, 1)
                dve.wait_ge(s_su, i + 2)
                dve.reciprocal(pr[:, :], su[:, :]).then_inc(s_pr, 1)

            def results(dve, i, par, k):
                dve.wait_ge(s_pr, i + 1)
                dve.wait_ge(s_gx[par], k * 32 + 32)
                for j in range(2):
                    e = dve.value_load(m.tile_exp[0:1, bass.ds(2 * i + j, 1)], min_val=0, max_val=NEXP - 1)
                    dve.wait_ge(s_dn, 2 * i + (j + 1))
                    dve.scalar_tensor_tensor(y[:, j, :], m.ps[:, DB + j, 0:C], m.inv_g[:, 0:1],
                                             bd[:, bass.ds(e, 1), :].rearrange("p a c -> p (a c)"), ALU.mult, ALU.add).then_inc(s_dnfree, 1)
                dve.wait_ge(s_dnfree, 2 * i + 4)
                for j in range(2):
                    last = dve.scalar_tensor_tensor(outt[:, par, j, :], y[:, j, :], pr[:, j:j + 1], x1t[:, par, j, :], ALU.mult, ALU.add)
                last.then_inc(s_out, 1)

            dve.wait_ge(s_bd, 16)
            dve_xt(dve, m, u, 0, 0, 2)
            halves(dve, 0, 0)
            dve_xt(dve, m, u, 1, 1, 2)
            with dve.Fori(0, NPAIR // 2 - 1) as k:
                for q in range(2):
                    i = 2 * k + q
                    probability(dve, i)
                    results(dve, i, q, k)
                    halves(dve, i + 1, 1 - q)
                    dve_xt(dve, m, u, i + 2, q, 2)
            probability(dve, NPAIR - 2)
            results(dve, NPAIR - 2, 0, NPAIR // 2 - 1)
            halves(dve, NPAIR - 1, 1)
            probability(dve, NPAIR - 1)
            results(dve, NPAIR - 1, 1, NPAIR // 2 - 1)


def lay_out(inputs):
    import numpy as np
    named = {"x": inputs["x"], "src": inputs["src"], "dst": inputs["dst"],
             "w1t": inputs["L0_gnn_W1"].T, "g1": inputs["L0_gnn_g1"], "b1": inputs["L0_gnn_b1"],
             "w2t": inputs["L0_gnn_W2"].T, "g2": inputs["L0_gnn_g2"], "b2": inputs["L0_gnn_b2"],
             "fw1": inputs["L0_ffn_W1"], "fb1": inputs["L0_ffn_b1"], "fwg": inputs["L0_ffn_Wg"],
             "fbg": inputs["L0_ffn_bg"], "fwd": inputs["L0_ffn_Wd"], "fbd": inputs["L0_ffn_bd"]}
    return {k: np.ascontiguousarray(v) for k, v in named.items()}


def kernel(**inputs):
    import numpy as np
    import concourse.bacc as bacc
    from concourse.bass_utils import run_bass_kernel_spmd
    arrays = lay_out(inputs)
    nc = bacc.Bacc("TRN2", target_bir_lowering=False, num_devices=1)
    aps = [nc.dram_tensor(name, v.shape, mybir.dt.from_np(v.dtype), kind="ExternalInput").ap()
           for name, v in arrays.items()]
    out = nc.dram_tensor("out", (N, C), F32, kind="ExternalOutput").ap()
    gnn_ffn_kernel(nc, *aps, out)
    nc.compile()
    res = run_bass_kernel_spmd(nc, [arrays], core_ids=[0])
    return np.asarray(res.results[0]["out"])
```

```python
from contextlib import ExitStack

import concourse.bass as bass
from concourse import mybir

F32, F16, I32, F32R = mybir.dt.float32, mybir.dt.float16, mybir.dt.int32, mybir.dt.float32r
ACT = mybir.ActivationFunctionType
ALU = mybir.AluOpType
AX = mybir.AxisListType

P = 128
N, C, IC, HID, NEXP, NE = 6250, 256, 512, 1024, 8, 100000
EPS = 1e-5
NT = -(-N // P)
NP_ = NT * P
LAST = N - (NT - 1) * P
KC, KI, KH = C // P, IC // P, HID // P
WIN = 5
NW = N // WIN
SB = 250
NSB = N // SB
WPS = SB // WIN
GRP = 2
GPS = WPS // GRP
WP, WJ = 125, 10
KEYS = WIN * NT
RING = 5
NTE = -(-NE // P)
ROW = 8
NROWS = 12512
EPAD = 783 * P
PADROW = NE // ROW
FAR = 1 << 20
T1SCALE = 2048.0


def gnn_ffn_kernel(nc, x, src, dst, w1t, g1, b1, w2t, g2, b2, fw1, fb1, fwg, fbg, fwd, fbd, out, upto=99):
    with ExitStack() as ctx:
        m = Names()
        m.sem = lambda name: ctx.enter_context(nc.semaphore(name))
        base = 16512

        def at(name, off, shape, dt):
            return nc.alloc_sbuf_tensor_at(name, shape, dt, offset=base + off)

        R1, R2, R3, R4, R5 = 0, 52224, 102400, 152576, 177664
        END = 229368 - base
        m.at = at
        m.r1, m.r2, m.r3, m.r4, m.r5 = R1, R2, R3, R4, R5
        m.x = at("x_sb", R3, [P, NT, C], F32)
        m.table1 = at("table1", R1, [P, NT, 2 * C], F16)
        m.table2 = at("table2", R2, [P, NT, 2 * C], F16)
        m.agg1 = at("agg1", R2, [P, KC, NP_], F32)
        m.agg2 = at("agg2", R1, [P, KC, NP_], F32)
        m.adj = at("adj", R3, [P, 2, NT, SB], F16)
        m.probs = at("probs", R2 - 256, [P, NT], F32)
        m.rows = at("rows", R1, [P, NT, RW], F32)
        m.disB = at("disB", R4, [P, NP_], F32)
        m.h01 = at("h01", R1, [P, 2, NP_], F32)
        m.h23 = at("h23", R3, [P, 2, NP_], F32)
        m.end = END
        take = Place(m, R5)

        def small(name, shape, dt):
            return take(name, [P, *shape], dt)

        m.key = small("key", [WJ, WP + WPS // WJ], F32)
        m.rem = small("rem", [WJ, WP + WPS // WJ], F32)
        m.id32 = small("id32", [P], F32)
        m.id16 = small("id16", [P], F16)
        m.iota_r = small("iota_r", [P], F16)
        m.iota_k = small("iota_k", [KEYS + 1], F16)
        m.ones = small("ones", [P], F32)
        m.disP = small("disP", [NT], F32)
        m.mean = small("mean", [NT], F32)
        m.rstd = small("rstd", [NT], F32)
        m.levels = small("levels", [1], I32)
        m.row0 = small("row0", [WJ], F32)
        m.w5 = small("w5", [WJ], F32)
        m.step16 = small("step16", [1], F32)
        m.bn_g1 = small("bn_g1", [KI], F32)
        m.bn_b1 = small("bn_b1", [KI], F32)
        m.bn_g2 = small("bn_g2", [KC], F32)
        m.bn_b2 = small("bn_b2", [KC], F32)
        m.aff_a1 = small("aff_a1", [KI], F32)
        m.aff_b1 = small("aff_b1", [KI], F32)
        m.scale2 = small("scale2", [1], F32)
        m.sc_col = small("sc_col", [8], F32)
        m.alpha = small("alpha", [KH], F32)
        m.beta = small("beta", [KH], F32)
        m.inv_g = small("inv_g", [1], F32)
        m.b1f = small("b1f", [KH], F32)
        m.reg_base = small("reg_base", [NEXP], F32)
        m.tile_row = small("tile_row", [64], I32)
        m.tile_exp = small("tile_exp", [64], I32)
        m.stats1 = small("stats1", [KI, NSB, 6], F32)
        m.work = take.next
        m.ps = ctx.enter_context(nc.psum_tensor("ps", [P, 8, 512], F32))
        m.src_pad = nc.dram_tensor("src_pad", [EPAD], I32, kind="Internal").ap()
        m.dst_pad = nc.dram_tensor("dst_pad", [EPAD], I32, kind="Internal").ap()
        m.edge_rows = nc.dram_tensor("edge_rows", [NROWS, 2 * P], I32, kind="Internal").ap()
        m.first_dram = nc.dram_tensor("first_dram", [(NT + 1) * P], F32, kind="Internal").ap()
        m.dis_dram = nc.dram_tensor("dis_dram", [NP_], F32, kind="Internal").ap()
        m.sorted_rows = nc.dram_tensor("sorted_rows", [(NEXP + 1) * REG, RW], F32, kind="Internal").ap()
        m.x1_dram = nc.dram_tensor("x1_dram", [NP_, C + 1], F32, kind="Internal").ap()
        m.s_chain, m.chained = m.sem("chain"), 0
        args = Names()
        args.x, args.src, args.dst, args.out = x, src, dst, out
        args.w1t, args.g1, args.b1, args.w2t, args.g2, args.b2 = w1t, g1, b1, w2t, g2, b2
        args.fw1, args.fb1, args.fwg, args.fbg, args.fwd, args.fbd = fw1, fb1, fwg, fbg, fwd, fbd
        m.s_align = [m.sem(f"align_{n}") for n in ("dve", "rowi", "edges", "keyw", "keyt", "spare")]
        prepare(nc, m, args)
        if upto < 2: return m
        ffn_scales(nc, m, args)
        build_table1(nc, m, args)
        m.agg = aggregate_tensors(m)
        aggregate(nc, m, 0, m.table1, m.agg1)
        if upto < 3: return m
        linear1(nc, m, args)
        if upto < 4: return m
        linear2(nc, m, args)
        aggregate(nc, m, 1, m.table2, m.agg2)
        if upto < 5: return m
        finish_gnn(nc, m, args)
        if upto < 6: return m
        ffn(nc, m, args)
        return m


class Names:
    pass


class Place:

    def __init__(self, m, start):
        self.m, self.next = m, start

    def __call__(self, name, shape, dt):
        size = mybir.dt.size(dt)
        for n in shape[1:]:
            size *= n
        t = self.m.at(name, self.next, shape, dt)
        self.next += -(-size // 32) * 32
        assert self.next <= self.m.end, (name, self.next - self.m.end)
        return t


def align_edges(m, t, eng, name, runs, level0):
    if name == "vector":
        if level0:
            eng.tensor_copy(t.rowf[:, :], m.row0[:WP, :]).then_inc(t.s_dve, 1)
        else:
            eng.tensor_scalar(t.rowf[:, :], m.row0[:WP, :], m.step16[:WP, 0:1], float(PADROW), ALU.add, ALU.min).then_inc(t.s_dve, 1)
        eng.wait_ge(t.s_dve, runs * 6 + 1)
        eng.tensor_copy(t.rowi[:, :], t.rowf[:, :]).then_inc(t.s_rowi, 1)
        eng.wait_ge(t.s_edges, (runs + 1) * 16 * WJ)
        eng.wait_ge(t.s_spare, runs + 1)
        dstv = t.edges[:, :, P:2 * P]
        srcv = t.edges[:, :, 0:P]
        eng.tensor_tensor(t.dl[:, :, :], dstv, m.w5[:WP, :].unsqueeze(2).to_broadcast([WP, WJ, P]), ALU.subtract).then_inc(t.s_dve, 1)
        eng.tensor_scalar(t.chunk[:, :, :], srcv, 7, None, ALU.arith_shift_right).then_inc(t.s_dve, 1)
        eng.tensor_scalar(t.lowi[:, :, :], srcv, P - 1, None, ALU.bitwise_and).then_inc(t.s_dve, 1)
        eng.wait_ge(t.s_dve, runs * 6 + 4)
        eng.scalar_tensor_tensor(t.keyw[:, :, :], t.dl[:, :, :], float(NT), t.chunk[:, :, :], ALU.mult, ALU.add).then_inc(t.s_keyw, 1)
        eng.tensor_copy(t.lowf[:, :, :], t.lowi[:, :, :]).then_inc(t.s_keyw, 1)
        for b in range(5):
            eng.wait_ge(t.s_keyt, runs * 5 + b + 1)
            for q in range(4):
                k = 4 * b + q
                dest = (m.key if k < WJ else m.rem)[:, k % WJ, 0:WP]
                last = eng.tensor_copy(dest, m.ps[:, b, q * WP:(q + 1) * WP])
            if b == 4:
                last.then_inc(t.s_dve, 2)
        eng.wait_ge(t.s_dve, runs * 6 + 6)
    elif name == "gpsimd":
        eng.wait_ge(t.s_rowi, runs + 1)
        eng.tensor_tensor(t.spare[:, :], t.rowf[:, :], t.rowf[:, :], ALU.add).then_inc(t.s_spare, 1)
        for j in range(WJ):
            eng.indirect_dma_start(t.edges[:, j, :], None, m.edge_rows,
                                   bass.IndirectOffsetOnAxis(ap=t.rowi[:, j:j + 1], axis=0)).then_inc(t.s_edges, 16)
    elif name == "tensor":
        eng.wait_ge(t.s_keyw, runs * 2 + 2)
        for k in range(2 * WJ):
            b, q = divmod(k, 4)
            from_ = (t.keyw if k < WJ else t.lowf)[:, k % WJ, :]
            ins = eng.transpose(m.ps[:, b, q * WP:(q + 1) * WP], from_, m.id32[:WP, :WP])
            if q == 3:
                ins.then_inc(t.s_keyt, 1)


def align_tensors(m, tag, off):
    t = Names()
    t.s_dve, t.s_rowi, t.s_edges, t.s_keyw, t.s_keyt, t.s_spare = m.s_align
    t.edges = m.at(f"edges_{tag}", off, [WP, WJ, 2 * P], I32)
    t.dl = m.at(f"dl_{tag}", off + 10240, [WP, WJ, P], F32)
    t.chunk = m.at(f"chunk_{tag}", off + 15360, [WP, WJ, P], I32)
    t.lowi = m.at(f"lowi_{tag}", off + 20480, [WP, WJ, P], I32)
    t.keyw = m.at(f"keyw_{tag}", off + 25600, [WP, WJ, P], F32)
    t.lowf = m.at(f"lowf_{tag}", off + 30720, [WP, WJ, P], F32)
    t.rowf = m.at(f"rowf_{tag}", off + 35840, [WP, WJ], F32)
    t.spare = m.at(f"spare_{tag}", off + 35968, [WP, WJ], F32)
    t.rowi = m.at(f"rowi_{tag}", off + 35904, [WP, WJ], I32)
    return t


def prepare(nc, m, a):
    NHALF = NTE // 2
    off = m.r4
    head_i = m.at("head_i", off, [1, NTE], I32)
    head_f = m.at("head_f", off + 3136, [1, NTE], F32)
    heads = m.at("heads", off + 6272, [P, NTE], F32)
    junk = m.at("junk", off + 9408, [P, 2, NTE], F16)
    near = m.at("near", 0, [P, NT, P], I32)
    less = m.at("less", m.r2, [P, NT, P], F16)
    take = Place(m, m.work)
    padt = take("padt", [1, 2, EPAD - NE], I32)
    far_f = take("far_f", [1, P], F32)
    nodes, tcnt, rowf = take("nodes", [P, NT], F32), take("tcnt", [P, NT], F32), take("nrowf", [P, NT], F32)
    rowi = take("nrowi", [P, NT], I32)
    cnt, first = take("cnt", [P, NT], F32), take("first", [P, NT], F32)
    firstT, nextT = take("firstT", [NT, P], F32), take("nextT", [NT, P], F32)
    degT, disT = take("degT", [NT, P], F32), take("disT", [NT, P], F32)
    mhalfT = take("mhalfT", [P, P], F32)
    wa, wb = take("win_a", [WP, 5 * WJ], F32), take("win_b", [WP, 5 * WJ], F32)
    wi, wi8 = take("win_i", [WP, WJ], I32), take("win_i8", [WP, WJ], I32)
    wn, wm = take("win_n", [WP, WJ], F32), take("win_m", [WP, 1], F32)
    lv, lvi = take("lv", [1, 4], F32), take("lvi", [1, 4], I32)
    st, mv, vare = take("ln_st", [P, NT, 6], F32), take("ln_mv", [P, NT, 2], F32), take("vare", [P, NT], F32)
    t = align_tensors(m, "pa", m.r2 + 12544)
    S = m.sem
    s_x, s_heads, s_pads, s_pad_mem, s_copy, s_rows = S("a_x"), S("a_heads"), S("a_pads"), S("a_pad_mem"), S("a_copy"), S("a_rows")
    s_const, s_headf, s_headp, s_nrow, s_near, s_first, s_firstT = S("a_const"), S("a_headf"), S("a_headp"), S("a_nrow"), S("a_near"), S("a_first"), S("a_firstT")
    s_firstS, s_fd, s_next, s_deg, s_dis, s_disd, s_disB = S("a_firstS"), S("a_fd"), S("a_next"), S("a_deg"), S("a_dis"), S("a_disd"), S("a_disB")
    s_disT, s_wm, s_wmT, s_vare, s_rstd, s_par, s_xtail = S("a_disT"), S("a_wm"), S("a_wmT"), S("a_vare"), S("a_rstd"), S("a_par"), S("a_xtail")

    with nc.Block() as block:
        @block.sync
        def _(sp):
            with nc.allow_non_contiguous_dma("the first dst of each edge tile"):
                sp.dma_start(head_i[0:1, :], bass.AP(a.dst.tensor, 0, [[P, 1], [P, NTE]])).then_inc(s_heads, 16)
            sp.dma_start(m.dst_pad[0:NE], a.dst).then_inc(s_copy, 16)
            sp.dma_start(m.src_pad[0:NE], a.src).then_inc(s_copy, 16)
            sp.wait_ge(s_pad_mem, 1)
            sp.dma_start(m.src_pad[NE:EPAD].rearrange("(a n) -> a n", a=1), padt[0:1, 0, :]).then_inc(s_pads, 16)
            sp.dma_start(m.dst_pad[NE:EPAD].rearrange("(a n) -> a n", a=1), padt[0:1, 1, :]).then_inc(s_pads, 16)
            sp.dma_start(m.first_dram[NP_:NP_ + P].rearrange("(a n) -> a n", a=1), far_f[0:1, :]).then_inc(s_pads, 16)
            for i in range(6):
                sp.dma_start(m.x[:, 8 * i:8 * i + 8, :],
                             a.x[1024 * i:1024 * (i + 1), :].rearrange("(t p) c -> p t c", p=P)).then_inc(s_x, 16)
            sp.wait_ge(s_xtail, 1)
            sp.dma_start(m.x[:LAST, NT - 1, :], a.x[(NT - 1) * P:N, :]).then_inc(s_x, 16)
            sp.wait_ge(s_copy, 32)
            sp.wait_ge(s_pads, 48)
            for k, pad in enumerate((m.src_pad, m.dst_pad)):
                sp.dma_start(m.edge_rows[:, k * P:(k + 1) * P],
                             bass.AP(pad.tensor, 0, [[ROW, NROWS], [1, P]])).then_inc(s_rows, 16)
            with nc.allow_non_contiguous_dma("batch norm's parameters to partitions"):
                sp.dma_start(m.bn_g1[:, :], a.g1.rearrange("(f p) -> p f", p=P)).then_inc(s_par, 16)
                sp.dma_start(m.bn_b1[:, :], a.b1.rearrange("(f p) -> p f", p=P)).then_inc(s_par, 16)
                sp.dma_start(m.bn_g2[:, :], a.g2.rearrange("(f p) -> p f", p=P)).then_inc(s_par, 16)
                sp.dma_start(m.bn_b2[:, :], a.b2.rearrange("(f p) -> p f", p=P)).then_inc(s_par, 16)
            sp.wait_ge(s_firstS, 1)
            sp.dma_start(m.first_dram[0:NP_].rearrange("(t p) -> t p", p=P), firstT[:, :]).then_inc(s_fd, 16)
            sp.wait_ge(s_fd, 16)
            sp.dma_start(nextT[:, :], m.first_dram[1:NP_ + 1].rearrange("(t p) -> t p", p=P)).then_inc(s_next, 16)
            sp.dma_start(wa[:, :], m.first_dram[0:N].rearrange("(p w) -> p w", p=WP)).then_inc(s_next, 16)
            sp.dma_start(wb[:, :], m.first_dram[WIN:N + WIN].rearrange("(p w) -> p w", p=WP)).then_inc(s_next, 16)
            sp.wait_ge(s_dis, 1)
            sp.dma_start(m.dis_dram.rearrange("(t p) -> t p", p=P), disT[:, :]).then_inc(s_disd, 16)
            sp.wait_ge(s_disd, 16)
            sp.dma_start(m.disB[:, :], bass.AP(m.dis_dram.tensor, 0, [[0, P], [1, NP_]])).then_inc(s_disB, 16)
            sp.wait_ge(s_par, 64)
            sp.wait_ge(s_disB, 16)

        @block.gpsimd
        def _(pool):
            pool.iota(nodes[:, :], [[P, NT]], base=0, channel_multiplier=1, allow_small_or_imprecise_dtypes=True).then_inc(s_const, 1)
            pool.memset(m.id32[:, :], 0.0).then_inc(s_const, 1)
            pool.memset(m.id16[:, :], 0.0).then_inc(s_const, 1)
            pool.memset(mhalfT[:, :], -0.5).then_inc(s_const, 1)
            pool.wait_ge(s_const, 4)
            for mat in (m.id32, m.id16):
                pool.affine_select(out=mat[:, :], in_=mat[:, :], compare_op=ALU.not_equal, fill=1.0,
                                   base=0, pattern=[[-1, P]], channel_multiplier=1).then_inc(s_const, 1)
            pool.iota(m.iota_r[:, :], [[1, P]], base=0, channel_multiplier=0, allow_small_or_imprecise_dtypes=True).then_inc(s_const, 1)
            pool.iota(m.iota_k[:, :], [[1, KEYS + 1]], base=0, channel_multiplier=0, allow_small_or_imprecise_dtypes=True).then_inc(s_const, 1)
            pool.iota(m.w5[:WP, :], [[WIN, WJ]], base=0, channel_multiplier=WIN * WJ, allow_small_or_imprecise_dtypes=True).then_inc(s_const, 1)
            pool.wait_ge(s_nrow, 1)
            pool.wait_ge(s_copy, 32)
            pool.wait_ge(s_pads, 48)
            for i in range(NT):
                pool.indirect_dma_start(near[:, i, :], None, m.dst_pad.rearrange("(t p) -> t p", p=P),
                                        bass.IndirectOffsetOnAxis(ap=rowi[:, i:i + 1], axis=0)).then_inc(s_near, 16)
            pool.wait_ge(s_vare, 1)
            pool.tensor_tensor(m.rstd[:, :], vare[:, :], mhalfT[:, :NT], ALU.pow).then_inc(s_rstd, 1)
            pool.wait_ge(s_deg, 1)
            pool.tensor_tensor(disT[:, :], degT[:, :], mhalfT[:NT, :], ALU.pow).then_inc(s_dis, 1)
            pool.wait_ge(s_rows, 32)
            align_edges(m, t, pool, "gpsimd", 0, True)

        @block.tensor
        def _(pe):
            pe.wait_ge(s_headf, 2)
            for k in range(2):
                pe.matmul(m.ps[:, k, 0:NHALF], m.ones[0:1, :], head_f[0:1, k * NHALF:(k + 1) * NHALF],
                          start=True, stop=True).then_inc(s_headp, 1)
            pe.wait_ge(s_const, 6)
            pe.wait_ge(s_first, 1)
            pe.transpose(m.ps[:NT, 2, 0:P], first[:, :], m.id32[:, :]).then_inc(s_firstT, 1)
            pe.wait_ge(s_wm, 1)
            pe.transpose(m.ps[:1, 3, 0:WP], wm[:, :], m.id32[:WP, :WP]).then_inc(s_wmT, 1)
            pe.wait_ge(s_dis, 1)
            pe.transpose(m.ps[:, 4, 0:NT], disT[:, :], m.id32[:NT, :NT]).then_inc(s_disT, 1)
            align_edges(m, t, pe, "tensor", 0, True)

        @block.vector
        def _(dve):
            link = chain_on(m, dve)
            dve.memset(m.ones[:, :], 1.0).then_inc(s_headf, 1)
            for t_ in (m.key, m.rem):
                dve.memset(t_[:, :, WP:], 0.0)
            link(dve.memset(far_f[:, :], float(NE)))
            link(dve.memset(padt[:, 0, :], 0))
            dve.memset(padt[:, 1, :], FAR).then_inc(s_pad_mem, 1)
            dve.memset(m.x[:, NT - 1, :], 0.0).then_inc(s_xtail, 1)
            link(dve.memset(m.step16[:, :], 0.0))
            dve.wait_ge(s_heads, 16)
            dve.tensor_copy(head_f[:, :], head_i[:, :]).then_inc(s_headf, 1)
            dve.wait_ge(s_headp, 2)
            link(dve.tensor_copy(heads[:, :].rearrange("p (k n) -> p k n", k=2), m.ps[:, 0:2, 0:NHALF]))
            dve.wait_ge(s_const, 1)
            for i in range(NT):
                if i >= 2:
                    dve.wait_ge(m.s_chain, m.chained - 1)
                m.chained += 1
                dve.tensor_scalar(junk[:, i % 2, :], heads[:, :], nodes[:, i:i + 1], None, ALU.is_lt, ALU.add,
                                  accum_out=tcnt[:, i:i + 1]).then_inc(m.s_chain, 1)
            dve.wait_ge(m.s_chain, m.chained)
            link(dve.tensor_scalar(rowf[:, :], tcnt[:, :], -1.0, 0.0, ALU.add, ALU.max))
            dve.tensor_copy(rowi[:, :], rowf[:, :]).then_inc(s_nrow, 1)
            dve.wait_ge(s_x, 16 * 7)
            for i in range(NT):
                last = dve.bn_stats(st[:, i, :], m.x[:, i, :])
            link(last)
            for i in range(NT):
                last = dve.bn_aggr(mv[:, i, :], st[:, i, :])
            link(last)
            dve.tensor_copy(m.mean[:, :], mv[:, :, 0])
            dve.tensor_scalar(vare[:, :], mv[:, :, 1], EPS, None, ALU.add).then_inc(s_vare, 1)
            dve.wait_ge(s_near, 16 * NT)
            link(dve.tensor_tensor(less[:, :, :], near[:, :, :], nodes[:, :].unsqueeze(2).to_broadcast([P, NT, P]), ALU.is_lt))
            link(dve.tensor_reduce(cnt[:, :], less[:, :, :], AX.X, ALU.add))
            dve.scalar_tensor_tensor(first[:, :], rowf[:, :], float(P), cnt[:, :], ALU.mult, ALU.add).then_inc(s_first, 1)
            dve.wait_ge(s_firstT, 1)
            dve.tensor_copy(firstT[:, :], m.ps[:NT, 2, 0:P]).then_inc(s_firstS, 1)
            dve.wait_ge(s_next, 48)
            link(dve.tensor_tensor(degT[:, :], nextT[:, :], firstT[:, :], ALU.subtract))
            dve.tensor_scalar(degT[:, :], degT[:, :], 1.0, None, ALU.add).then_inc(s_deg, 1)
            link(dve.tensor_copy(wi[:, :], wa[:, 0::WIN]))
            link(dve.tensor_scalar(wi8[:, :], wi[:, :], 3, None, ALU.arith_shift_right))
            link(dve.tensor_copy(m.row0[:WP, :], wi8[:, :]))
            link(dve.scalar_tensor_tensor(wn[:, :], m.row0[:WP, :], float(-ROW), wb[:, 0::WIN], ALU.mult, ALU.add))
            dve.tensor_reduce(wm[:, :], wn[:, :], AX.X, ALU.max).then_inc(s_wm, 1)
            dve.wait_ge(s_wmT, 1)
            link(dve.tensor_reduce(lv[:, 0:1], m.ps[:1, 3, 0:WP], AX.X, ALU.max))
            link(dve.tensor_scalar(lv[:, 1:2], lv[:, 0:1], float(P - 1), float(P), ALU.add, ALU.max))
            link(dve.tensor_copy(lvi[:, 0:1], lv[:, 1:2]))
            link(dve.tensor_scalar(m.levels[0:1, :], lvi[:, 0:1], 7, None, ALU.arith_shift_right))
            dve.wait_ge(s_disT, 1)
            link(dve.tensor_copy(m.disP[:, :], m.ps[:, 4, 0:NT]))
            dve.wait_ge(s_rstd, 1)
            align_edges(m, t, dve, "vector", 0, True)


def build_table1(nc, m, a):
    scale = m.at("t1_scale", m.work, [P, NT], F32)
    xs, xs32 = m.x, m.x
    s_scale, s_xs, s_hi, s_lo = m.sem("b_scale"), m.sem("b_xs"), m.sem("b_hi"), m.sem("b_lo")
    groups = [(4 * g, min(4, NT - 4 * g)) for g in range(-(-NT // 4))]
    def low_half(dve, g):
        t0, k = groups[g]
        dve.wait_ge(s_hi, g + 1)
        dve.tensor_tensor(m.table1[:, t0:t0 + k, C:], xs[:, t0:t0 + k, :], m.table1[:, t0:t0 + k, :C],
                          ALU.subtract).then_inc(s_lo, 1)

    with nc.Block() as block:
        @block.vector
        def _(dve):
            dve.scalar_tensor_tensor(scale[:, :], m.rstd[:, :], T1SCALE, m.disP[:, :], ALU.mult, ALU.mult).then_inc(s_scale, 1)
            dve.wait_ge(s_scale, 1)
            for g, (t0, k) in enumerate(groups):
                for i in range(t0, t0 + k):
                    last = dve.tensor_scalar(xs[:, i, :], m.x[:, i, :], m.mean[:, i:i + 1], scale[:, i:i + 1],
                                             ALU.subtract, ALU.mult)
                last.then_inc(s_xs, 1)
                if g >= 1:
                    low_half(dve, g - 1)
            low_half(dve, len(groups) - 1)

        @block.scalar
        def _(act):
            for g, (t0, k) in enumerate(groups):
                act.wait_ge(s_xs, g + 1)
                act.activation(m.table1[:, t0:t0 + k, :C], xs[:, t0:t0 + k, :], ACT.Copy).then_inc(s_hi, 1)
    self_loops(nc, m, "l1", m.table1, m.agg1)


def self_loops(nc, m, tag, table, agg):
    s_tr, s_ev = m.sem(f"{tag}_tr"), m.sem(f"{tag}_ev")
    groups = [(4 * g, min(4, NT - 4 * g)) for g in range(-(-NT // 4))]
    with nc.Block() as block:
        @block.tensor
        def _(pe):
            for g, (t0, k) in enumerate(groups):
                for h in range(KC):
                    n = g * KC + h
                    if n >= 8:
                        pe.wait_ge(s_ev, n - 7)
                    for i in range(k):
                        for half in range(2):
                            last = pe.matmul(m.ps[:, n % 8, i * P:(i + 1) * P],
                                             table[:, t0 + i, half * C + h * P:half * C + (h + 1) * P], m.id16[:, :],
                                             start=half == 0, stop=half == 1)
                    last.then_inc(s_tr, 1)

        @block.scalar
        def _(act):
            for g, (t0, k) in enumerate(groups):
                for h in range(KC):
                    n = g * KC + h
                    act.wait_ge(s_tr, n + 1)
                    act.activation(agg[:, h, t0 * P:(t0 + k) * P], m.ps[:, n % 8, 0:k * P], ACT.Copy).then_inc(s_ev, 1)


def aggregate_tensors(m):
    take = Place(m, m.work)
    g = Names()
    g.oh_r, g.oh_k = take("oh_r", [P, RING, GRP, P], F16), take("oh_k", [P, RING, GRP, KEYS + 1], F16)
    g.col_k, g.col_r = take("col_k", [P, 2, WPS], F32), take("col_r", [P, 2, WPS], F32)
    g.align = align_tensors(m, "agg", m.r3)
    g.s_col = m.sem("agg_col")
    g.s_oh = m.sem("agg_oh")
    g.s_used = m.sem("agg_used")
    g.s_adj = m.sem("agg_adj")
    g.s_half = m.sem("agg_half")
    g.s_evac = m.sem("agg_evac")
    g.s_go = m.sem("agg_go")
    g.s_step = m.sem("agg_step")
    return g


def aggregate(nc, m, second, table, agg):
    a = m.agg
    oh_r, oh_k, col_k, col_r, t = a.oh_r, a.oh_k, a.col_k, a.col_r, a.align
    s_col, s_oh, s_used, s_adj, s_half, s_evac = a.s_col, a.s_oh, a.s_used, a.s_adj, a.s_half, a.s_evac
    EVERY = 6

    def walk(eng, name, head, step, tail):
        nlev = eng.value_load(m.levels[0:1, 0:1], min_val=1, max_val=NTE + 1)
        with eng.Fori(0, nlev) as level:
            run = eng.snap(level + nlev) if second else level
            with eng.If(nlev > 1):
                between_levels(eng, name, run)
            b = eng.snap(run * NSB)
            a.run = run
            head(eng, b)
            for k in range(2):
                step(eng, b + k, k, k)
            with eng.Fori(1, (NSB - 1) // 2) as k:
                bb = eng.snap(b + 2 * k)
                step(eng, bb, 2 * k, 0)
                step(eng, bb + 1, 2 * k + 1, 1)
            tail(eng, b)

    def between_levels(eng, name, run):
        align_edges(m, t, eng, name, run + 1, False)
        if name == "vector":
            eng.tensor_scalar(m.step16[:, :], m.step16[:, :], float(P // ROW), None, ALU.add).then_inc(a.s_step, 1)
            eng.wait_ge(a.s_step, run + 1)
            eng.sem_inc(a.s_go, 1)
        elif name == "tensor":
            eng.wait_ge(a.s_go, run + 1)

    def columns(dve, par, s):
        for col, whole in ((col_k, m.key), (col_r, m.rem)):
            last = dve.tensor_copy(col[:, par, :].rearrange("e (p j) -> e p j", j=WJ),
                                   whole[:, :, bass.ds(s * (WPS // WJ), WPS // WJ)].rearrange("e j p -> e p j"))
        last.then_inc(s_col, 1)

    def one_hots(dve, b, par, g):
        dve.wait_ge(s_used, b * GPS + (g + 1))
        for i in range(GRP):
            window = GRP * g + i
            dve.tensor_scalar(oh_r[:, g % RING, i, :], m.iota_r[:, :], col_r[:, par, window:window + 1], None, ALU.is_equal)
            last = dve.tensor_scalar(oh_k[:, g % RING, i, :], m.iota_k[:, :], col_k[:, par, window:window + 1], None, ALU.is_equal)
        last.then_inc(s_oh, 1)

    def add_half(dve, b, s, h):
        dve.wait_ge(s_half, b * KC + (KC + h + 1))
        dve.tensor_tensor(agg[:, h, bass.ds(s * SB, SB)], agg[:, h, bass.ds(s * SB, SB)],
                          m.ps[:, RING + h, 0:SB], ALU.add).then_inc(s_evac, 1)

    def v_head(dve, b):
        columns(dve, 0, 0)
        dve.wait_ge(s_col, b + a.run + 1)
        for g in range(GPS):
            one_hots(dve, b, 0, g)
        columns(dve, 1, 1)

    def v_step(dve, b, s, par):
        dve.wait_ge(s_col, b + a.run + 2)
        for g in range(GPS):
            one_hots(dve, b + 1, 1 - par, g)
            if g == 5 and not (isinstance(s, int) and s == 0):
                add_half(dve, b - 1, s - 1, 1)
            if g == 16:
                add_half(dve, b, s, 0)
            if g == 20 and not (isinstance(s, int) and s == NSB - 2):
                columns(dve, par, s + 2)

    def v_tail(dve, b):
        add_half(dve, b + (NSB - 2), NSB - 2, 1)
        add_half(dve, b + (NSB - 1), NSB - 1, 0)
        add_half(dve, b + (NSB - 1), NSB - 1, 1)
        dve.wait_ge(s_evac, b * KC + (NSB + 1) * KC)

    def build_group(pe, b, g):
        pe.wait_ge(s_oh, b * GPS + (g + 1))
        pe.wait_ge(s_adj, b * GPS + (g + 1))
        for i in range(GRP):
            last = pe.matmul(m.ps[:, g % RING, i * KEYS:(i + 1) * KEYS], oh_r[:, g % RING, i, :],
                             oh_k[:, g % RING, i, 0:KEYS], start=True, stop=True)
        last.then_inc(s_used, 1)

    def t_head(pe, b):
        for g in range(GPS):
            build_group(pe, b, g)

    def dense(pe, b, par, build):
        pe.wait_ge(s_adj, b * GPS + (GPS + RING))
        g, n = 0, 0
        for h in range(KC):
            pe.wait_ge(s_evac, b * KC + (h + 1))
            for c in range(NT):
                for half in range(2):
                    if build and n % EVERY == 0 and g < GPS:
                        build_group(pe, b + 1, g)
                        g += 1
                    n += 1
                    last = pe.matmul(m.ps[:, RING + h, 0:SB], table[:, c, half * C + h * P:half * C + (h + 1) * P],
                                     m.adj[:, par, c, :], start=c == 0 and half == 0, stop=c == NT - 1 and half == 1)
            last.then_inc(s_half, 1)

    def t_step(pe, b, s, par):
        dense(pe, b, par, True)

    def t_tail(pe, b):
        dense(pe, b + (NSB - 1), 0, False)

    def evacuate(act, b, par, g):
        act.wait_ge(s_used, b * GPS + (RING + g + 1))
        act.activation(m.adj[:, par, :, GRP * WIN * g:GRP * WIN * (g + 1)].rearrange("r c w -> r w c"),
                       m.ps[:, g % RING, 0:GRP * KEYS].rearrange("r (w c) -> r w c", c=NT), ACT.Copy).then_inc(s_adj, 1)

    def a_head(act, b):
        for g in range(GPS):
            evacuate(act, b, 0, g)

    def a_step(act, b, s, par):
        act.wait_ge(s_half, b * KC + KC)
        for g in range(GPS):
            evacuate(act, b + 1, 1 - par, g)

    def a_tail(act, b):
        act.wait_ge(s_half, b * KC + (NSB + 1) * KC)

    with nc.Block() as block:
        @block.vector
        def _(dve):
            chain_on(m, dve)(dve.memset(m.step16[:, :], 0.0))
            if not second:
                dve.sem_inc(s_evac, KC)
            walk(dve, "vector", v_head, v_step, v_tail)

        @block.tensor
        def _(pe):
            if not second:
                pe.sem_inc(s_used, RING)
                pe.sem_inc(s_half, KC)
            walk(pe, "tensor", t_head, t_step, t_tail)

        @block.scalar
        def _(act):
            if not second:
                act.sem_inc(s_adj, RING)
            walk(act, "scalar", a_head, a_step, a_tail)

        @block.gpsimd
        def _(pool):
            nlev = pool.value_load(m.levels[0:1, 0:1], min_val=1, max_val=NTE + 1)
            with pool.Fori(0, nlev) as level:
                run = pool.snap(level + nlev) if second else level
                with pool.If(nlev > 1):
                    between_levels(pool, "gpsimd", run)


def f32r_halves(dve, act, raw, hi, lo, s_in, n_in, s_hi, n_hi, s_lo):
    if act is not None:
        act.wait_ge(s_in, n_in)
        act.activation(hi, raw, ACT.Copy).then_inc(s_hi, 1)
    if dve is not None:
        dve.wait_ge(s_hi, n_hi)
        dve.tensor_tensor(lo, raw, hi.bitcast(F32), ALU.subtract).then_inc(s_lo, 1)


def linear1(nc, m, a):
    take = Place(m, m.work)
    w_hi, w_lo = take("w1_hi", [P, KC, IC], F32R), take("w1_lo", [P, KC, IC], F32R)
    raw = m.at("w1_raw", m.r3, [P, KC, IC], F32)
    u_hi, u_lo = take("u_hi", [P, 2, KC, SB], F32R), take("u_lo", [P, 2, KC, SB], F32R)
    S = m.sem
    s_raw, s_whi, s_wlo = S("d_raw"), S("d_whi"), S("d_wlo")
    s_u, s_uhi, s_ulo = S("d_u"), S("d_uhi"), S("d_ulo")
    s_mm = S("d_mm")
    s_h = S("d_h")
    h_of = (m.h01, m.h23)
    cols = lambda s: bass.ds(s * SB, SB)

    with nc.Block() as block:
        @block.sync
        def _(sp):
            sp.dma_start(raw[:, :, :], a.w1t.rearrange("(k p) f -> p k f", p=P)).then_inc(s_raw, 16)

        def walk(eng, step):
            for n in range(3):
                step(n, n % 2, n)
            with eng.Fori(1, (NSB - 3) // 2) as k:
                step(2 * k + 1, 1, None)
                step(2 * k + 2, 0, None)
            for n in range(NSB - 2, NSB):
                step(n, n % 2, n)

        @block.vector
        def _(dve):
            for h in h_of:
                dve.memset(h[:, :, N:NP_], 0.0)
            f32r_halves(dve, None, raw[:, :, :], w_hi[:, :, :], w_lo[:, :, :], None, 0, s_whi, 1, s_wlo)

            def scale(s):
                dis = m.disB[:, cols(s)].unsqueeze(1).to_broadcast([P, KC, SB])
                dve.scalar_tensor_tensor(m.agg1[:, :, cols(s)], m.agg1[:, :, cols(s)], 1.0 / T1SCALE, dis,
                                         ALU.mult, ALU.mult).then_inc(s_u, 1)

            def low(s, par):
                dve.wait_ge(s_uhi, s + 1)
                dve.tensor_tensor(u_lo[:, par, :, :], m.agg1[:, :, cols(s)], u_hi[:, par, :, :].bitcast(F32),
                                  ALU.subtract).then_inc(s_ulo, 1)

            def stats(s):
                dve.wait_ge(s_h, 2 * s + (2 + 4))
                for f in range(KI):
                    dve.bn_stats(m.stats1[:, f, bass.ds(s, 1), :].rearrange("p a b -> p (a b)"), h_of[f // 2][:, f % 2, cols(s)])

            def step(s, par, n):
                if n is None or n + 2 < NSB:
                    scale(s + 2)
                if n is None or n + 1 < NSB:
                    low(s + 1, 1 - par)
                if n is None or n >= 1:
                    stats(s - 1)
            scale(0)
            scale(1)
            low(0, 0)
            walk(dve, step)
            stats(NSB - 1)

        @block.scalar
        def _(act):
            act.sem_inc(s_h, 4)
            f32r_halves(None, act, raw[:, :, :], w_hi[:, :, :], w_lo[:, :, :], s_raw, 16, s_whi, 1, s_wlo)

            def high(s, par):
                act.wait_ge(s_u, s + 1)
                act.wait_ge(s_mm, 2 * s + 2)
                act.activation(u_hi[:, par, :, :], m.agg1[:, :, cols(s)], ACT.Copy).then_inc(s_uhi, 1)

            def evacuate(s, par):
                for q in range(2):
                    act.wait_ge(s_mm, 2 * s + (q + 1 + 4))
                    act.activation(h_of[q][:, :, cols(s)], m.ps[:, 4 * par + 2 * q:4 * par + 2 * q + 2, 0:SB], ACT.Copy).then_inc(s_h, 1)

            def step(s, par, n):
                if n is None or n + 1 < NSB:
                    high(s + 1, 1 - par)
                if n is None or n >= 1:
                    evacuate(s - 1, 1 - par)
            high(0, 0)
            walk(act, step)
            evacuate(NSB - 1, 0)

        @block.tensor
        def _(pe):
            pe.sem_inc(s_mm, 4)
            pe.wait_ge(s_wlo, 1)

            def step(s, par, n):
                pe.wait_ge(s_ulo, s + 1)
                for q in range(2):
                    pe.wait_ge(s_h, 2 * s + (q + 1))
                    for f in (2 * q, 2 * q + 1):
                        for n, (w, u) in enumerate(((w_hi, u_hi), (w_lo, u_hi), (w_hi, u_lo))):
                            for k in range(KC):
                                last = pe.matmul(m.ps[:, 4 * par + f, 0:SB], w[:, k, f * P:(f + 1) * P], u[:, par, k, :],
                                                 start=n == 0 and k == 0, stop=n == 2 and k == KC - 1)
                    last.then_inc(s_mm, 1)
            walk(pe, step)


def chain_on(m, dve):
    def link(ins):
        m.chained += 1
        ins.then_inc(m.s_chain, 1)
        dve.wait_ge(m.s_chain, m.chained)
    return link


def norm1(nc, m, a):
    take = Place(m, m.work)
    m.w2_hi, m.w2_lo = take("w2_hi", [P, KI, C], F32R), take("w2_lo", [P, KI, C], F32R)
    m.work2 = take.next
    raw, wabs = take("w2_raw", [P, KI, C], F32), take("w2_abs", [P, KI, C], F32)
    take = Place(m, m.r3 - 2048)
    mv, ve, mh = take("n1_mv", [P, KI, 2], F32), take("n1_ve", [P, KI], F32), take("n1_mh", [P, KI], F32)
    rs, tmp = take("n1_rs", [P, KI], F32), take("n1_tmp", [P, KI], F32)
    bnd, babs = take("n1_bnd", [P, KI], F32), take("n1_babs", [P, KI], F32)
    top, one = take("n1_top", [P, 1], F32), take("n1_one", [1, 4], F32)
    S = m.sem
    s_raw, s_whi, s_wlo, s_ve, s_mh, s_rs = S("e_raw"), S("e_whi"), S("e_wlo"), S("e_ve"), S("e_mh"), S("e_rs")
    s_b, s_bp, s_top, s_topT, s_sc, s_scB = S("e_b"), S("e_bp"), S("e_top"), S("e_topT"), S("e_sc"), S("e_scB")
    with nc.Block() as block:
        @block.sync
        def _(sp):
            sp.dma_start(raw[:, :, :], a.w2t.rearrange("(k p) c -> p k c", p=P)).then_inc(s_raw, 16)

        @block.scalar
        def _(act):
            f32r_halves(None, act, raw[:, :, :], m.w2_hi[:, :, :], m.w2_lo[:, :, :], s_raw, 16, s_whi, 1, s_wlo)

        @block.gpsimd
        def _(pool):
            pool.memset(mh[:, :], -0.5).then_inc(s_mh, 1)
            pool.wait_ge(s_mh, 1)
            pool.wait_ge(s_ve, 1)
            pool.tensor_tensor(rs[:, :], ve[:, :], mh[:, :], ALU.pow).then_inc(s_rs, 1)

        @block.tensor
        def _(pe):
            pe.wait_ge(s_b, 1)
            for c in range(KC):
                for k in range(KI):
                    last = pe.matmul(m.ps[:, 0, c:c + 1], wabs[:, k, c * P:(c + 1) * P], bnd[:, k:k + 1],
                                     start=k == 0, stop=k == KI - 1)
            last.then_inc(s_bp, 1)
            pe.wait_ge(s_top, 1)
            pe.transpose(m.ps[:1, 1, 0:P], top[:, :], m.id32[:, :]).then_inc(s_topT, 1)
            pe.wait_ge(s_sc, 1)
            pe.matmul(m.ps[:, 2, 0:1], m.ones[0:1, :], one[0:1, 3:4], start=True, stop=True).then_inc(s_scB, 1)

        @block.vector
        def _(dve):
            link = chain_on(m, dve)
            for f in range(KI):
                last = dve.bn_aggr(mv[:, f, :], m.stats1[:, f, :, :].rearrange("p a b -> p (a b)"))
            link(last)
            dve.tensor_scalar(ve[:, :], mv[:, :, 1], EPS, None, ALU.add).then_inc(s_ve, 1)
            dve.wait_ge(s_raw, 16)
            link(dve.scalar_tensor_tensor(wabs[:, :, :], raw[:, :, :], -1.0, raw[:, :, :], ALU.mult, ALU.max))
            link(dve.scalar_tensor_tensor(babs[:, :], m.bn_b1[:, :], -1.0, m.bn_b1[:, :], ALU.mult, ALU.max))
            link(dve.scalar_tensor_tensor(bnd[:, :], m.bn_g1[:, :], -1.0, m.bn_g1[:, :], ALU.mult, ALU.max))
            dve.scalar_tensor_tensor(bnd[:, :], bnd[:, :], float(N) ** 0.5 + 1.0, babs[:, :], ALU.mult, ALU.add).then_inc(s_b, 1)
            dve.wait_ge(s_bp, 1)
            dve.tensor_reduce(top[:, :], m.ps[:, 0, 0:KC], AX.X, ALU.max).then_inc(s_top, 1)
            dve.wait_ge(s_topT, 1)
            link(dve.tensor_reduce(one[:, 0:1], m.ps[:1, 1, 0:P], AX.X, ALU.max))
            link(dve.tensor_scalar(one[:, 1:2], one[:, 0:1], 1e-6, 1.0 / 32768.0, ALU.max, ALU.mult))
            link(dve.reciprocal(one[:, 2:3], one[:, 1:2]))
            dve.tensor_scalar(one[:, 3:4].bitcast(I32), one[:, 2:3].bitcast(I32), 0x7F800000, None, ALU.bitwise_and).then_inc(s_sc, 1)
            dve.wait_ge(s_scB, 1)
            link(dve.tensor_copy(m.scale2[:, :], m.ps[:, 2, 0:1]))
            link(dve.tensor_scalar(m.disP[:, :], m.disP[:, :], m.scale2[:, 0:1], None, ALU.mult))
            dve.wait_ge(s_rs, 1)
            link(dve.tensor_tensor(m.aff_a1[:, :], m.bn_g1[:, :], rs[:, :], ALU.mult))
            link(dve.tensor_tensor(tmp[:, :], mv[:, :, 0], m.aff_a1[:, :], ALU.mult))
            link(dve.tensor_tensor(m.aff_b1[:, :], m.bn_b1[:, :], tmp[:, :], ALU.subtract))
            f32r_halves(dve, None, raw[:, :, :], m.w2_hi[:, :, :], m.w2_lo[:, :, :], None, 0, s_whi, 1, s_wlo)


def linear2(nc, m, a):
    norm1(nc, m, a)
    take = Place(m, m.work2)
    h_hi, h_lo = take("h_hi", [P, 2, KI, P], F32R), take("h_lo", [P, 2, KI, P], F32R)
    S = m.sem
    s_r = S("f_r")
    s_hhi, s_split = S("f_hhi"), S("f_split")
    s_mm = S("f_mm")
    s_thi = S("f_thi")
    s_tlo = S("f_tlo")
    h_of = (m.h01, m.h23)

    def walk(step):
        def run(eng):
            for n in range(4):
                step(eng, n, n, n // 2, n)
            with eng.Fori(1, NT // 4 - 1) as k:
                for q in range(4):
                    step(eng, 4 * k + q, q, 2 * k + q // 2, None)
            for n in range(NT // 4 * 4 - 4, NT):
                step(eng, n, n % 4, n // 2, n)
        return run

    with nc.Block() as block:
        @block.vector
        def _(dve):
            dve.sem_inc(s_tlo, 4)

            def split(i, par, pair):
                cols = bass.ds(i * P, P)
                dve.wait_ge(s_r, pair + 1)
                dve.wait_ge(s_mm, i + 1)
                for q in range(2):
                    last = dve.tensor_copy(h_hi[:, par, 2 * q:2 * q + 2, :], h_of[q][:, :, cols])
                last.then_inc(s_hhi, 1)
                dve.wait_ge(s_hhi, i + 1)
                for q in range(2):
                    last = dve.tensor_tensor(h_lo[:, par, 2 * q:2 * q + 2, :], h_of[q][:, :, cols],
                                             h_hi[:, par, 2 * q:2 * q + 2, :].bitcast(F32), ALU.subtract)
                last.then_inc(s_split, 1)

            def low(i, bank):
                dve.wait_ge(s_thi, i + 1)
                dve.scalar_tensor_tensor(m.table2[:, bass.ds(i, 1), C:].rearrange("p a c -> p (a c)"), m.ps[:, bank, 0:C],
                                         m.disP[:, bass.ds(i, 1)], m.table2[:, bass.ds(i, 1), :C].rearrange("p a c -> p (a c)"),
                                         ALU.mult, ALU.subtract).then_inc(s_tlo, 1)

            def step(dve, i, q, pair, n):
                if n is None or n + 1 < NT:
                    split(i + 1, (q + 1) % 2, pair + q % 2)
                if n is None or n >= 1:
                    low(i - 1, (q - 1) % 4)
            split(0, 0, 0)
            walk(step)(dve)
            low(NT - 1, (NT - 1) % 4)

        @block.scalar
        def _(act):
            def relu(pair, width):
                for f in range(KI):
                    h = h_of[f // 2][:, f % 2, bass.ds(pair * 2 * P, width)]
                    last = act.activation(h, h, ACT.Relu, bias=m.aff_b1[:, f:f + 1], scale=m.aff_a1[:, f:f + 1])
                last.then_inc(s_r, 1)

            def high(i, bank):
                act.wait_ge(s_mm, i + (1 + 2))
                act.activation(m.table2[:, bass.ds(i, 1), :C].rearrange("p a c -> p (a c)"), m.ps[:, bank, 0:C], ACT.Copy,
                               scale=m.disP[:, bass.ds(i, 1)]).then_inc(s_thi, 1)

            def step(act, i, q, pair, n):
                if q % 2 == 0 and (n is None or n + 2 < NT):
                    relu(pair + 1, 2 * P if n is None or n + 3 < NT else P)
                if n is None or n >= 1:
                    high(i - 1, (q - 1) % 4)
            relu(0, 2 * P)
            walk(step)(act)
            high(NT - 1, (NT - 1) % 4)

        @block.tensor
        def _(pe):
            pe.sem_inc(s_mm, 2)

            def step(pe, i, q, pair, n):
                pe.wait_ge(s_split, i + 1)
                pe.wait_ge(s_tlo, i + 1)
                for k, (h, w) in enumerate(((h_hi, m.w2_hi), (h_hi, m.w2_lo), (h_lo, m.w2_hi))):
                    for f in range(KI):
                        last = pe.matmul(m.ps[:, q, 0:C], h[:, q % 2, f, :], w[:, f, :],
                                         start=k == 0 and f == 0, stop=k == 2 and f == KI - 1)
                last.then_inc(s_mm, 1)
            walk(step)(pe)
    self_loops(nc, m, "l2", m.table2, m.agg2)


def finish_gnn(nc, m, a):
    x = m.x
    x1 = m.at("x1_sb", m.r2, [P, NT, C], F32)
    take = Place(m, m.work)
    st2, mv2 = take("st2", [P, KC, NSB, 6], F32), take("mv2", [P, KC, 2], F32)
    e2, ve2, mh, rs2 = take("e2", [P, 1], F32), take("ve2", [P, KC], F32), take("mh2", [P, NT], F32), take("rs2", [P, KC], F32)
    a2, b2, tmp = take("a2", [P, KC], F32), take("b2c", [P, KC], F32), take("tmp2", [P, KC], F32)
    xn = take("xn", [P, 2, 2, C], F32)
    st3, mv3 = take("st3", [P, NT, 6], F32), take("mv3", [P, NT, 2], F32)
    ve3, rs3 = take("ve3", [P, NT], F32), take("rs3", [P, NT], F32)
    S = m.sem
    s_x, s_xt, s_u, s_ve, s_mh, s_rs, s_aff, s_v, s_tr, s_sum = (S("g_" + n) for n in ("x", "xt", "u", "ve", "mh", "rs", "aff", "v", "tr", "sum"))
    s_x1, s_ve3, s_rs3, s_out = (S("g_" + n) for n in ("x1", "ve3", "rs3", "out"))
    pairs = [(2 * g, min(2, NT - 2 * g)) for g in range(-(-NT // 2))]
    eights = [(8 * g, min(8, NT - 8 * g)) for g in range(-(-NT // 8))]
    with nc.Block() as block:
        @block.sync
        def _(sp):
            for i in range(6):
                sp.dma_start(x[:, 8 * i:8 * i + 8, :],
                             a.x[1024 * i:1024 * (i + 1), :].rearrange("(t p) c -> p t c", p=P)).then_inc(s_x, 16)
            sp.wait_ge(s_xt, 1)
            sp.dma_start(x[:LAST, NT - 1, :], a.x[(NT - 1) * P:N, :]).then_inc(s_x, 16)
            for t0, k in eights:
                sp.wait_ge(s_x1, (t0 + k + 1) // 2)
                sp.dma_start(m.x1_dram[t0 * P:(t0 + k) * P, 0:C].rearrange("(t p) c -> p t c", p=P), x1[:, t0:t0 + k, :]).then_inc(s_out, 16)
            sp.wait_ge(s_out, 16 * len(eights))

        @block.gpsimd
        def _(pool):
            pool.memset(mh[:, :], -0.5).then_inc(s_mh, 1)
            pool.wait_ge(s_mh, 1)
            pool.wait_ge(s_ve, 1)
            pool.tensor_tensor(rs2[:, :], ve2[:, :], mh[:, :KC], ALU.pow).then_inc(s_rs, 1)
            pool.wait_ge(s_ve3, 1)
            pool.tensor_tensor(rs3[:, :], ve3[:, :], mh[:, :], ALU.pow).then_inc(s_rs3, 1)

        @block.vector
        def _(dve):
            link = chain_on(m, dve)
            dve.memset(x[:, NT - 1, :], 0.0).then_inc(s_xt, 1)
            with dve.Fori(0, NSB) as s:
                c = bass.ds(s * SB, SB)
                dve.tensor_tensor(m.agg2[:, :, c], m.agg2[:, :, c], m.disB[:, c].unsqueeze(1).to_broadcast([P, KC, SB]),
                                  ALU.mult).then_inc(s_u, 1)
                dve.wait_ge(s_u, s + 1)
                for h in range(KC):
                    dve.bn_stats(st2[:, h, bass.ds(s, 1), :].rearrange("p a b -> p (a b)"), m.agg2[:, h, c])
            link(dve.tensor_tensor(e2[:, :], m.scale2[:, :], m.scale2[:, :], ALU.mult))
            for h in range(KC):
                last = dve.bn_aggr(mv2[:, h, :], st2[:, h, :, :].rearrange("p a b -> p (a b)"))
            link(last)
            dve.scalar_tensor_tensor(ve2[:, :], e2[:, 0:1].to_broadcast([P, KC]), EPS, mv2[:, :, 1], ALU.mult, ALU.add).then_inc(s_ve, 1)
            dve.wait_ge(s_rs, 1)
            link(dve.tensor_tensor(a2[:, :], m.bn_g2[:, :], rs2[:, :], ALU.mult))
            link(dve.tensor_tensor(tmp[:, :], mv2[:, :, 0], a2[:, :], ALU.mult))
            dve.tensor_tensor(b2[:, :], m.bn_b2[:, :], tmp[:, :], ALU.subtract).then_inc(s_aff, 1)
            dve.wait_ge(s_x, 16 * 7)
            for g, (t0, k) in enumerate(pairs):
                for i in range(k):
                    last = dve.tensor_scalar(xn[:, g % 2, i, :], x[:, t0 + i, :], m.mean[:, t0 + i:t0 + i + 1],
                                             m.rstd[:, t0 + i:t0 + i + 1], ALU.subtract, ALU.mult)
                link(last)
                dve.wait_ge(s_tr, g + 1)
                link(dve.tensor_tensor(xn[:, g % 2, 0:k, :], xn[:, g % 2, 0:k, :],
                                       m.ps[:, g % 4, 0:k * C].rearrange("p (t c) -> p t c", c=C), ALU.add))
                dve.scalar_tensor_tensor(x1[:, t0:t0 + k, :], xn[:, g % 2, 0:k, :], 0.0, x[:, t0:t0 + k, :],
                                         ALU.max, ALU.add).then_inc(s_x1, 1)
                dve.wait_ge(s_x1, g + 1)
                for i in range(t0, t0 + k):
                    dve.bn_stats(st3[:, i, :], x1[:, i, :]).then_inc(s_sum, 1)
            dve.wait_ge(s_sum, NT)
            for i in range(NT):
                last = dve.bn_aggr(mv3[:, i, :], st3[:, i, :])
            link(last)
            dve.tensor_scalar(ve3[:, :], mv3[:, :, 1], EPS, None, ALU.add).then_inc(s_ve3, 1)
            dve.wait_ge(s_rs3, 1)
            for i in range(NT):
                last = dve.tensor_scalar(m.rows[:, i, 0:C], x1[:, i, :], mv3[:, i, 0:1], rs3[:, i:i + 1], ALU.subtract, ALU.mult)
            link(last)

        @block.scalar
        def _(act):
            act.wait_ge(s_aff, 1)
            for g, (t0, k) in enumerate(pairs):
                for h in range(KC):
                    v = m.agg2[:, h, t0 * P:(t0 + k) * P]
                    last = act.activation(v, v, ACT.Identity, bias=b2[:, h:h + 1], scale=a2[:, h:h + 1])
                last.then_inc(s_v, 1)

        @block.tensor
        def _(pe):
            for g, (t0, k) in enumerate(pairs):
                pe.wait_ge(s_v, g + 1)
                if g >= 4:
                    pe.wait_ge(s_x1, g - 3)
                for i in range(k):
                    for h in range(KC):
                        last = pe.transpose(m.ps[:, g % 4, i * C + h * P:i * C + (h + 1) * P],
                                            m.agg2[:, h, (t0 + i) * P:(t0 + i + 1) * P], m.id32[:, :])
                last.then_inc(s_tr, 1)



def ffn_scales(nc, m, a):
    raw = m.at("w1f_abs", m.r1, [P, KC, HID], F32)
    wd_raw = m.at("wd_abs", m.r1 + 8192, [P, 2, NEXP, C], F32)
    take = Place(m, m.r1 + 8192 * 3)
    asum, bsum, babs = take("asum", [P, KH], F32), take("bsum", [P, KH], F32), take("babs", [P, KH], F32)
    rb, inv, prod, low = take("rb", [P, KH], F32), take("inv", [P, KH], F32), take("prod", [P, KH], F32), take("low", [P, 1], F32)
    one = take("one_f", [1, 1], F32)
    wg_abs, gsum = take("wg_abs", [P, KH, NEXP], F32), take("gsum", [P, KH], F32)
    S = m.sem
    s_w1, s_b1, s_wd, s_abs, s_free, s_wabs, s_bp, s_low, s_lowT, s_one, s_G = (
        S("h_" + n) for n in ("w1", "b1", "wd", "abs", "free", "wabs", "bp", "low", "lowT", "one", "G"))
    s_wdp = [S("h_wd0"), S("h_wd1")]
    with nc.Block() as block:
        @block.sync
        def _(sp):
            sp.dma_start(raw[:, :, :], a.fw1.rearrange("(k p) h -> p k h", p=P)).then_inc(s_w1, 16)
            with nc.allow_non_contiguous_dma("the bias of the hidden units to partitions"):
                sp.dma_start(m.b1f[:, :], a.fb1.rearrange("(k p) -> p k", p=P)).then_inc(s_b1, 16)
            sp.dma_start(wg_abs[:, :, :], a.fwg.rearrange("(k p) e -> p k e", p=P)).then_inc(s_b1, 16)
            for k in range(KH):
                if k >= 2:
                    sp.wait_ge(s_free, k - 1)
                sp.dma_start(wd_raw[:, k % 2, :, :], a.fwd[:, k * P:(k + 1) * P, :].rearrange("e p c -> p e c")).then_inc(s_wdp[k % 2], 16)

        @block.scalar
        def _(act):
            for k in range(KH):
                act.wait_ge(s_wdp[k % 2], 16 * (k // 2 + 1))
                act.activation(wd_raw[:, k % 2, :, :], wd_raw[:, k % 2, :, :], ACT.Abs, accum_out=asum[:, k:k + 1]).then_inc(s_free, 1)

        @block.tensor
        def _(pe):
            pe.wait_ge(s_wabs, 1)
            for h in range(KH):
                for k in range(KC):
                    last = pe.matmul(m.ps[:, 0, h:h + 1], raw[:, k, h * P:(h + 1) * P], m.ones[:, 0:1], start=k == 0, stop=k == KC - 1)
            last.then_inc(s_bp, 1)
            pe.wait_ge(s_low, 1)
            pe.transpose(m.ps[:1, 1, 0:P], low[:, :], m.id32[:, :]).then_inc(s_lowT, 1)
            pe.wait_ge(s_one, 1)
            pe.matmul(m.ps[:, 2, 0:1], m.ones[0:1, :], one[0:1, 0:1], start=True, stop=True).then_inc(s_G, 1)

        @block.vector
        def _(dve):
            link = chain_on(m, dve)

            def power(out, bound):
                link(dve.tensor_scalar(out, bound, 1e-6, 1.0 / 32768.0, ALU.max, ALU.mult))
                link(dve.reciprocal(out, out))
                link(dve.tensor_scalar(out.bitcast(I32), out.bitcast(I32), 0x7F800000, None, ALU.bitwise_and))

            def inverse(out, x):
                link(dve.tensor_scalar(out.bitcast(I32), x.bitcast(I32), -1.0, float(254 << 23), ALU.mult, ALU.add))

            dve.wait_ge(s_w1, 16)
            dve.scalar_tensor_tensor(raw[:, :, :], raw[:, :, :], -1.0, raw[:, :, :], ALU.mult, ALU.max).then_inc(s_wabs, 1)
            dve.wait_ge(s_b1, 32)
            link(dve.scalar_tensor_tensor(wg_abs[:, :, :], wg_abs[:, :, :], -1.0, wg_abs[:, :, :], ALU.mult, ALU.max))
            link(dve.tensor_reduce(gsum[:, :], wg_abs[:, :, :], AX.X, ALU.add))
            link(dve.scalar_tensor_tensor(babs[:, :], m.b1f[:, :], -1.0, m.b1f[:, :], ALU.mult, ALU.max))
            dve.wait_ge(s_bp, 1)
            link(dve.scalar_tensor_tensor(bsum[:, :], m.ps[:, 0, 0:KH], 16.25, babs[:, :], ALU.mult, ALU.add))
            power(rb[:, :], bsum[:, :])
            dve.wait_ge(s_free, KH)
            link(dve.tensor_tensor(asum[:, :], asum[:, :], gsum[:, :], ALU.add))
            power(m.alpha[:, :], asum[:, :])
            link(dve.tensor_tensor(prod[:, :], rb[:, :], m.alpha[:, :], ALU.mult))
            dve.tensor_reduce(low[:, :], prod[:, :], AX.X, ALU.min).then_inc(s_low, 1)
            dve.wait_ge(s_lowT, 1)
            dve.tensor_reduce(one[:, :], m.ps[:1, 1, 0:P], AX.X, ALU.min).then_inc(s_one, 1)
            dve.wait_ge(s_G, 1)
            link(dve.tensor_copy(low[:, :], m.ps[:, 2, 0:1]))
            inverse(m.inv_g[:, :], low[:, :])
            inverse(inv[:, :], m.alpha[:, :])
            link(dve.tensor_scalar(m.beta[:, :], inv[:, :], low[:, 0:1], None, ALU.mult))


def ffn(nc, m, a):
    take = Place(m, m.r2)
    m.wd_hi, m.wd_lo = take("wd_hi", [P, NEXP, KH, C], F16), take("wd_lo", [P, NEXP, KH, C], F16)
    m.w1_hi, m.w1_lo = take("fw1_hi", [P, KC, HID], F32R), take("fw1_lo", [P, KC, HID], F32R)
    m.xt_hi, m.xt_lo = take("xt_hi", [P, 2, KC, 2 * P], F32R), take("xt_lo", [P, 2, KC, 2 * P], F32R)
    m.hf = take("hf", [P, KH, 2 * P], F32)
    m.h_hi, m.h_lo = take("h16_hi", [P, 2, KH, 2 * P], F16), take("h16_lo", [P, 2, KH, 2 * P], F16)
    m.work3 = take.next
    gate(nc, m, a)
    experts(nc, m, a)



UB = 4
TBANK = 4


def hidden_semaphores(m, tag):
    u = Names()
    u.tr = m.sem(f"{tag}_tr")
    u.xthi = m.sem(f"{tag}_xthi")
    u.xt = m.sem(f"{tag}_xt")
    u.up = m.sem(f"{tag}_up")
    u.gelu = m.sem(f"{tag}_gelu")
    u.hi = m.sem(f"{tag}_hi")
    u.split = m.sem(f"{tag}_split")
    u.done = m.sem(f"{tag}_done")
    return u


def pe_ahead(pe, u):
    pe.sem_inc(u.up, 2 * KH)
    pe.sem_inc(u.done, 2)


def dve_ahead(dve, u):
    dve.sem_inc(u.xt, 1)
    dve.sem_inc(u.split, KH)


def pe_transpose(pe, m, u, i, rows, ntile):
    pe.wait_ge(u.xt, i + 1)
    for j in range(ntile):
        for k in range(KC):
            last = pe.transpose(m.ps[:, TBANK, k * 2 * P + j * P:k * 2 * P + (j + 1) * P], rows(j, k), m.id32[:, :])
    last.then_inc(u.tr, 1)


def pe_hidden(pe, m, u, i, par, ntile, between):
    n = ntile * P
    pe.wait_ge(u.xt, i + 2)
    for h in range(KH):
        pe.wait_ge(u.gelu, i * KH + (h + 1))
        for q, (w, x) in enumerate(((m.w1_hi, m.xt_hi), (m.w1_lo, m.xt_hi), (m.w1_hi, m.xt_lo))):
            for k in range(KC):
                last = pe.matmul(m.ps[:, h % UB, 0:n], w[:, k, h * P:(h + 1) * P], x[:, par, k, 0:n],
                                 start=q == 0 and k == 0, stop=q == 2 and k == KC - 1)
        last.then_inc(u.up, 1)
        if h in between:
            between[h]()


def act_xt(act, m, u, i, par, ntile):
    act.wait_ge(u.tr, i + 1)
    act.wait_ge(u.up, i * KH + KH)
    act.activation(m.xt_hi[:, par, :, 0:ntile * P],
                   m.ps[:, TBANK, :].rearrange("p (k n) -> p k n", k=KC)[:, :, 0:ntile * P], ACT.Copy).then_inc(u.xthi, 1)


def act_hidden(act, m, u, i, par, ntile, nxt):
    n = ntile * P

    def high(h):
        act.wait_ge(u.gelu, i * KH + (h + 1 + UB))
        act.activation(m.h_hi[:, par, h, 0:n], m.hf[:, h, 0:n], ACT.Copy, scale=m.beta[:, h:h + 1]).then_inc(u.hi, 1)

    for h in range(KH):
        act.wait_ge(u.up, i * KH + (h + 1 + 2 * KH))
        act.wait_ge(u.split, i * KH + (h + 1))
        act.activation(m.hf[:, h, 0:n], m.ps[:, h % UB, 0:n], ACT.Gelu, bias=m.b1f[:, h:h + 1]).then_inc(u.gelu, 1)
        if h == 0:
            act.wait_ge(u.done, i + 1)
        else:
            high(h - 1)
        if h == 3 and nxt:
            act_xt(act, m, u, i + 1, 1 - par, nxt)
    high(KH - 1)


def dve_xt(dve, m, u, i, par, ntile):
    dve.wait_ge(u.xthi, i + 1)
    dve.tensor_tensor(m.xt_lo[:, par, :, 0:ntile * P],
                      m.ps[:, TBANK, :].rearrange("p (k n) -> p k n", k=KC)[:, :, 0:ntile * P],
                      m.xt_hi[:, par, :, 0:ntile * P].bitcast(F32), ALU.subtract).then_inc(u.xt, 1)


def dve_hidden(dve, m, u, i, par, ntile, nxt, between={}):
    n = ntile * P
    for h in range(KH):
        dve.wait_ge(u.hi, i * KH + (h + 1))
        dve.scalar_tensor_tensor(m.h_lo[:, par, h, 0:n], m.hf[:, h, 0:n], m.beta[:, h:h + 1], m.h_hi[:, par, h, 0:n],
                                 ALU.mult, ALU.subtract).then_inc(u.split, 1)
        if h == 3 and nxt:
            dve_xt(dve, m, u, i + 1, 1 - par, nxt)
        if h in between:
            between[h]()


REG = 6400
MAXT = 56
assert MAXT * P >= N + NEXP * (P - 1) - P + 1 and REG >= NP_ + P
RW = C + 1


def gate(nc, m, a):
    rows = m.rows
    w1_raw = m.at("fw1_raw", m.work3 - 16384, [P, KC, HID], F32)
    wd_raw = (m.at("wd_raw0", m.work3, [P, NEXP, C], F32), m.at("wd_raw1", m.work, [P, NEXP, C], F32))
    assert m.work3 + 8192 <= m.r5
    take = Place(m, m.work + 8192)
    wg_raw, wg = take("wg_raw", [P, KH, NEXP], F32), take("wg", [P, KH, 2 * NEXP], F16)
    bg = take("bgB", [P, NEXP], F32)
    tri, ones16 = take("tri", [P, P], F16), take("ones16", [P, P], F16)
    prio, run = take("prio", [P, NEXP], F32), take("run", [P, NEXP], F32)
    lg, mx = take("lg", [P, NT + 1, NEXP], F32), take("mx", [P, 2], F32)
    now = take("now", [P, 2, NEXP], F32)
    sc, best = take("sc", [P, 2, NEXP], F32), take("best", [P, 2], F32)
    oh, ohf = take("oh", [P, 2, 2, NEXP], F16), take("ohf", [P, 2, 2, NEXP], F32)
    rk, slotf, slot = take("rk", [P, 2, NEXP], F32), take("slotf", [P, 2], F32), take("slot", [P, NT], I32)
    valid = take("valid", [P, 1], F32)
    padi, padf, prow = take("padi", [P, NEXP + 1], I32), take("padf", [P, NEXP + 1], F32), take("prow", [P, RW], F32)
    pcol = take("pcol", [P, 1], F32)
    stage = take("stage", [P, 2, 2, C], F32)
    tv, tb, nt, nti = take("tv", [1, 64], F32), take("tb", [1, NEXP + 1], F32), take("nt", [1, NEXP], F32), take("nti", [1, NEXP], I32)
    te, tr_, tq, tf = take("te", [1, 64], F32), take("tr_", [1, 64], F32), take("tq", [1, 64], F32), take("tf", [1, 64], F32)
    u = hidden_semaphores(m, "i")
    S = m.sem
    (s_w1, s_w1hi, s_w1lo, s_par, s_wdhi, s_wdfree, s_const, s_oh, s_rk, s_slot, s_scat,
     s_init, s_choose, s_place, s_lgfree, s_pads, s_stage, s_ex, s_prob, s_store) = (S("i_" + n) for n in (
         "w1", "w1hi", "w1lo", "par", "wdhi", "wdfree", "const", "oh", "rk", "slot", "scat",
         "init", "choose", "place", "lgfree", "pads", "stage", "ex", "prob", "store"))
    s_wd = (S("i_wd0"), S("i_wd1"))
    NPAIR = NT // 2
    LB, RB = (5, 7), 6
    tiles = lambda i: 1 if i == NPAIR else 2

    def steps(eng, step):
        for i in range(4):
            step(eng, i, i % 2, i)
        with eng.Fori(2, NPAIR // 2 - 1) as k:
            step(eng, 2 * k, 0, None)
            step(eng, 2 * k + 1, 1, None)
        for i in range(NPAIR - 2, NPAIR + 1):
            step(eng, i, i % 2, i)

    with nc.Block() as block:
        @block.sync
        def _(sp):
            sp.dma_start(w1_raw[:, :, :], a.fw1.rearrange("(k p) h -> p k h", p=P)).then_inc(s_w1, 16)
            sp.dma_start(wg_raw[:, :, :], a.fwg.rearrange("(k p) e -> p k e", p=P)).then_inc(s_par, 16)
            sp.dma_start(bg[:, :], bass.AP(a.fbg.tensor, 0, [[0, P], [1, NEXP]])).then_inc(s_par, 16)
            for k in range(KH):
                if k >= 2:
                    sp.wait_ge(s_wdfree, k - 1)
                sp.dma_start(wd_raw[k % 2][:, :, :], a.fwd[:, k * P:(k + 1) * P, :].rearrange("e p c -> p e c")).then_inc(s_wd[k % 2], 16)
            sp.wait_ge(s_prob, 1)
            with nc.allow_non_contiguous_dma("each token's probability behind its row of x1"):
                sp.dma_start(m.x1_dram[:, C:C + 1].rearrange("(t p) c -> p t c", p=P), m.probs[:, :].unsqueeze(2)).then_inc(s_store, 16)
            sp.wait_ge(s_store, 16)

        @block.gpsimd
        def _(pool):
            pool.iota(rows[:, :, RW - 1].bitcast(I32), [[P, NT]], base=0, channel_multiplier=1).then_inc(s_const, 1)
            pool.memset(tri[:, :], 1.0).then_inc(s_init, 1)
            pool.memset(prow[:, :], 0.0).then_inc(s_init, 1)
            pool.memset(valid[:, :], 1.0).then_inc(s_init, 1)
            pool.wait_ge(s_init, 3)
            pool.affine_select(out=tri[:, :], in_=tri[:, :], compare_op=ALU.is_ge, fill=0.0,
                               base=-1, pattern=[[1, P]], channel_multiplier=-1).then_inc(s_const, 1)
            pool.affine_select(out=valid[:, :], in_=valid[:, :], compare_op=ALU.is_ge, fill=0.0,
                               base=LAST - 1, pattern=[[0, 1]], channel_multiplier=-1).then_inc(s_const, 1)
            pool.iota(prow[:, RW - 1:RW].bitcast(I32), [[0, 1]], base=N, channel_multiplier=0).then_inc(s_const, 1)
            pool.iota(prio[:, :], [[-1, NEXP]], base=NEXP, channel_multiplier=0, allow_small_or_imprecise_dtypes=True).then_inc(s_const, 1)
            for t in (run, m.reg_base):
                pool.iota(t[:, :], [[REG, NEXP]], base=0, channel_multiplier=0, allow_small_or_imprecise_dtypes=True).then_inc(s_const, 1)
            pool.iota(padf[:, :], [[REG, NEXP + 1]], base=0, channel_multiplier=1, allow_small_or_imprecise_dtypes=True).then_inc(s_const, 1)
            pool.iota(pcol[:, :], [[0, 1]], base=0, channel_multiplier=1, allow_small_or_imprecise_dtypes=True).then_inc(s_const, 1)
            pool.iota(tv[:, :], [[1, 64]], base=0, channel_multiplier=0, allow_small_or_imprecise_dtypes=True).then_inc(s_const, 1)
            pool.wait_ge(s_const, 10)
            LATE = 6
            for i in range(NPAIR + 1 + LATE):
                if i <= NPAIR:
                    n = tiles(i)
                    if i >= 2:
                        pool.wait_ge(u.tr, i - 1)
                    pool.tensor_copy(stage[:, i % 2, 0:n, :], rows[:, 2 * i:2 * i + n, 0:C]).then_inc(s_stage, 1)
                if i >= LATE:
                    pool.wait_ge(s_slot, i - LATE + 1)
                    for t in range(2 * (i - LATE), 2 * (i - LATE) + tiles(i - LATE)):
                        n = P if t < NT - 1 else LAST
                        pool.indirect_dma_start(m.sorted_rows, bass.IndirectOffsetOnAxis(ap=slot[:n, t:t + 1], axis=0),
                                                rows[:n, t, :], None).then_inc(s_scat, 16)
            pool.wait_ge(s_pads, 1)
            for e in range(NEXP + 1):
                pool.indirect_dma_start(m.sorted_rows, bass.IndirectOffsetOnAxis(ap=padi[:, e:e + 1], axis=0),
                                        prow[:, :], None).then_inc(s_scat, 16)
            pool.wait_ge(s_scat, 16 * (NT + NEXP + 1))

        @block.tensor
        def _(pe):
            pe_ahead(pe, u)
            pe.wait_ge(s_w1lo, 1)
            pe.wait_ge(s_const, 10)

            def logits(pe, i, par, ntile):
                pe.wait_ge(u.split, i * KH + 2 * KH)
                pe.wait_ge(s_lgfree, i + 1)
                for j in range(ntile):
                    for n, h in enumerate((m.h_hi, m.h_lo)):
                        for k in range(KH):
                            last = pe.matmul(m.ps[:, LB[par], j * 16:j * 16 + 2 * NEXP], h[:, par, k, j * P:(j + 1) * P], wg[:, k, :],
                                             start=n == 0 and k == 0, stop=n == 1 and k == KH - 1)
                last.then_inc(u.done, 1)

            def ranks(pe, i, par, ntile, n):
                pe.wait_ge(s_oh, i + 1)
                if n is None or n > 3:
                    pe.wait_ge(s_slot, i)
                pe.matmul(m.ps[:, RB, 0:NEXP], tri[:, :], oh[:, par, 0, :], start=True, stop=True)
                if ntile == 2:
                    pe.matmul(m.ps[:, RB, NEXP:2 * NEXP], tri[:, :], oh[:, par, 1, :], start=True, stop=False)
                    pe.matmul(m.ps[:, RB, NEXP:2 * NEXP], ones16[:, :], oh[:, par, 0, :], start=False, stop=True)
                for j in range(ntile):
                    last = pe.matmul(m.ps[:, RB, 2 * NEXP:3 * NEXP], ones16[:, :], oh[:, par, j, :], start=j == 0, stop=j == ntile - 1)
                last.then_inc(s_rk, 1)

            def transpose(i, par, ntile):
                pe.wait_ge(s_stage, i + 1)
                pe_transpose(pe, m, u, i, lambda j, k: stage[:, par, j, k * P:(k + 1) * P], ntile)

            def step(pe, i, par, n):
                nxt = 0 if n == NPAIR else 1 if n == NPAIR - 1 else 2

                between = {}
                if nxt:
                    between[1] = lambda: transpose(i + 1, 1 - par, nxt)
                if n is None or n >= 3:
                    between[4] = lambda: ranks(pe, i - 3, 1 - par, 2, n)
                pe_hidden(pe, m, u, i, par, 1 if n == NPAIR else 2, between)
                if n is None or n >= 1:
                    logits(pe, i - 1, 1 - par, 2)

            transpose(0, 0, 2)
            steps(pe, step)
            logits(pe, NPAIR, 0, 1)
            for i in range(NPAIR - 2, NPAIR + 1):
                ranks(pe, i, i % 2, tiles(i), i)

        @block.scalar
        def _(act):
            act.sem_inc(u.gelu, UB)
            act.wait_ge(s_w1, 16)
            act.activation(m.w1_hi[:, :, :], w1_raw[:, :, :], ACT.Copy).then_inc(s_w1hi, 1)
            act.wait_ge(s_par, 48)
            act.activation(wg[:, :, 0:NEXP], wg_raw[:, :, :], ACT.Copy).then_inc(s_w1hi, 1)
            act_xt(act, m, u, 0, 0, 2)

            def step(act, i, par, n):
                nxt = 0 if n == NPAIR else 1 if n == NPAIR - 1 else 2
                act_hidden(act, m, u, i, par, 1 if n == NPAIR else 2, nxt)
                if n is not None and n < 4:
                    for k in (2 * n, 2 * n + 1):
                        act.wait_ge(s_wd[k % 2], 16 * (k // 2 + 1))
                        act.activation(m.wd_hi[:, :, k, :], wd_raw[k % 2][:, :, :], ACT.Copy, scale=m.alpha[:, k:k + 1]).then_inc(s_wdhi, 1)
            steps(act, step)
            act.wait_ge(s_oh, NPAIR + 1)
            act.activation(lg[:, 0:NT, :], lg[:, 0:NT, :], ACT.Exp).then_inc(s_ex, 1)

        @block.vector
        def _(dve):
            link = chain_on(m, dve)
            dve_ahead(dve, u)
            dve.sem_inc(s_lgfree, 2)
            link(dve.memset(ones16[:, :], 1.0))
            dve.wait_ge(s_par, 32)
            dve.tensor_tensor(wg_raw[:, :, :], wg_raw[:, :, :], m.alpha[:, :].unsqueeze(2).to_broadcast([P, KH, NEXP]),
                              ALU.mult).then_inc(s_par, 16)
            dve.wait_ge(s_w1hi, 1)
            link(dve.tensor_tensor(m.w1_lo[:, :, :], w1_raw[:, :, :], m.w1_hi[:, :, :].bitcast(F32), ALU.subtract))
            dve.wait_ge(s_w1hi, 2)
            dve.tensor_tensor(wg[:, :, NEXP:], wg_raw[:, :, :], wg[:, :, 0:NEXP], ALU.subtract).then_inc(s_w1lo, 1)
            dve.wait_ge(s_const, 10)

            def choose(dve, i, par, ntile):
                t = slice(0, ntile)

                def lk(ins, n):
                    ins.then_inc(s_choose, 1)
                    dve.wait_ge(s_choose, i * 7 + n)
                dve.wait_ge(u.done, i + 3)
                ps = m.ps[:, LB[par], 0:16 * ntile].rearrange("p (t e) -> p t e", e=16)
                l = now[:, t, :]
                lk(dve.scalar_tensor_tensor(l, ps[:, :, 0:NEXP], m.inv_g[:, 0:1], bg[:, :].unsqueeze(1).to_broadcast([P, ntile, NEXP]), ALU.mult, ALU.add), 1)
                lk(dve.scalar_tensor_tensor(l, ps[:, :, NEXP:], m.inv_g[:, 0:1], l, ALU.mult, ALU.add), 2)
                lk(dve.tensor_reduce(mx[:, t], l, AX.X, ALU.max), 3)
                lk(dve.tensor_tensor(l, l, mx[:, t].unsqueeze(2).to_broadcast([P, ntile, NEXP]), ALU.subtract), 4)
                dve.sem_inc(s_lgfree, 1)
                dve.tensor_copy(lg[:, bass.ds(2 * i, ntile), :], l)
                lk(dve.scalar_tensor_tensor(sc[:, t, :], l, 0.0, prio[:, :].unsqueeze(1).to_broadcast([P, ntile, NEXP]), ALU.is_equal, ALU.mult), 5)
                lk(dve.tensor_reduce(best[:, t], sc[:, t, :], AX.X, ALU.max), 6)
                lk(dve.tensor_tensor(ohf[:, par, t, :], sc[:, t, :], best[:, t].unsqueeze(2).to_broadcast([P, ntile, NEXP]), ALU.is_equal), 7)
                if ntile == 1:
                    link(dve.tensor_scalar(ohf[:, par, 0, :], ohf[:, par, 0, :], valid[:, 0:1], None, ALU.mult))
                dve.tensor_copy(oh[:, par, t, :], ohf[:, par, t, :]).then_inc(s_oh, 1)

            def place(dve, i, par, ntile):
                t = slice(0, ntile)

                def lk(ins, n):
                    ins.then_inc(s_place, 1)
                    dve.wait_ge(s_place, i * 4 + n)
                dve.wait_ge(s_rk, i + 1)
                lk(dve.tensor_tensor(rk[:, t, :], m.ps[:, RB, 0:NEXP * ntile].rearrange("p (t e) -> p t e", e=NEXP),
                                     run[:, :].unsqueeze(1).to_broadcast([P, ntile, NEXP]), ALU.add), 1)
                lk(dve.tensor_tensor(rk[:, t, :], rk[:, t, :], ohf[:, par, t, :], ALU.mult), 2)
                lk(dve.tensor_tensor(run[:, :], run[:, :], m.ps[:, RB, 2 * NEXP:3 * NEXP], ALU.add), 3)
                lk(dve.tensor_reduce(slotf[:, t], rk[:, t, :], AX.X, ALU.add), 4)
                dve.tensor_copy(slot[:, bass.ds(2 * i, ntile)], slotf[:, t]).then_inc(s_slot, 1)

            def step(dve, i, par, n):
                nxt = 0 if n == NPAIR else 1 if n == NPAIR - 1 else 2

                between = {}
                if n is None or n >= 4:
                    between[0] = lambda: place(dve, i - 4, par, 2)
                if n is None or n >= 2:
                    between[3] = lambda: choose(dve, i - 2, par, 2)
                dve_hidden(dve, m, u, i, par, 1 if n == NPAIR else 2, nxt, between)
                if n is not None and n < 4:
                    for k in (2 * n, 2 * n + 1):
                        dve.wait_ge(s_wdhi, k + 1)
                        dve.scalar_tensor_tensor(m.wd_lo[:, :, k, :], wd_raw[k % 2][:, :, :], m.alpha[:, k:k + 1],
                                                 m.wd_hi[:, :, k, :], ALU.mult, ALU.subtract).then_inc(s_wdfree, 1)
            dve_xt(dve, m, u, 0, 0, 2)
            steps(dve, step)
            for i in range(NPAIR - 3, NPAIR + 1):
                place(dve, i, i % 2, tiles(i))
                if i < NPAIR - 1:
                    choose(dve, i + 2, i % 2, tiles(i + 2))
            link(dve.tensor_scalar(padf[:, 0:NEXP], run[:, :], pcol[:, 0:1], None, ALU.add))
            dve.tensor_copy(padi[:, :], padf[:, :]).then_inc(s_pads, 1)
            link(dve.tensor_tensor(nt[:, :], run[0:1, :], m.reg_base[0:1, :], ALU.subtract))
            link(dve.tensor_scalar(nt[:, :], nt[:, :], float(P - 1), None, ALU.add))
            link(dve.tensor_copy(nti[:, :], nt[:, :]))
            link(dve.tensor_scalar(nti[:, :], nti[:, :], 7, None, ALU.arith_shift_right))
            link(dve.tensor_copy(nt[:, :], nti[:, :]))
            dve.memset(tb[:, :], 0.0)
            dve.memset(te[:, :], 0.0)
            link(dve.memset(tr_[:, :], 0.0))
            for e in range(NEXP):
                link(dve.tensor_tensor(tb[:, e + 1:e + 2], tb[:, e:e + 1], nt[:, e:e + 1], ALU.add))
                link(dve.tensor_scalar(tq[:, :], tv[:, :], tb[0:1, e + 1:e + 2], None, ALU.is_ge))
                dve.tensor_tensor(te[:, :], te[:, :], tq[:, :], ALU.add)
                link(dve.scalar_tensor_tensor(tr_[:, :], tq[:, :], nt[0:1, e:e + 1], tr_[:, :], ALU.mult, ALU.add))
            link(dve.tensor_tensor(tr_[:, :], tv[:, :], tr_[:, :], ALU.subtract))
            link(dve.tensor_scalar(tf[:, :], te[:, :], float(REG), None, ALU.mult))
            link(dve.scalar_tensor_tensor(tr_[:, :], tr_[:, :], float(P), tf[:, :], ALU.mult, ALU.add))
            link(dve.tensor_scalar(tr_[:, :], tr_[:, :], float(NEXP * REG), None, ALU.min))
            link(dve.tensor_copy(m.tile_row[0:1, :], tr_[:, :]))
            link(dve.tensor_scalar(te[:, :], te[:, :], float(NEXP - 1), None, ALU.min))
            link(dve.tensor_copy(m.tile_exp[0:1, :], te[:, :]))
            dve.wait_ge(s_ex, 1)
            link(dve.tensor_reduce(m.probs[:, :], lg[:, 0:NT, :], AX.X, ALU.add))
            dve.reciprocal(m.probs[:, :], m.probs[:, :]).then_inc(s_prob, 1)


def experts(nc, m, a):
    RB4 = 4
    take = Place(m, m.r1)
    r = take("in_rows", [P, RB4, 2, RW], F32)
    x1t, outt = take("x1_rows", [P, 2, 2, C + 1], F32), take("out_rows", [P, 2, 2, C], F32)
    bd = take("bdB", [P, NEXP, C], F32)
    y = take("y", [P, 2, 2, C], F32)
    assert take.next <= m.r2
    u = hidden_semaphores(m, "j")
    S = m.sem
    s_bd, s_y, s_out, s_used = S("j_bd"), S("j_y"), S("j_out"), S("j_used")
    s_row = [S(f"j_row{q}") for q in range(RB4)]
    s_gx = [S("j_gx0"), S("j_gx1")]
    s_st = [S("j_st0"), S("j_st1")]
    NPAIR = MAXT // 2
    DB = 5

    with nc.Block() as block:
        @block.sync
        def _(sp):
            def load(i, q):
                for j in range(2):
                    at = sp.value_load(m.tile_row[0:1, bass.ds(2 * i + j, 1)], min_val=0, max_val=NEXP * REG)
                    sp.dma_start(r[:, q, j, :], m.sorted_rows[bass.ds(at, P), :]).then_inc(s_row[q], 16)

            for i in range(RB4):
                load(i, i)
            sp.dma_start(bd[:, :, :].rearrange("p e c -> p (e c)"), bass.AP(a.fbd.tensor, 0, [[0, P], [1, NEXP * C]])).then_inc(s_bd, 16)
            with sp.Fori(1, NPAIR // RB4) as k:
                for q in range(RB4):
                    sp.wait_ge(s_used, k * RB4 + (q + 1 - RB4))
                    load(k * RB4 + q, q)
            sp.wait_ge(s_bd, 16)

        @block.gpsimd
        def _(pool):
            for i in range(NPAIR + 1):
                par, q = i % 2, i % RB4
                if i >= 2:
                    pool.wait_ge(s_st[par], 32 * (i // 2))
                    pool.sem_inc(s_used, 1)
                if i < NPAIR:
                    pool.wait_ge(s_row[q], 32 * (i // RB4 + 1))
                    for j in range(2):
                        pool.indirect_dma_start(x1t[:, par, j, :], None, m.x1_dram,
                                                bass.IndirectOffsetOnAxis(ap=r[:, q, j, RW - 1:RW].bitcast(I32), axis=0)).then_inc(s_gx[par], 16)
                if i >= 1:
                    pool.wait_ge(s_out, i)
                    for j in range(2):
                        pool.indirect_dma_start(a.out, bass.IndirectOffsetOnAxis(ap=r[:, (i - 1) % RB4, j, RW - 1:RW].bitcast(I32), axis=0),
                                                outt[:, 1 - par, j, :], None, bounds_check=N - 1, oob_is_err=False).then_inc(s_st[1 - par], 16)
            for par in range(2):
                pool.wait_ge(s_st[par], 32 * (NPAIR // 2))

        @block.tensor
        def _(pe):
            pe_ahead(pe, u)

            def transpose(i, par, q, uses):
                pe.wait_ge(s_row[q], uses)
                pe_transpose(pe, m, u, i, lambda j, k: r[:, q, j, k * P:(k + 1) * P], 2)

            def down(pe, i, par):
                for j in range(2):
                    e = pe.value_load(m.tile_exp[0:1, bass.ds(2 * i + j, 1)], min_val=0, max_val=NEXP - 1)
                    if j == 0:
                        pe.wait_ge(u.split, KH * i + 2 * KH)
                    pe.wait_ge(s_y, 2 * i + (j + 1))
                    for k in range(KH):
                        w_hi = m.wd_hi[:, bass.ds(e, 1), k, :].rearrange("p a c -> p (a c)")
                        w_lo = m.wd_lo[:, bass.ds(e, 1), k, :].rearrange("p a c -> p (a c)")
                        for q, (h, w) in enumerate(((m.h_hi, w_hi), (m.h_hi, w_lo), (m.h_lo, w_hi))):
                            last = pe.matmul(m.ps[:, DB + j, 0:C], h[:, par, k, j * P:(j + 1) * P], w,
                                             start=q == 0 and k == 0, stop=q == 2 and k == KH - 1)
                last.then_inc(u.done, 1)

            def step(i, q, k):
                par = q % 2
                pe_hidden(pe, m, u, i, par, 2, {1: lambda: transpose(i + 1, 1 - par, (q + 1) % RB4, k * 32 + 32 * (1 + (q + 1) // RB4))})
                down(pe, i - 1, 1 - par)

            transpose(0, 0, 0, 32)
            pe_hidden(pe, m, u, 0, 0, 2, {1: lambda: transpose(1, 1, 1, 32)})
            with pe.Fori(0, (NPAIR - 2) // RB4) as k:
                for q in range(1, RB4 + 1):
                    step(k * RB4 + q, q, k)
            last = (NPAIR - 2) // RB4
            for q in range(1, NPAIR - 1 - last * RB4):
                step(last * RB4 + q, q, last)
            pe_hidden(pe, m, u, NPAIR - 1, 1, 2, {})
            down(pe, NPAIR - 2, 0)
            down(pe, NPAIR - 1, 1)

        def steps(eng, step):
            step(0, 0, 2, True)
            with eng.Fori(0, (NPAIR - 2) // 2) as k:
                step(2 * k + 1, 1, 2, False)
                step(2 * k + 2, 0, 2, False)
            step(NPAIR - 1, 1, 0, False)

        @block.scalar
        def _(act):
            act.sem_inc(u.gelu, UB)
            act_xt(act, m, u, 0, 0, 2)
            steps(act, lambda i, par, nxt, first: act_hidden(act, m, u, i, par, 2, nxt))

        @block.vector
        def _(dve):
            dve_ahead(dve, u)
            dve.sem_inc(s_y, 2)
            dve.wait_ge(s_bd, 16)

            def results(i, par, k):
                e = [dve.value_load(m.tile_exp[0:1, bass.ds(2 * i + j, 1)], min_val=0, max_val=NEXP - 1) for j in range(2)]
                dve.wait_ge(u.done, i + 3)
                dve.wait_ge(s_gx[par], k * 32 + 32)
                for j in range(2):
                    dve.scalar_tensor_tensor(y[:, par, j, :], m.ps[:, DB + j, 0:C], m.inv_g[:, 0:1],
                                             bd[:, bass.ds(e[j], 1), :].rearrange("p a c -> p (a c)"), ALU.mult, ALU.add).then_inc(s_y, 1)
                for j in range(2):
                    dve.wait_ge(s_y, 2 * i + (j + 3))
                    last = dve.scalar_tensor_tensor(outt[:, par, j, :], y[:, par, j, :], x1t[:, par, j, C:C + 1], x1t[:, par, j, 0:C], ALU.mult, ALU.add)
                last.then_inc(s_out, 1)

            dve_xt(dve, m, u, 0, 0, 2)
            dve_hidden(dve, m, u, 0, 0, 2, 2)
            with dve.Fori(0, (NPAIR - 2) // 2) as k:
                dve_hidden(dve, m, u, 2 * k + 1, 1, 2, 2)
                results(2 * k, 0, k)
                dve_hidden(dve, m, u, 2 * k + 2, 0, 2, 2)
                results(2 * k + 1, 1, k)
            dve_hidden(dve, m, u, NPAIR - 1, 1, 2, 0)
            results(NPAIR - 2, 0, NPAIR // 2 - 1)
            results(NPAIR - 1, 1, NPAIR // 2 - 1)


def lay_out(inputs):
    import numpy as np
    named = {"x": inputs["x"], "src": inputs["src"], "dst": inputs["dst"],
             "w1t": inputs["L0_gnn_W1"].T, "g1": inputs["L0_gnn_g1"], "b1": inputs["L0_gnn_b1"],
             "w2t": inputs["L0_gnn_W2"].T, "g2": inputs["L0_gnn_g2"], "b2": inputs["L0_gnn_b2"],
             "fw1": inputs["L0_ffn_W1"], "fb1": inputs["L0_ffn_b1"], "fwg": inputs["L0_ffn_Wg"],
             "fbg": inputs["L0_ffn_bg"], "fwd": inputs["L0_ffn_Wd"], "fbd": inputs["L0_ffn_bd"]}
    return {k: np.ascontiguousarray(v) for k, v in named.items()}


def kernel(**inputs):
    import numpy as np
    import concourse.bacc as bacc
    from concourse.bass_utils import run_bass_kernel_spmd
    arrays = lay_out(inputs)
    nc = bacc.Bacc("TRN2", target_bir_lowering=False, num_devices=1)
    aps = [nc.dram_tensor(name, v.shape, mybir.dt.from_np(v.dtype), kind="ExternalInput").ap()
           for name, v in arrays.items()]
    out = nc.dram_tensor("out", (N, C), F32, kind="ExternalOutput").ap()
    gnn_ffn_kernel(nc, *aps, out)
    nc.compile()
    res = run_bass_kernel_spmd(nc, [arrays], core_ids=[0])
    return np.asarray(res.results[0]["out"])
```

```python
from contextlib import ExitStack

import concourse.bass as bass
from concourse import mybir

F32, F16, I32, F32R = mybir.dt.float32, mybir.dt.float16, mybir.dt.int32, mybir.dt.float32r
ACT = mybir.ActivationFunctionType
ALU = mybir.AluOpType
AX = mybir.AxisListType

P = 128
N, C, IC, HID, NEXP, NE = 6250, 256, 512, 1024, 8, 100000
EPS = 1e-5
NT = -(-N // P)
NP_ = NT * P
LAST = N - (NT - 1) * P
KC, KI, KH = C // P, IC // P, HID // P
WIN = 5
NW = N // WIN
SB = 250
NSB = N // SB
WPS = SB // WIN
GRP = 2
GPS = WPS // GRP
WP, WJ = 125, 10
KEYS = WIN * NT
RING = 5
NTE = -(-NE // P)
ROW = 8
NROWS = 12512
EPAD = 783 * P
PADROW = NE // ROW
FAR = 1 << 20
T1SCALE = 2048.0


def gnn_ffn_kernel(nc, x, src, dst, w1t, g1, b1, w2t, g2, b2, fw1, fb1, fwg, fbg, fwd, fbd, out):
    with ExitStack() as ctx:
        m = Names()
        m.sem = lambda name: ctx.enter_context(nc.semaphore(name))
        base = 16512

        def at(name, off, shape, dt):
            return nc.alloc_sbuf_tensor_at(name, shape, dt, offset=base + off)

        R1, R2, R3, R4, R5 = 0, 52224, 102400, 152576, 177664
        END = 229368 - base
        m.at = at
        m.r1, m.r2, m.r3, m.r4, m.r5 = R1, R2, R3, R4, R5
        m.x = at("x_sb", R3, [P, NT, C], F32)
        m.table1 = at("table1", R1, [P, NT, 2 * C], F16)
        m.table2 = at("table2", R2, [P, NT, 2 * C], F16)
        m.agg1 = at("agg1", R2, [P, KC, NP_], F32)
        m.agg2 = at("agg2", R1, [P, KC, NP_], F32)
        m.adj = at("adj", R3, [P, 2, NT, SB], F16)
        m.probs = at("probs", R2 - 256, [P, NT], F32)
        m.rows = at("rows", R1, [P, NT, RW], F32)
        m.disB = at("disB", R4, [P, NP_], F32)
        m.h01 = at("h01", R1, [P, 2, NP_], F32)
        m.h23 = at("h23", R3, [P, 2, NP_], F32)
        m.end = END
        take = Place(m, R5)

        def small(name, shape, dt):
            return take(name, [P, *shape], dt)

        m.key = small("key", [WJ, WP + WPS // WJ], F32)
        m.rem = small("rem", [WJ, WP + WPS // WJ], F32)
        m.id32 = small("id32", [P], F32)
        m.id16 = small("id16", [P], F16)
        m.iota_r = small("iota_r", [P], F16)
        m.iota_k = small("iota_k", [KEYS + 1], F16)
        m.ones = small("ones", [P], F32)
        m.disP = small("disP", [NT], F32)
        m.mean = small("mean", [NT], F32)
        m.rstd = small("rstd", [NT], F32)
        m.levels = small("levels", [1], I32)
        m.row0 = small("row0", [WJ], F32)
        m.w5 = small("w5", [WJ], F32)
        m.step16 = small("step16", [1], F32)
        m.bn_g1 = small("bn_g1", [KI], F32)
        m.bn_b1 = small("bn_b1", [KI], F32)
        m.bn_g2 = small("bn_g2", [KC], F32)
        m.bn_b2 = small("bn_b2", [KC], F32)
        m.aff_a1 = small("aff_a1", [KI], F32)
        m.aff_b1 = small("aff_b1", [KI], F32)
        m.scale2 = small("scale2", [1], F32)
        m.sc_col = small("sc_col", [8], F32)
        m.alpha = small("alpha", [KH], F32)
        m.beta = small("beta", [KH], F32)
        m.inv_g = small("inv_g", [1], F32)
        m.b1f = small("b1f", [KH], F32)
        m.reg_base = small("reg_base", [NEXP], F32)
        m.tile_row = small("tile_row", [64], I32)
        m.tile_exp = small("tile_exp", [64], I32)
        m.stats1 = small("stats1", [KI, NSB, 6], F32)
        m.work = take.next
        m.ps = ctx.enter_context(nc.psum_tensor("ps", [P, 8, 512], F32))
        m.src_pad = nc.dram_tensor("src_pad", [EPAD], I32, kind="Internal").ap()
        m.dst_pad = nc.dram_tensor("dst_pad", [EPAD], I32, kind="Internal").ap()
        m.edge_rows = nc.dram_tensor("edge_rows", [NROWS, 2 * P], I32, kind="Internal").ap()
        m.first_dram = nc.dram_tensor("first_dram", [(NT + 1) * P], F32, kind="Internal").ap()
        m.dis_dram = nc.dram_tensor("dis_dram", [NP_], F32, kind="Internal").ap()
        m.sorted_rows = nc.dram_tensor("sorted_rows", [(NEXP + 1) * REG, RW], F32, kind="Internal").ap()
        m.x1_dram = nc.dram_tensor("x1_dram", [NP_, C + 1], F32, kind="Internal").ap()
        m.s_chain, m.chained = m.sem("chain"), 0
        args = Names()
        args.x, args.src, args.dst, args.out = x, src, dst, out
        args.w1t, args.g1, args.b1, args.w2t, args.g2, args.b2 = w1t, g1, b1, w2t, g2, b2
        args.fw1, args.fb1, args.fwg, args.fbg, args.fwd, args.fbd = fw1, fb1, fwg, fbg, fwd, fbd
        m.s_align = [m.sem(f"align_{n}") for n in ("dve", "rowi", "edges", "keyw", "keyt", "spare")]
        prepare(nc, m, args)
        build_table1(nc, m, args)
        m.agg = aggregate_tensors(m)
        aggregate(nc, m, 0, m.table1, m.agg1, T1SCALE)
        linear1(nc, m, args)
        linear2(nc, m, args)
        aggregate(nc, m, 1, m.table2, m.agg2, 1.0)
        m.gw = gate_weights(m)
        finish_gnn(nc, m, args)
        ffn(nc, m, args)


class Names:
    pass


class Place:

    def __init__(self, m, start):
        self.m, self.next = m, start

    def __call__(self, name, shape, dt):
        size = mybir.dt.size(dt)
        for n in shape[1:]:
            size *= n
        t = self.m.at(name, self.next, shape, dt)
        self.next += -(-size // 32) * 32
        assert self.next <= self.m.end, (name, self.next - self.m.end)
        return t


def align_edges(m, t, eng, name, runs, level0, meanwhile=None):
    if name == "vector":
        if level0:
            eng.tensor_copy(t.rowf[:, :], m.row0[:WP, :]).then_inc(t.s_dve, 1)
        else:
            eng.tensor_scalar(t.rowf[:, :], m.row0[:WP, :], m.step16[:WP, 0:1], float(PADROW), ALU.add, ALU.min).then_inc(t.s_dve, 1)
        eng.wait_ge(t.s_dve, runs * 6 + 1)
        eng.tensor_copy(t.rowi[:, :], t.rowf[:, :]).then_inc(t.s_rowi, 1)
        if meanwhile:
            meanwhile(eng)
        eng.wait_ge(t.s_edges, (runs + 1) * 16 * WJ)
        eng.wait_ge(t.s_spare, runs + 1)
        dstv = t.edges[:, :, P:2 * P]
        srcv = t.edges[:, :, 0:P]
        eng.tensor_tensor(t.dl[:, :, :], dstv, m.w5[:WP, :].unsqueeze(2).to_broadcast([WP, WJ, P]), ALU.subtract).then_inc(t.s_dve, 1)
        eng.tensor_scalar(t.chunk[:, :, :], srcv, 7, None, ALU.arith_shift_right).then_inc(t.s_dve, 1)
        eng.tensor_scalar(t.lowi[:, :, :], srcv, P - 1, None, ALU.bitwise_and).then_inc(t.s_dve, 1)
        eng.wait_ge(t.s_dve, runs * 6 + 4)
        eng.scalar_tensor_tensor(t.keyw[:, :, :], t.dl[:, :, :], float(NT), t.chunk[:, :, :], ALU.mult, ALU.add).then_inc(t.s_keyw, 1)
        eng.tensor_copy(t.lowf[:, :, :], t.lowi[:, :, :]).then_inc(t.s_keyw, 1)
        for b in range(5):
            eng.wait_ge(t.s_keyt, runs * 5 + b + 1)
            for q in range(4):
                k = 4 * b + q
                dest = (m.key if k < WJ else m.rem)[:, k % WJ, 0:WP]
                last = eng.tensor_copy(dest, m.ps[:, b, q * WP:(q + 1) * WP])
            if b == 4:
                last.then_inc(t.s_dve, 2)
        eng.wait_ge(t.s_dve, runs * 6 + 6)
    elif name == "gpsimd":
        eng.wait_ge(t.s_rowi, runs + 1)
        eng.tensor_tensor(t.spare[:, :], t.rowf[:, :], t.rowf[:, :], ALU.add).then_inc(t.s_spare, 1)
        for j in range(WJ):
            eng.indirect_dma_start(t.edges[:, j, :], None, m.edge_rows,
                                   bass.IndirectOffsetOnAxis(ap=t.rowi[:, j:j + 1], axis=0)).then_inc(t.s_edges, 16)
    elif name == "tensor":
        eng.wait_ge(t.s_keyw, runs * 2 + 2)
        for k in range(2 * WJ):
            b, q = divmod(k, 4)
            from_ = (t.keyw if k < WJ else t.lowf)[:, k % WJ, :]
            ins = eng.transpose(m.ps[:, b, q * WP:(q + 1) * WP], from_, m.id32[:WP, :WP])
            if q == 3:
                ins.then_inc(t.s_keyt, 1)


def align_tensors(m, tag, off):
    t = Names()
    t.s_dve, t.s_rowi, t.s_edges, t.s_keyw, t.s_keyt, t.s_spare = m.s_align
    t.edges = m.at(f"edges_{tag}", off, [WP, WJ, 2 * P], I32)
    t.dl = m.at(f"dl_{tag}", off + 10240, [WP, WJ, P], F32)
    t.chunk = m.at(f"chunk_{tag}", off + 15360, [WP, WJ, P], I32)
    t.lowi = m.at(f"lowi_{tag}", off + 20480, [WP, WJ, P], I32)
    t.keyw = m.at(f"keyw_{tag}", off + 25600, [WP, WJ, P], F32)
    t.lowf = m.at(f"lowf_{tag}", off + 30720, [WP, WJ, P], F32)
    t.rowf = m.at(f"rowf_{tag}", off + 35840, [WP, WJ], F32)
    t.spare = m.at(f"spare_{tag}", off + 35968, [WP, WJ], F32)
    t.rowi = m.at(f"rowi_{tag}", off + 35904, [WP, WJ], I32)
    return t


def prepare(nc, m, a):
    NHALF = NTE // 2
    NG = 7
    ND = 4
    assert NT % NG == 0
    scales = ffn_scales(m, a)
    off = m.r4
    head_i = m.at("head_i", off, [1, NTE], I32)
    head_f = m.at("head_f", off + 3136, [1, NTE], F32)
    heads = m.at("heads", off + 6272, [P, NTE], F32)
    junk = m.at("junk", off + 9408, [P, 2, NTE], F16)
    junk_a = m.at("junk_a", off + 12544, [P, 2, NTE], F16)
    near = m.at("near", 0, [P, NT, P], I32)
    less = m.at("less", m.r2, [P, NT, P], F16)
    take = Place(m, m.work)
    padt = take("padt", [1, 2, EPAD - NE], I32)
    far_f = take("far_f", [1, P], F32)
    nodes, tcnt, rowf = take("nodes", [P, NT], F32), take("tcnt", [P, NT], F32), take("nrowf", [P, NT], F32)
    rowi = take("nrowi", [P, NT], I32)
    cnt, first = take("cnt", [P, NT], F32), take("first", [P, NT], F32)
    firstT, nextT = take("firstT", [NT, P], F32), take("nextT", [NT, P], F32)
    degT, disT = take("degT", [NT, P], F32), take("disT", [NT, P], F32)
    degP, nodesm = take("degP", [P, NT], F32), take("nodesm", [P, NT], F32)
    mhalfT = take("mhalfT", [P, P], F32)
    wa, wb = take("win_a", [WP, 5 * WJ], F32), take("win_b", [WP, 5 * WJ], F32)
    wi, wi8 = take("win_i", [WP, WJ], I32), take("win_i8", [WP, WJ], I32)
    wn, wm = take("win_n", [WP, WJ], F32), take("win_m", [WP, 1], F32)
    lv, lvi = take("lv", [1, 4], F32), take("lvi", [1, 4], I32)
    st, mv, vare = take("ln_st", [P, NT, 6], F32), take("ln_mv", [P, NT, 2], F32), take("vare", [P, NT], F32)
    t = align_tensors(m, "pa", m.r2 + 12544)
    S = m.sem
    s_x, s_heads, s_pads, s_pad_mem, s_copy, s_rows = S("a_x"), S("a_heads"), S("a_pads"), S("a_pad_mem"), S("a_copy"), S("a_rows")
    s_const, s_headf, s_headp, s_nrow, s_near, s_first, s_firstT = S("a_const"), S("a_headf"), S("a_headp"), S("a_nrow"), S("a_near"), S("a_first"), S("a_firstT")
    s_firstS, s_fd, s_next, s_deg, s_dis, s_disd, s_disB = S("a_firstS"), S("a_fd"), S("a_next"), S("a_deg"), S("a_dis"), S("a_disd"), S("a_disB")
    s_degP, s_disS = S("a_degP"), S("a_disS")
    s_heads_b, s_sign, s_signs = S("a_heads_b"), S("a_sign"), S("a_signs")
    s_disT, s_wm, s_wmT, s_vare, s_rstd, s_par, s_xtail = S("a_disT"), S("a_wm"), S("a_wmT"), S("a_vare"), S("a_rstd"), S("a_par"), S("a_xtail")

    with nc.Block() as block:
        @block.sync
        def _(sp):
            with nc.allow_non_contiguous_dma("the first dst of each edge tile"):
                sp.dma_start(head_i[0:1, :], bass.AP(a.dst.tensor, 0, [[P, 1], [P, NTE]])).then_inc(s_heads, 16)
            sp.dma_start(m.dst_pad[0:NE], a.dst).then_inc(s_copy, 16)
            sp.dma_start(m.src_pad[0:NE], a.src).then_inc(s_copy, 16)
            sp.wait_ge(s_pad_mem, 1)
            sp.dma_start(m.src_pad[NE:EPAD].rearrange("(a n) -> a n", a=1), padt[0:1, 0, :]).then_inc(s_pads, 16)
            sp.dma_start(m.dst_pad[NE:EPAD].rearrange("(a n) -> a n", a=1), padt[0:1, 1, :]).then_inc(s_pads, 16)
            sp.dma_start(m.first_dram[NP_:NP_ + P].rearrange("(a n) -> a n", a=1), far_f[0:1, :]).then_inc(s_pads, 16)
            for i in range(6):
                sp.dma_start(m.x[:, 8 * i:8 * i + 8, :],
                             a.x[1024 * i:1024 * (i + 1), :].rearrange("(t p) c -> p t c", p=P)).then_inc(s_x, 16)
            sp.wait_ge(s_xtail, 1)
            sp.dma_start(m.x[:LAST, NT - 1, :], a.x[(NT - 1) * P:N, :]).then_inc(s_x, 16)
            sp.wait_ge(s_copy, 32)
            sp.wait_ge(s_pads, 48)
            for k, pad in enumerate((m.src_pad, m.dst_pad)):
                sp.dma_start(m.edge_rows[:, k * P:(k + 1) * P],
                             bass.AP(pad.tensor, 0, [[ROW, NROWS], [1, P]])).then_inc(s_rows, 16)
            with nc.allow_non_contiguous_dma("batch norm's parameters to partitions"):
                sp.dma_start(m.bn_g1[:, :], a.g1.rearrange("(f p) -> p f", p=P)).then_inc(s_par, 16)
                sp.dma_start(m.bn_b1[:, :], a.b1.rearrange("(f p) -> p f", p=P)).then_inc(s_par, 16)
                sp.dma_start(m.bn_g2[:, :], a.g2.rearrange("(f p) -> p f", p=P)).then_inc(s_par, 16)
                sp.dma_start(m.bn_b2[:, :], a.b2.rearrange("(f p) -> p f", p=P)).then_inc(s_par, 16)
            scales[0](nc, sp)
            sp.wait_ge(s_firstS, 1)
            sp.dma_start(m.first_dram[0:NP_].rearrange("(t p) -> t p", p=P), firstT[:, :]).then_inc(s_fd, 16)
            sp.wait_ge(s_fd, 16)
            sp.dma_start(nextT[:, :], m.first_dram[1:NP_ + 1].rearrange("(t p) -> t p", p=P)).then_inc(s_next, 16)
            sp.dma_start(wa[:, :], m.first_dram[0:N].rearrange("(p w) -> p w", p=WP)).then_inc(s_next, 16)
            sp.dma_start(wb[:, :], m.first_dram[WIN:N + WIN].rearrange("(p w) -> p w", p=WP)).then_inc(s_next, 16)
            sp.wait_ge(s_disS, 1)
            sp.dma_start(m.dis_dram.rearrange("(t p) -> t p", p=P), disT[:, :]).then_inc(s_disd, 16)
            sp.wait_ge(s_disd, 16)
            sp.dma_start(m.disB[:, :], bass.AP(m.dis_dram.tensor, 0, [[0, P], [1, NP_]])).then_inc(s_disB, 16)
            sp.wait_ge(s_par, 64)
            sp.wait_ge(s_disB, 16)

        @block.scalar
        def _(act):
            act.wait_ge(s_heads_b, 1)
            for i in range(NT):
                if i % NG >= ND:
                    n = i // NG * (NG - ND) + i % NG - ND
                    if n >= 2:
                        act.wait_ge(s_sign, n - 1)
                    act.activation(junk_a[:, n % 2, :], heads[:, :], ACT.Sign, bias=nodesm[:, i:i + 1], scale=-1.0,
                                   accum_out=tcnt[:, i:i + 1]).then_inc(s_sign, 1)
                    if i % NG == NG - 1:
                        act.wait_ge(s_sign, n + 1)
                        act.sem_inc(s_signs, 1)
            act.wait_ge(s_near, 16 * NT)
            scales[1](act)

        @block.gpsimd
        def _(pool):
            pool.iota(nodes[:, :], [[P, NT]], base=0, channel_multiplier=1, allow_small_or_imprecise_dtypes=True).then_inc(s_const, 1)
            pool.memset(m.id32[:, :], 0.0).then_inc(s_const, 1)
            pool.memset(m.id16[:, :], 0.0).then_inc(s_const, 1)
            pool.memset(mhalfT[:, :], -0.5).then_inc(s_const, 1)
            pool.wait_ge(s_const, 4)
            for mat in (m.id32, m.id16):
                pool.affine_select(out=mat[:, :], in_=mat[:, :], compare_op=ALU.not_equal, fill=1.0,
                                   base=0, pattern=[[-1, P]], channel_multiplier=1).then_inc(s_const, 1)
            pool.iota(m.iota_r[:, :], [[1, P]], base=0, channel_multiplier=0, allow_small_or_imprecise_dtypes=True).then_inc(s_const, 1)
            pool.iota(m.iota_k[:, :], [[1, KEYS + 1]], base=0, channel_multiplier=0, allow_small_or_imprecise_dtypes=True).then_inc(s_const, 1)
            pool.iota(m.w5[:WP, :], [[WIN, WJ]], base=0, channel_multiplier=WIN * WJ, allow_small_or_imprecise_dtypes=True).then_inc(s_const, 1)
            pool.wait_ge(s_copy, 32)
            pool.wait_ge(s_pads, 48)
            for i in range(NT):
                if i % NG == 0:
                    pool.wait_ge(s_nrow, i // NG + 1)
                pool.indirect_dma_start(near[:, i, :], None, m.dst_pad.rearrange("(t p) -> t p", p=P),
                                        bass.IndirectOffsetOnAxis(ap=rowi[:, i:i + 1], axis=0)).then_inc(s_near, 16)
            pool.wait_ge(s_vare, 1)
            pool.tensor_tensor(m.rstd[:, :], vare[:, :], mhalfT[:, :NT], ALU.pow).then_inc(s_rstd, 1)
            pool.wait_ge(s_degP, 2)
            pool.tensor_tensor(m.disP[:, :], degP[:, :], mhalfT[:, :NT], ALU.pow).then_inc(s_dis, 1)
            pool.wait_ge(s_rows, 32)
            align_edges(m, t, pool, "gpsimd", 0, True)

        @block.tensor
        def _(pe):
            pe.wait_ge(s_headf, 2)
            for k in range(2):
                pe.matmul(m.ps[:, k, 0:NHALF], m.ones[0:1, :], head_f[0:1, k * NHALF:(k + 1) * NHALF],
                          start=True, stop=True).then_inc(s_headp, 1)
            pe.wait_ge(s_const, 6)
            pe.wait_ge(s_first, 1)
            pe.transpose(m.ps[:NT, 2, 0:P], first[:, :], m.id32[:, :]).then_inc(s_firstT, 1)
            pe.wait_ge(s_deg, 1)
            pe.transpose(m.ps[:, 4, 0:NT], degT[:, :], m.id32[:NT, :NT]).then_inc(s_degP, 1)
            pe.wait_ge(s_wm, 1)
            pe.transpose(m.ps[:1, 3, 0:WP], wm[:, :], m.id32[:WP, :WP]).then_inc(s_wmT, 1)
            pe.wait_ge(s_dis, 1)
            pe.transpose(m.ps[:NT, 5, 0:P], m.disP[:, :], m.id32[:, :]).then_inc(s_disT, 1)
            scales[2](pe)
            align_edges(m, t, pe, "tensor", 0, True)

        @block.vector
        def _(dve):
            link = chain_on(m, dve)
            dve.memset(m.ones[:, :], 1.0).then_inc(s_headf, 1)
            dve.memset(m.key[:, :, WP:], 0.0)
            dve.memset(m.rem[:, :, WP:], 0.0)
            link(dve.memset(far_f[:, :], float(NE)))
            link(dve.memset(padt[:, 0, :], 0))
            dve.memset(padt[:, 1, :], FAR).then_inc(s_pad_mem, 1)
            dve.memset(m.x[:, NT - 1, :], 0.0).then_inc(s_xtail, 1)
            link(dve.memset(m.step16[:, :], 0.0))
            dve.wait_ge(s_heads, 16)
            dve.tensor_copy(head_f[:, :], head_i[:, :]).then_inc(s_headf, 1)
            dve.wait_ge(s_headp, 2)
            link(dve.tensor_copy(heads[:, :].rearrange("p (k n) -> p k n", k=2), m.ps[:, 0:2, 0:NHALF]))
            dve.wait_ge(s_const, 1)
            dve.tensor_scalar(nodesm[:, :], nodes[:, :], -0.5, None, ALU.add).then_inc(s_heads_b, 1)
            for q in range(NT // NG):
                for i in range(q * NG, q * NG + ND):
                    if q or i >= 2:
                        dve.wait_ge(m.s_chain, m.chained - 1)
                    m.chained += 1
                    dve.tensor_scalar(junk[:, m.chained % 2, :], heads[:, :], nodes[:, i:i + 1], None, ALU.is_lt, ALU.add,
                                      accum_out=tcnt[:, i:i + 1]).then_inc(m.s_chain, 1)
                mine, acts = slice(q * NG, q * NG + ND), slice(q * NG + ND, (q + 1) * NG)
                dve.wait_ge(m.s_chain, m.chained)
                dve.tensor_scalar(rowf[:, mine], tcnt[:, mine], -1.0, 0.0, ALU.add, ALU.max)
                dve.wait_ge(s_signs, q + 1)
                link(dve.tensor_scalar(rowf[:, acts], tcnt[:, acts], 0.5, NTE / 2.0 - 1.0, ALU.mult, ALU.add))
                link(dve.tensor_scalar(rowf[:, acts], rowf[:, acts], 0.0, None, ALU.max))
                g = slice(q * NG, (q + 1) * NG)
                dve.tensor_copy(rowi[:, g], rowf[:, g]).then_inc(s_nrow, 1)
            dve.wait_ge(s_x, 16 * 7)
            for i in range(NT):
                last = dve.bn_stats(st[:, i, :], m.x[:, i, :])
            link(last)
            for i in range(NT):
                last = dve.bn_aggr(mv[:, i, :], st[:, i, :])
            link(last)
            dve.tensor_copy(m.mean[:, :], mv[:, :, 0])
            dve.tensor_scalar(vare[:, :], mv[:, :, 1], EPS, None, ALU.add).then_inc(s_vare, 1)
            dve.wait_ge(s_near, 16 * NT)
            link(dve.tensor_tensor(less[:, :, :], near[:, :, :], nodes[:, :].unsqueeze(2).to_broadcast([P, NT, P]), ALU.is_lt))
            link(dve.tensor_reduce(cnt[:, :], less[:, :, :], AX.X, ALU.add))
            dve.scalar_tensor_tensor(first[:, :], rowf[:, :], float(P), cnt[:, :], ALU.mult, ALU.add).then_inc(s_first, 1)
            dve.wait_ge(s_firstT, 1)
            dve.tensor_copy(firstT[:, :], m.ps[:NT, 2, 0:P]).then_inc(s_firstS, 1)
            dve.wait_ge(s_next, 48)
            link(dve.tensor_tensor(degT[:, :], nextT[:, :], firstT[:, :], ALU.subtract))
            dve.tensor_scalar(degT[:, :], degT[:, :], 1.0, None, ALU.add).then_inc(s_deg, 1)
            dve.wait_ge(s_degP, 1)
            dve.tensor_copy(degP[:, :], m.ps[:, 4, 0:NT]).then_inc(s_degP, 1)
            link(dve.tensor_copy(wi[:, :], wa[:, 0::WIN]))
            link(dve.tensor_scalar(wi8[:, :], wi[:, :], 3, None, ALU.arith_shift_right))
            link(dve.tensor_copy(m.row0[:WP, :], wi8[:, :]))
            link(dve.scalar_tensor_tensor(wn[:, :], m.row0[:WP, :], float(-ROW), wb[:, 0::WIN], ALU.mult, ALU.add))
            dve.tensor_reduce(wm[:, :], wn[:, :], AX.X, ALU.max).then_inc(s_wm, 1)
            dve.wait_ge(s_wmT, 1)
            link(dve.tensor_reduce(lv[:, 0:1], m.ps[:1, 3, 0:WP], AX.X, ALU.max))
            link(dve.tensor_scalar(lv[:, 1:2], lv[:, 0:1], float(P - 1), float(P), ALU.add, ALU.max))
            link(dve.tensor_copy(lvi[:, 0:1], lv[:, 1:2]))
            link(dve.tensor_scalar(m.levels[0:1, :], lvi[:, 0:1], 7, None, ALU.arith_shift_right))
            dve.wait_ge(s_disT, 1)
            dve.tensor_copy(disT[:, :], m.ps[:NT, 5, 0:P]).then_inc(s_disS, 1)
            dve.wait_ge(s_rstd, 1)
            align_edges(m, t, dve, "vector", 0, True, meanwhile=scales[3])


def table_groups():
    return [(4 * g, min(4, NT - 4 * g)) for g in range(-(-NT // 4))]


def build_table1(nc, m, a):
    scale, shift = m.at("t1_scale", m.work, [P, NT], F32), m.at("t1_shift", m.work + 224, [P, NT], F32)
    s_scale, s_xs, s_hi, s_lo = m.sem("b_scale"), m.sem("b_xs"), m.sem("b_hi"), m.sem("b_lo")
    s_tr, s_ev = m.sem("l1_tr"), m.sem("l1_ev")
    groups = table_groups()
    last = len(groups) - 1
    ours = [g for g in range(last) if g % 4 == 3]
    s_xd = m.sem("b_xd")

    with nc.Block() as block:
        @block.vector
        def _(dve):
            link = chain_on(m, dve)
            link(dve.scalar_tensor_tensor(scale[:, :], m.rstd[:, :], T1SCALE, m.disP[:, :], ALU.mult, ALU.mult))
            dve.scalar_tensor_tensor(shift[:, :], m.mean[:, :], -1.0, scale[:, :], ALU.mult, ALU.mult).then_inc(s_scale, 1)
            for g, (t0, k) in enumerate(groups):
                if g + 2 in ours:
                    t2, k2 = groups[g + 2]
                    for i in range(t2, t2 + k2):
                        ins = dve.tensor_scalar(m.x[:, i, :], m.x[:, i, :], m.mean[:, i:i + 1], scale[:, i:i + 1], ALU.subtract, ALU.mult)
                    ins.then_inc(s_xd, 1)
                    dve.wait_ge(s_xd, ours.index(g + 2) + 1)
                dve.wait_ge(s_hi, g + 1)
                dve.tensor_tensor(m.table1[:, t0:t0 + k, C:], m.x[:, t0:t0 + k, :], m.table1[:, t0:t0 + k, :C],
                                  ALU.subtract).then_inc(s_lo, 1)
                if g >= 1:
                    loops_out(dve, m, m.agg1, T1SCALE, g - 1, s_tr, s_ev)
            loops_out(dve, m, m.agg1, T1SCALE, last, s_tr, s_ev)

        @block.scalar
        def _(act):
            def normalise(g):
                t0, k = groups[g]
                for i in range(t0, t0 + k):
                    ins = act.activation(m.x[:, i, :], m.x[:, i, :], ACT.Identity, bias=shift[:, i:i + 1], scale=scale[:, i:i + 1])
                ins.then_inc(s_xs, 1)

            act.wait_ge(s_scale, 1)
            normalise(0)
            for g, (t0, k) in enumerate(groups):
                if g < last and g + 1 not in ours:
                    normalise(g + 1)
                if g in ours:
                    act.wait_ge(s_xd, ours.index(g) + 1)
                else:
                    act.wait_ge(s_xs, g + 1 - sum(o < g for o in ours))
                act.activation(m.table1[:, t0:t0 + k, :C], m.x[:, t0:t0 + k, :], ACT.Copy).then_inc(s_hi, 1)

        @block.tensor
        def _(pe):
            for g in range(len(groups)):
                pe.wait_ge(s_lo, g + 1)
                loops_in(pe, m, m.table1, g, s_tr, s_ev)


def loops_in(pe, m, table, g, s_tr, s_ev):
    t0, k = table_groups()[g]
    for h in range(KC):
        n = g * KC + h
        if n >= 8:
            pe.wait_ge(s_ev, n - 7)
        for i in range(k):
            for half in range(2):
                last = pe.matmul(m.ps[:, n % 8, i * P:(i + 1) * P],
                                 table[:, t0 + i, half * C + h * P:half * C + (h + 1) * P], m.id16[:, :],
                                 start=half == 0, stop=half == 1)
        last.then_inc(s_tr, 1)


def loops_out(dve, m, agg, factor, g, s_tr, s_ev):
    t0, k = table_groups()[g]
    cols = slice(t0 * P, (t0 + k) * P)
    for h in range(KC):
        n = g * KC + h
        dve.wait_ge(s_tr, n + 1)
        dve.scalar_tensor_tensor(agg[:, h, cols], m.ps[:, n % 8, 0:k * P], 1.0 / factor, m.disB[:, cols],
                                 ALU.mult, ALU.mult).then_inc(s_ev, 1)


def self_loops(nc, m, tag, table, agg, factor):
    s_tr, s_ev = m.sem(f"{tag}_tr"), m.sem(f"{tag}_ev")
    with nc.Block() as block:
        @block.tensor
        def _(pe):
            for g in range(len(table_groups())):
                loops_in(pe, m, table, g, s_tr, s_ev)

        @block.vector
        def _(dve):
            for g in range(len(table_groups())):
                loops_out(dve, m, agg, factor, g, s_tr, s_ev)


def aggregate_tensors(m):
    take = Place(m, m.work)
    g = Names()
    g.oh_r, g.oh_k = take("oh_r", [P, RING, GRP, P], F16), take("oh_k", [P, RING, GRP, KEYS + 1], F16)
    g.col_k, g.col_r = take("col_k", [P, 2, WPS], F32), take("col_r", [P, 2, WPS], F32)
    g.part = take("agg_part", [P, KC, SB], F32)
    g.align = align_tensors(m, "agg", m.r3)
    g.s_col = m.sem("agg_col")
    g.s_oh = m.sem("agg_oh")
    g.s_used = m.sem("agg_used")
    g.s_adj = m.sem("agg_adj")
    g.s_half = m.sem("agg_half")
    g.s_part = m.sem("agg_part")
    g.s_evac = m.sem("agg_evac")
    g.s_go = m.sem("agg_go")
    g.s_step = m.sem("agg_step")
    return g


def aggregate(nc, m, second, table, agg, factor):
    a = m.agg
    oh_r, oh_k, col_k, col_r, t = a.oh_r, a.oh_k, a.col_k, a.col_r, a.align
    s_col, s_oh, s_used, s_adj, s_half, s_evac = a.s_col, a.s_oh, a.s_used, a.s_adj, a.s_half, a.s_evac
    EVERY = 6

    def walk(eng, name, head, step, tail):
        nlev = eng.value_load(m.levels[0:1, 0:1], min_val=1, max_val=NTE + 1)
        with eng.Fori(0, nlev) as level:
            run = eng.snap(level + nlev) if second else level
            with eng.If(nlev > 1):
                between_levels(eng, name, run)
            b = eng.snap(run * NSB)
            a.run = run
            head(eng, b)
            for k in range(2):
                step(eng, b + k, k, k)
            with eng.Fori(1, (NSB - 1) // 2) as k:
                bb = eng.snap(b + 2 * k)
                step(eng, bb, 2 * k, 0)
                step(eng, bb + 1, 2 * k + 1, 1)
            tail(eng, b)

    def between_levels(eng, name, run):
        align_edges(m, t, eng, name, run + 1, False)
        if name == "vector":
            eng.tensor_scalar(m.step16[:, :], m.step16[:, :], float(P // ROW), None, ALU.add).then_inc(a.s_step, 1)
            eng.wait_ge(a.s_step, run + 1)
            eng.sem_inc(a.s_go, 1)
        elif name == "tensor":
            eng.wait_ge(a.s_go, run + 1)

    def columns(dve, par, s):
        for col, whole in ((col_k, m.key), (col_r, m.rem)):
            last = dve.tensor_copy(col[:, par, :].rearrange("e (p j) -> e p j", j=WJ),
                                   whole[:, :, bass.ds(s * (WPS // WJ), WPS // WJ)].rearrange("e j p -> e p j"))
        last.then_inc(s_col, 1)

    def one_hots(dve, b, par, g):
        dve.wait_ge(s_used, b * GPS + (g + 1))
        for i in range(GRP):
            window = GRP * g + i
            dve.tensor_scalar(oh_r[:, g % RING, i, :], m.iota_r[:, :], col_r[:, par, window:window + 1], None, ALU.is_equal)
            last = dve.tensor_scalar(oh_k[:, g % RING, i, :], m.iota_k[:, :], col_k[:, par, window:window + 1], None, ALU.is_equal)
        last.then_inc(s_oh, 1)

    def add_half(dve, b, s, h, part):
        cols = bass.ds(s * SB, SB)
        if part == 0:
            dve.wait_ge(s_half, b * KC + (KC + h + 1))
            dve.wait_ge(s_evac, b * KC + (h + 1))
            dve.scalar_tensor_tensor(a.part[:, h, :], m.ps[:, RING + h, 0:SB], 1.0 / factor, m.disB[:, cols],
                                     ALU.mult, ALU.mult).then_inc(a.s_part, 1)
        elif part == 1:
            dve.wait_ge(a.s_part, b * KC + (h + 1))
            dve.tensor_tensor(agg[:, h, cols], agg[:, h, cols], a.part[:, h, :], ALU.add).then_inc(s_evac, 1)
        elif second:
            dve.wait_ge(s_evac, b * KC + (KC + h + 1))
            dve.bn_stats(m.stats1[:, h, bass.ds(s, 1), :].rearrange("p a b -> p (a b)"), agg[:, h, cols])

    def v_head(dve, b):
        columns(dve, 0, 0)
        dve.wait_ge(s_col, b + a.run + 1)
        for g in range(GPS):
            one_hots(dve, b, 0, g)
        columns(dve, 1, 1)

    def v_step(dve, b, s, par):
        dve.wait_ge(s_col, b + a.run + 2)
        for g in range(GPS):
            one_hots(dve, b + 1, 1 - par, g)
            if 5 <= g <= 7 and not (isinstance(s, int) and s == 0):
                add_half(dve, b - 1, s - 1, 1, g - 5)
            if g >= GPS - 3:
                add_half(dve, b, s, 0, g - (GPS - 3))
            if g == 20 and not (isinstance(s, int) and s == NSB - 2):
                columns(dve, par, s + 2)

    def v_tail(dve, b):
        for s, h in ((NSB - 2, 1), (NSB - 1, 0), (NSB - 1, 1)):
            for part in range(3):
                add_half(dve, b + s, s, h, part)
        dve.wait_ge(s_evac, b * KC + (NSB + 1) * KC)

    def build_group(pe, b, g):
        pe.wait_ge(s_oh, b * GPS + (g + 1))
        pe.wait_ge(s_adj, b * GPS + (g + 1))
        for i in range(GRP):
            last = pe.matmul(m.ps[:, g % RING, i * KEYS:(i + 1) * KEYS], oh_r[:, g % RING, i, :],
                             oh_k[:, g % RING, i, 0:KEYS], start=True, stop=True)
        last.then_inc(s_used, 1)

    def t_head(pe, b):
        for g in range(GPS):
            build_group(pe, b, g)

    def dense(pe, b, par, build):
        pe.wait_ge(s_adj, b * GPS + (GPS + RING))
        g, n = 0, 0
        for h in range(KC):
            pe.wait_ge(s_evac, b * KC + (h + 1))
            for c in range(NT):
                for half in range(2):
                    if build and n % EVERY == 0 and g < GPS:
                        build_group(pe, b + 1, g)
                        g += 1
                    n += 1
                    last = pe.matmul(m.ps[:, RING + h, 0:SB], table[:, c, half * C + h * P:half * C + (h + 1) * P],
                                     m.adj[:, par, c, :], start=c == 0 and half == 0, stop=c == NT - 1 and half == 1)
            last.then_inc(s_half, 1)

    def t_step(pe, b, s, par):
        dense(pe, b, par, True)

    def t_tail(pe, b):
        dense(pe, b + (NSB - 1), 0, False)

    def evacuate(act, b, par, g):
        act.wait_ge(s_used, b * GPS + (RING + g + 1))
        act.activation(m.adj[:, par, :, GRP * WIN * g:GRP * WIN * (g + 1)].rearrange("r c w -> r w c"),
                       m.ps[:, g % RING, 0:GRP * KEYS].rearrange("r (w c) -> r w c", c=NT), ACT.Copy).then_inc(s_adj, 1)

    def a_head(act, b):
        for g in range(GPS):
            evacuate(act, b, 0, g)

    def a_step(act, b, s, par):
        act.wait_ge(s_half, b * KC + KC)
        for g in range(GPS):
            evacuate(act, b + 1, 1 - par, g)

    def a_tail(act, b):
        act.wait_ge(s_half, b * KC + (NSB + 1) * KC)

    with nc.Block() as block:
        @block.vector
        def _(dve):
            chain_on(m, dve)(dve.memset(m.step16[:, :], 0.0))
            if not second:
                dve.sem_inc(s_evac, KC)
            walk(dve, "vector", v_head, v_step, v_tail)

        @block.tensor
        def _(pe):
            if not second:
                pe.sem_inc(s_used, RING)
                pe.sem_inc(s_half, KC)
            walk(pe, "tensor", t_head, t_step, t_tail)

        @block.scalar
        def _(act):
            if not second:
                act.sem_inc(s_adj, RING)
            walk(act, "scalar", a_head, a_step, a_tail)

        @block.gpsimd
        def _(pool):
            nlev = pool.value_load(m.levels[0:1, 0:1], min_val=1, max_val=NTE + 1)
            with pool.Fori(0, nlev) as level:
                run = pool.snap(level + nlev) if second else level
                with pool.If(nlev > 1):
                    between_levels(pool, "gpsimd", run)


def f32r_halves(dve, act, raw, hi, lo, s_in, n_in, s_hi, n_hi, s_lo):
    if act is not None:
        act.wait_ge(s_in, n_in)
        act.activation(hi, raw, ACT.Copy).then_inc(s_hi, 1)
    if dve is not None:
        dve.wait_ge(s_hi, n_hi)
        dve.tensor_tensor(lo, raw, hi.bitcast(F32), ALU.subtract).then_inc(s_lo, 1)


def linear1(nc, m, a):
    take = Place(m, m.work)
    w_hi, w_lo = take("w1_hi", [P, KC, IC], F32R), take("w1_lo", [P, KC, IC], F32R)
    raw = m.at("w1_raw", m.r3, [P, KC, IC], F32)
    u_hi, u_lo = take("u_hi", [P, 2, KC, SB], F32R), take("u_lo", [P, 2, KC, SB], F32R)
    S = m.sem
    s_raw, s_whi, s_wlo = S("d_raw"), S("d_whi"), S("d_wlo")
    s_uhi, s_ulo = S("d_uhi"), S("d_ulo")
    s_mm = S("d_mm")
    s_h = S("d_h")
    h_of = (m.h01, m.h23)
    cols = lambda s: bass.ds(s * SB, SB)

    with nc.Block() as block:
        @block.sync
        def _(sp):
            sp.dma_start(raw[:, :, :], a.w1t.rearrange("(k p) f -> p k f", p=P)).then_inc(s_raw, 16)

        def walk(eng, step):
            for n in range(3):
                step(n, n % 2, n)
            with eng.Fori(1, (NSB - 3) // 2) as k:
                step(2 * k + 1, 1, None)
                step(2 * k + 2, 0, None)
            for n in range(NSB - 2, NSB):
                step(n, n % 2, n)

        @block.vector
        def _(dve):
            for h in h_of:
                dve.memset(h[:, :, N:NP_], 0.0)
            f32r_halves(dve, None, raw[:, :, :], w_hi[:, :, :], w_lo[:, :, :], None, 0, s_whi, 1, s_wlo)

            def low(s, par):
                dve.wait_ge(s_uhi, s + 1)
                dve.tensor_tensor(u_lo[:, par, :, :], m.agg1[:, :, cols(s)], u_hi[:, par, :, :].bitcast(F32),
                                  ALU.subtract).then_inc(s_ulo, 1)

            def stats(s):
                dve.wait_ge(s_h, 2 * s + (2 + 4))
                for f in range(KI):
                    dve.bn_stats(m.stats1[:, f, bass.ds(s, 1), :].rearrange("p a b -> p (a b)"), h_of[f // 2][:, f % 2, cols(s)])

            def step(s, par, n):
                if n is None or n + 1 < NSB:
                    low(s + 1, 1 - par)
                if n is None or n >= 1:
                    stats(s - 1)
            low(0, 0)
            walk(dve, step)
            stats(NSB - 1)

        @block.scalar
        def _(act):
            act.sem_inc(s_h, 4)
            f32r_halves(None, act, raw[:, :, :], w_hi[:, :, :], w_lo[:, :, :], s_raw, 16, s_whi, 1, s_wlo)

            def high(s, par):
                act.wait_ge(s_mm, 2 * s + 2)
                act.activation(u_hi[:, par, :, :], m.agg1[:, :, cols(s)], ACT.Copy).then_inc(s_uhi, 1)

            def evacuate(s, par):
                for q in range(2):
                    act.wait_ge(s_mm, 2 * s + (q + 1 + 4))
                    act.activation(h_of[q][:, :, cols(s)], m.ps[:, 4 * par + 2 * q:4 * par + 2 * q + 2, 0:SB], ACT.Copy).then_inc(s_h, 1)

            def step(s, par, n):
                if n is None or n + 1 < NSB:
                    high(s + 1, 1 - par)
                if n is None or n >= 1:
                    evacuate(s - 1, 1 - par)
            high(0, 0)
            walk(act, step)
            evacuate(NSB - 1, 0)

        @block.tensor
        def _(pe):
            pe.sem_inc(s_mm, 4)
            pe.wait_ge(s_wlo, 1)

            def step(s, par, n):
                pe.wait_ge(s_ulo, s + 1)
                for q in range(2):
                    pe.wait_ge(s_h, 2 * s + (q + 1))
                    for f in (2 * q, 2 * q + 1):
                        for n, (w, u) in enumerate(((w_hi, u_hi), (w_lo, u_hi), (w_hi, u_lo))):
                            for k in range(KC):
                                last = pe.matmul(m.ps[:, 4 * par + f, 0:SB], w[:, k, f * P:(f + 1) * P], u[:, par, k, :],
                                                 start=n == 0 and k == 0, stop=n == 2 and k == KC - 1)
                    last.then_inc(s_mm, 1)
            walk(pe, step)


def chain_on(m, dve):
    def link(ins):
        m.chained += 1
        ins.then_inc(m.s_chain, 1)
        dve.wait_ge(m.s_chain, m.chained)
    return link


def norm1(nc, m, a):
    take = Place(m, m.work)
    m.w2_hi, m.w2_lo = take("w2_hi", [P, KI, C], F32R), take("w2_lo", [P, KI, C], F32R)
    m.work2 = take.next
    raw, wabs = take("w2_raw", [P, KI, C], F32), take("w2_abs", [P, KI, C], F32)
    take = Place(m, m.r3 - 2048)
    mv, ve, mh = take("n1_mv", [P, KI, 2], F32), take("n1_ve", [P, KI], F32), take("n1_mh", [P, KI], F32)
    rs, tmp = take("n1_rs", [P, KI], F32), take("n1_tmp", [P, KI], F32)
    bnd, babs = take("n1_bnd", [P, KI], F32), take("n1_babs", [P, KI], F32)
    top, one = take("n1_top", [P, 1], F32), take("n1_one", [1, 4], F32)
    S = m.sem
    s_raw, s_whi, s_wlo, s_ve, s_mh, s_rs = S("e_raw"), S("e_whi"), S("e_wlo"), S("e_ve"), S("e_mh"), S("e_rs")
    s_b, s_bp, s_top, s_topT, s_sc, s_scB = S("e_b"), S("e_bp"), S("e_top"), S("e_topT"), S("e_sc"), S("e_scB")
    with nc.Block() as block:
        @block.sync
        def _(sp):
            sp.dma_start(raw[:, :, :], a.w2t.rearrange("(k p) c -> p k c", p=P)).then_inc(s_raw, 16)

        @block.scalar
        def _(act):
            f32r_halves(None, act, raw[:, :, :], m.w2_hi[:, :, :], m.w2_lo[:, :, :], s_raw, 16, s_whi, 1, s_wlo)

        @block.gpsimd
        def _(pool):
            pool.memset(mh[:, :], -0.5).then_inc(s_mh, 1)
            pool.wait_ge(s_mh, 1)
            pool.wait_ge(s_ve, 1)
            pool.tensor_tensor(rs[:, :], ve[:, :], mh[:, :], ALU.pow).then_inc(s_rs, 1)

        @block.tensor
        def _(pe):
            pe.wait_ge(s_b, 1)
            for c in range(KC):
                for k in range(KI):
                    last = pe.matmul(m.ps[:, 0, c:c + 1], wabs[:, k, c * P:(c + 1) * P], bnd[:, k:k + 1],
                                     start=k == 0, stop=k == KI - 1)
            last.then_inc(s_bp, 1)
            pe.wait_ge(s_top, 1)
            pe.transpose(m.ps[:1, 1, 0:P], top[:, :], m.id32[:, :]).then_inc(s_topT, 1)
            pe.wait_ge(s_sc, 1)
            pe.matmul(m.ps[:, 2, 0:1], m.ones[0:1, :], one[0:1, 3:4], start=True, stop=True).then_inc(s_scB, 1)

        @block.vector
        def _(dve):
            link = chain_on(m, dve)
            for f in range(KI):
                last = dve.bn_aggr(mv[:, f, :], m.stats1[:, f, :, :].rearrange("p a b -> p (a b)"))
            link(last)
            dve.tensor_scalar(ve[:, :], mv[:, :, 1], EPS, None, ALU.add).then_inc(s_ve, 1)
            dve.wait_ge(s_raw, 16)
            link(dve.scalar_tensor_tensor(wabs[:, :, :], raw[:, :, :], -1.0, raw[:, :, :], ALU.mult, ALU.max))
            link(dve.scalar_tensor_tensor(babs[:, :], m.bn_b1[:, :], -1.0, m.bn_b1[:, :], ALU.mult, ALU.max))
            link(dve.scalar_tensor_tensor(bnd[:, :], m.bn_g1[:, :], -1.0, m.bn_g1[:, :], ALU.mult, ALU.max))
            dve.scalar_tensor_tensor(bnd[:, :], bnd[:, :], float(N) ** 0.5 + 1.0, babs[:, :], ALU.mult, ALU.add).then_inc(s_b, 1)
            dve.wait_ge(s_bp, 1)
            dve.tensor_reduce(top[:, :], m.ps[:, 0, 0:KC], AX.X, ALU.max).then_inc(s_top, 1)
            dve.wait_ge(s_topT, 1)
            link(dve.tensor_reduce(one[:, 0:1], m.ps[:1, 1, 0:P], AX.X, ALU.max))
            link(dve.tensor_scalar(one[:, 1:2], one[:, 0:1], 1e-6, 1.0 / 32768.0, ALU.max, ALU.mult))
            link(dve.reciprocal(one[:, 2:3], one[:, 1:2]))
            dve.tensor_scalar(one[:, 3:4].bitcast(I32), one[:, 2:3].bitcast(I32), 0x7F800000, None, ALU.bitwise_and).then_inc(s_sc, 1)
            dve.wait_ge(s_scB, 1)
            link(dve.tensor_copy(m.scale2[:, :], m.ps[:, 2, 0:1]))
            link(dve.tensor_scalar(m.disP[:, :], m.disP[:, :], m.scale2[:, 0:1], None, ALU.mult))
            dve.wait_ge(s_rs, 1)
            link(dve.tensor_tensor(m.aff_a1[:, :], m.bn_g1[:, :], rs[:, :], ALU.mult))
            link(dve.tensor_tensor(tmp[:, :], mv[:, :, 0], m.aff_a1[:, :], ALU.mult))
            link(dve.tensor_tensor(m.aff_b1[:, :], m.bn_b1[:, :], tmp[:, :], ALU.subtract))
            f32r_halves(dve, None, raw[:, :, :], m.w2_hi[:, :, :], m.w2_lo[:, :, :], None, 0, s_whi, 1, s_wlo)


def linear2(nc, m, a):
    norm1(nc, m, a)
    take = Place(m, m.work2)
    h_hi, h_lo = take("h_hi", [P, 2, KI, P], F32R), take("h_lo", [P, 2, KI, P], F32R)
    S = m.sem
    s_r = S("f_r")
    s_hhi, s_split = S("f_hhi"), S("f_split")
    s_mm = S("f_mm")
    s_thi = S("f_thi")
    s_tlo = S("f_tlo")
    h_of = (m.h01, m.h23)

    def walk(step):
        def run(eng):
            for n in range(4):
                step(eng, n, n, n // 2, n)
            with eng.Fori(1, NT // 4 - 1) as k:
                for q in range(4):
                    step(eng, 4 * k + q, q, 2 * k + q // 2, None)
            for n in range(NT // 4 * 4 - 4, NT):
                step(eng, n, n % 4, n // 2, n)
        return run

    with nc.Block() as block:
        @block.vector
        def _(dve):
            dve.sem_inc(s_tlo, 4)

            def split(i, par, pair):
                cols = bass.ds(i * P, P)
                dve.wait_ge(s_r, pair + 1)
                dve.wait_ge(s_mm, i + 1)
                for q in range(2):
                    last = dve.tensor_copy(h_hi[:, par, 2 * q:2 * q + 2, :], h_of[q][:, :, cols])
                last.then_inc(s_hhi, 1)
                dve.wait_ge(s_hhi, i + 1)
                for q in range(2):
                    last = dve.tensor_tensor(h_lo[:, par, 2 * q:2 * q + 2, :], h_of[q][:, :, cols],
                                             h_hi[:, par, 2 * q:2 * q + 2, :].bitcast(F32), ALU.subtract)
                last.then_inc(s_split, 1)

            def low(i, bank):
                dve.wait_ge(s_thi, i + 1)
                dve.scalar_tensor_tensor(m.table2[:, bass.ds(i, 1), C:].rearrange("p a c -> p (a c)"), m.ps[:, bank, 0:C],
                                         m.disP[:, bass.ds(i, 1)], m.table2[:, bass.ds(i, 1), :C].rearrange("p a c -> p (a c)"),
                                         ALU.mult, ALU.subtract).then_inc(s_tlo, 1)

            def step(dve, i, q, pair, n):
                if n is None or n + 1 < NT:
                    split(i + 1, (q + 1) % 2, pair + q % 2)
                if n is None or n >= 1:
                    low(i - 1, (q - 1) % 4)
            split(0, 0, 0)
            walk(step)(dve)
            low(NT - 1, (NT - 1) % 4)

        @block.scalar
        def _(act):
            def relu(pair, width):
                for f in range(KI):
                    h = h_of[f // 2][:, f % 2, bass.ds(pair * 2 * P, width)]
                    last = act.activation(h, h, ACT.Relu, bias=m.aff_b1[:, f:f + 1], scale=m.aff_a1[:, f:f + 1])
                last.then_inc(s_r, 1)

            def high(i, bank):
                act.wait_ge(s_mm, i + (1 + 2))
                act.activation(m.table2[:, bass.ds(i, 1), :C].rearrange("p a c -> p (a c)"), m.ps[:, bank, 0:C], ACT.Copy,
                               scale=m.disP[:, bass.ds(i, 1)]).then_inc(s_thi, 1)

            def step(act, i, q, pair, n):
                if q % 2 == 0 and (n is None or n + 2 < NT):
                    relu(pair + 1, 2 * P if n is None or n + 3 < NT else P)
                if n is None or n >= 1:
                    high(i - 1, (q - 1) % 4)
            relu(0, 2 * P)
            walk(step)(act)
            high(NT - 1, (NT - 1) % 4)

        @block.tensor
        def _(pe):
            pe.sem_inc(s_mm, 2)

            def step(pe, i, q, pair, n):
                pe.wait_ge(s_split, i + 1)
                pe.wait_ge(s_tlo, i + 1)
                for k, (h, w) in enumerate(((h_hi, m.w2_hi), (h_hi, m.w2_lo), (h_lo, m.w2_hi))):
                    for f in range(KI):
                        last = pe.matmul(m.ps[:, q, 0:C], h[:, q % 2, f, :], w[:, f, :],
                                         start=k == 0 and f == 0, stop=k == 2 and f == KI - 1)
                last.then_inc(s_mm, 1)
            walk(step)(pe)
    self_loops(nc, m, "l2", m.table2, m.agg2, 1.0)


def finish_gnn(nc, m, a):
    x = m.x
    x1 = m.at("x1_sb", m.r2, [P, NT, C], F32)
    take = Place(m, m.work)
    mv2 = take("mv2", [P, KC, 2], F32)
    e2, ve2, mh, rs2 = take("e2", [P, 1], F32), take("ve2", [P, KC], F32), take("mh2", [P, NT], F32), take("rs2", [P, KC], F32)
    a2, b2, tmp = take("a2", [P, KC], F32), take("b2c", [P, KC], F32), take("tmp2", [P, KC], F32)
    shift = take("shift", [P, NT], F32)
    ACTQ = 3
    RX, NG = 4, 7
    xn = take("xn", [P, RX, 2, C], F32)
    st3, mv3 = take("st3", [P, NT, 6], F32), take("mv3", [P, NT, 2], F32)
    ve3, rs3, shift3 = take("ve3", [P, NT], F32), take("rs3", [P, NT], F32), take("shift3", [P, NT], F32)
    S = m.sem
    s_x, s_xt, s_ve, s_mh, s_rs, s_aff, s_v, s_tr, s_sum = (S("g_" + n) for n in ("x", "xt", "ve", "mh", "rs", "aff", "v", "tr", "sum"))
    s_shift, s_xn, s_h, s_x1, s_ve3, s_rs3, s_shift3, s_out = (S("g_" + n) for n in ("shift", "xn", "h", "x1", "ve3", "rs3", "shift3", "out"))
    pairs = [(2 * g, min(2, NT - 2 * g)) for g in range(-(-NT // 2))]
    eights = [(8 * g, min(8, NT - 8 * g)) for g in range(-(-NT // 8))]
    with nc.Block() as block:
        @block.sync
        def _(sp):
            for i in range(6):
                sp.dma_start(x[:, 8 * i:8 * i + 8, :],
                             a.x[1024 * i:1024 * (i + 1), :].rearrange("(t p) c -> p t c", p=P)).then_inc(s_x, 16)
            sp.wait_ge(s_xt, 1)
            sp.dma_start(x[:LAST, NT - 1, :], a.x[(NT - 1) * P:N, :]).then_inc(s_x, 16)
            gw = m.gw
            sp.dma_start(gw.w1_raw[:, :, :], a.fw1.rearrange("(k p) h -> p k h", p=P)).then_inc(gw.s_w1, 16)
            sp.dma_start(gw.wg_raw[:, :, :], a.fwg.rearrange("(k p) e -> p k e", p=P)).then_inc(gw.s_par, 16)
            sp.dma_start(gw.bg[:, :], bass.AP(a.fbg.tensor, 0, [[0, P], [1, NEXP]])).then_inc(gw.s_par, 16)
            sp.dma_start(gw.wd_raw0[:, :, :], a.fwd[:, 0:P, :].rearrange("e p c -> p e c")).then_inc(gw.s_wd0, 16)
            for t0, k in eights:
                sp.wait_ge(s_x1, (t0 + k + 1) // 2)
                sp.dma_start(m.x1_dram[t0 * P:(t0 + k) * P, 0:C].rearrange("(t p) c -> p t c", p=P), x1[:, t0:t0 + k, :]).then_inc(s_out, 16)
            sp.wait_ge(s_out, 16 * len(eights))

        @block.gpsimd
        def _(pool):
            pool.memset(mh[:, :], -0.5).then_inc(s_mh, 1)
            pool.wait_ge(s_mh, 1)
            pool.wait_ge(s_ve, 1)
            pool.tensor_tensor(rs2[:, :], ve2[:, :], mh[:, :KC], ALU.pow).then_inc(s_rs, 1)
            for q in range(NT // NG):
                t = slice(q * NG, (q + 1) * NG)
                pool.wait_ge(s_ve3, q + 1)
                pool.tensor_tensor(rs3[:, t], ve3[:, t], mh[:, t], ALU.pow).then_inc(s_rs3, 1)

        @block.vector
        def _(dve):
            link = chain_on(m, dve)
            dve.memset(x[:, NT - 1, :], 0.0).then_inc(s_xt, 1)
            link(dve.tensor_tensor(e2[:, :], m.scale2[:, :], m.scale2[:, :], ALU.mult))
            for h in range(KC):
                last = dve.bn_aggr(mv2[:, h, :], m.stats1[:, h, :, :].rearrange("p a b -> p (a b)"))
            link(last)
            dve.scalar_tensor_tensor(ve2[:, :], e2[:, 0:1].to_broadcast([P, KC]), EPS, mv2[:, :, 1], ALU.mult, ALU.add).then_inc(s_ve, 1)
            dve.scalar_tensor_tensor(shift[:, :], m.mean[:, :], -1.0, m.rstd[:, :], ALU.mult, ALU.mult).then_inc(s_shift, 1)
            dve.wait_ge(s_rs, 1)
            link(dve.tensor_tensor(a2[:, :], m.bn_g2[:, :], rs2[:, :], ALU.mult))
            link(dve.tensor_tensor(tmp[:, :], mv2[:, :, 0], a2[:, :], ALU.mult))
            dve.tensor_tensor(b2[:, :], m.bn_b2[:, :], tmp[:, :], ALU.subtract).then_inc(s_aff, 1)

            def add(g):
                t0, k = pairs[g]
                dve.wait_ge(s_xn, g + 1)
                dve.wait_ge(s_tr, g + 1)
                dve.tensor_tensor(xn[:, g % RX, 0:k, :], xn[:, g % RX, 0:k, :],
                                  m.ps[:, g % 4, 0:k * C].rearrange("p (t c) -> p t c", c=C), ALU.add).then_inc(s_h, 1)

            def residual(g):
                t0, k = pairs[g]
                dve.wait_ge(s_h, g + 1)
                dve.scalar_tensor_tensor(x1[:, t0:t0 + k, :], xn[:, g % RX, 0:k, :], 0.0, x[:, t0:t0 + k, :],
                                         ALU.max, ALU.add).then_inc(s_x1, 1)

            def stats(g):
                t0, k = pairs[g]
                dve.wait_ge(s_x1, g + 1)
                for i in range(t0, t0 + k):
                    dve.bn_stats(st3[:, i, :], x1[:, i, :]).then_inc(s_sum, 1)
                    if (i + 1) % NG == 0:
                        t = slice(i + 1 - NG, i + 1)
                        dve.wait_ge(s_sum, i + 1)
                        for n in range(i + 1 - NG, i + 1):
                            last = dve.bn_aggr(mv3[:, n, :], st3[:, n, :])
                        link(last)
                        dve.tensor_scalar(ve3[:, t], mv3[:, t, 1], EPS, None, ALU.add).then_inc(s_ve3, 1)
                        if NG < i + 1 <= NG * (ACTQ + 1):
                            shifts((i + 1) // NG - 2)

            def shifts(q):
                t = slice(q * NG, (q + 1) * NG)
                dve.wait_ge(s_rs3, q + 1)
                dve.scalar_tensor_tensor(shift3[:, t], mv3[:, t, 0], -1.0, rs3[:, t], ALU.mult, ALU.mult).then_inc(s_shift3, 1)

            for g in range(len(pairs) + 2):
                if g < len(pairs):
                    add(g)
                if 1 <= g <= len(pairs):
                    residual(g - 1)
                if g >= 2:
                    stats(g - 2)
            dve.wait_ge(s_tr, len(pairs))
            dve.wait_ge(s_rs3, NT // NG)
            for i in range(ACTQ * NG, NT):
                dve.tensor_scalar(m.rows[:, i, 0:C], x1[:, i, :], mv3[:, i, 0:1], rs3[:, i:i + 1], ALU.subtract, ALU.mult)

        @block.scalar
        def _(act):
            def normalise(q):
                act.wait_ge(s_shift3, q + 1)
                for i in range(q * NG, (q + 1) * NG):
                    act.activation(m.rows[:, i, 0:C], x1[:, i, :], ACT.Identity, bias=shift3[:, i:i + 1], scale=rs3[:, i:i + 1])

            act.wait_ge(s_shift, 1)
            act.wait_ge(s_x, 16 * 7)
            for g, (t0, k) in enumerate(pairs):
                if g >= RX:
                    act.wait_ge(s_x1, g + 1 - RX)
                for i in range(k):
                    last = act.activation(xn[:, g % RX, i, :], x[:, t0 + i, :], ACT.Identity,
                                          bias=shift[:, t0 + i:t0 + i + 1], scale=m.rstd[:, t0 + i:t0 + i + 1])
                last.then_inc(s_xn, 1)
                if g == 0:
                    act.wait_ge(s_aff, 1)
                for h in range(KC):
                    v = m.agg2[:, h, t0 * P:(t0 + k) * P]
                    last = act.activation(v, v, ACT.Identity, bias=b2[:, h:h + 1], scale=a2[:, h:h + 1])
                last.then_inc(s_v, 1)
            act.wait_ge(s_tr, len(pairs))
            for q in range(ACTQ):
                normalise(q)

        @block.tensor
        def _(pe):
            for g, (t0, k) in enumerate(pairs):
                pe.wait_ge(s_v, g + 1)
                if g >= 4:
                    pe.wait_ge(s_x1, g - 3)
                for i in range(k):
                    for h in range(KC):
                        last = pe.transpose(m.ps[:, g % 4, i * C + h * P:i * C + (h + 1) * P],
                                            m.agg2[:, h, (t0 + i) * P:(t0 + i + 1) * P], m.id32[:, :])
                last.then_inc(s_tr, 1)



def ffn_scales(m, a):
    raw = m.at("w1f_abs", m.r1 + NP_ * 4, [P, KC, HID], F32)
    wd_raw = m.at("wd_abs", m.r1 + NP_ * 4 + 8192, [P, 2, NEXP, C], F32)
    take = Place(m, m.r1 + NP_ * 4 + 8192 * 3)
    asum, bsum, babs = take("asum", [P, KH], F32), take("bsum", [P, KH], F32), take("babs", [P, KH], F32)
    rb, inv, prod, low = take("rb", [P, KH], F32), take("inv", [P, KH], F32), take("prod", [P, KH], F32), take("low", [P, 1], F32)
    one = take("one_f", [1, 1], F32)
    wg_abs, gsum = take("wg_abs", [P, KH, NEXP], F32), take("gsum", [P, KH], F32)
    S = m.sem
    s_w1, s_b1, s_wd, s_abs, s_free, s_wabs, s_bp, s_low, s_lowT, s_one, s_G = (
        S("h_" + n) for n in ("w1", "b1", "wd", "abs", "free", "wabs", "bp", "low", "lowT", "one", "G"))
    s_wdp = [S("h_wd0"), S("h_wd1")]
    def on_sync(nc, sp):
        sp.dma_start(raw[:, :, :], a.fw1.rearrange("(k p) h -> p k h", p=P)).then_inc(s_w1, 16)
        with nc.allow_non_contiguous_dma("the bias of the hidden units to partitions"):
            sp.dma_start(m.b1f[:, :], a.fb1.rearrange("(k p) -> p k", p=P)).then_inc(s_b1, 16)
        sp.dma_start(wg_abs[:, :, :], a.fwg.rearrange("(k p) e -> p k e", p=P)).then_inc(s_b1, 16)

    def on_scalar(act):
        def load(k):
            act.dma_start(wd_raw[:, k % 2, :, :], a.fwd[:, k * P:(k + 1) * P, :].rearrange("e p c -> p e c")).then_inc(s_wdp[k % 2], 16)

        load(0)
        load(1)
        for k in range(KH):
            act.wait_ge(s_wdp[k % 2], 16 * (k // 2 + 1))
            act.activation(wd_raw[:, k % 2, :, :], wd_raw[:, k % 2, :, :], ACT.Abs, accum_out=asum[:, k:k + 1]).then_inc(s_free, 1)
            if k + 2 < KH:
                act.wait_ge(s_free, k + 1)
                load(k + 2)

    def on_tensor(pe):
        pe.wait_ge(s_wabs, 1)
        for h in range(KH):
            for k in range(KC):
                last = pe.matmul(m.ps[:, 0, h:h + 1], raw[:, k, h * P:(h + 1) * P], m.ones[:, 0:1], start=k == 0, stop=k == KC - 1)
        last.then_inc(s_bp, 1)
        pe.wait_ge(s_low, 1)
        pe.transpose(m.ps[:1, 1, 0:P], low[:, :], m.id32[:, :]).then_inc(s_lowT, 1)
        pe.wait_ge(s_one, 1)
        pe.matmul(m.ps[:, 2, 0:1], m.ones[0:1, :], one[0:1, 0:1], start=True, stop=True).then_inc(s_G, 1)

    def on_vector(dve):
        link = chain_on(m, dve)

        def power(out, bound):
            link(dve.tensor_scalar(out, bound, 1e-6, 1.0 / 32768.0, ALU.max, ALU.mult))
            link(dve.reciprocal(out, out))
            link(dve.tensor_scalar(out.bitcast(I32), out.bitcast(I32), 0x7F800000, None, ALU.bitwise_and))

        def inverse(out, x):
            link(dve.tensor_scalar(out.bitcast(I32), x.bitcast(I32), -1.0, float(254 << 23), ALU.mult, ALU.add))

        dve.wait_ge(s_w1, 16)
        dve.scalar_tensor_tensor(raw[:, :, :], raw[:, :, :], -1.0, raw[:, :, :], ALU.mult, ALU.max).then_inc(s_wabs, 1)
        dve.wait_ge(s_b1, 32)
        link(dve.scalar_tensor_tensor(wg_abs[:, :, :], wg_abs[:, :, :], -1.0, wg_abs[:, :, :], ALU.mult, ALU.max))
        link(dve.tensor_reduce(gsum[:, :], wg_abs[:, :, :], AX.X, ALU.add))
        link(dve.scalar_tensor_tensor(babs[:, :], m.b1f[:, :], -1.0, m.b1f[:, :], ALU.mult, ALU.max))
        dve.wait_ge(s_bp, 1)
        link(dve.scalar_tensor_tensor(bsum[:, :], m.ps[:, 0, 0:KH], 16.25, babs[:, :], ALU.mult, ALU.add))
        power(rb[:, :], bsum[:, :])
        dve.wait_ge(s_free, KH)
        link(dve.tensor_tensor(asum[:, :], asum[:, :], gsum[:, :], ALU.add))
        power(m.alpha[:, :], asum[:, :])
        link(dve.tensor_tensor(prod[:, :], rb[:, :], m.alpha[:, :], ALU.mult))
        dve.tensor_reduce(low[:, :], prod[:, :], AX.X, ALU.min).then_inc(s_low, 1)
        dve.wait_ge(s_lowT, 1)
        dve.tensor_reduce(one[:, :], m.ps[:1, 1, 0:P], AX.X, ALU.min).then_inc(s_one, 1)
        dve.wait_ge(s_G, 1)
        link(dve.tensor_copy(low[:, :], m.ps[:, 2, 0:1]))
        inverse(m.inv_g[:, :], low[:, :])
        inverse(inv[:, :], m.alpha[:, :])
        link(dve.tensor_scalar(m.beta[:, :], inv[:, :], low[:, 0:1], None, ALU.mult))

    return on_sync, on_scalar, on_tensor, on_vector


def ffn(nc, m, a):
    take = Place(m, m.r2)
    m.wd_hi, m.wd_lo = take("wd_hi", [P, NEXP, KH, C], F16), take("wd_lo", [P, NEXP, KH, C], F16)
    m.w1_hi, m.w1_lo = take("fw1_hi", [P, KC, HID], F32R), take("fw1_lo", [P, KC, HID], F32R)
    m.xt_hi, m.xt_lo = take("xt_hi", [P, 2, KC, 2 * P], F32R), take("xt_lo", [P, 2, KC, 2 * P], F32R)
    m.hf = take("hf", [P, KH, 2 * P], F32)
    m.h_hi, m.h_lo = take("h16_hi", [P, 2, KH, 2 * P], F16), take("h16_lo", [P, 2, KH, 2 * P], F16)
    m.work3 = take.next
    m.hidden = hidden_semaphores(m, "hid")
    gate(nc, m, a)
    experts(nc, m, a)



UB = 4
DVE_HIGH = (2, 6)
TBANK = 4


def hidden_semaphores(m, tag):
    u = Names()
    u.first = 0
    u.tr = m.sem(f"{tag}_tr")
    u.xthi = m.sem(f"{tag}_xthi")
    u.xt = m.sem(f"{tag}_xt")
    u.up = m.sem(f"{tag}_up")
    u.gelu = m.sem(f"{tag}_gelu")
    u.hi = m.sem(f"{tag}_hi")
    u.own = m.sem(f"{tag}_own")
    u.split = m.sem(f"{tag}_split")
    u.done = m.sem(f"{tag}_done")
    return u


def pe_ahead(pe, u):
    pe.sem_inc(u.up, 2 * KH)
    pe.sem_inc(u.done, 2)


def dve_ahead(dve, u):
    dve.sem_inc(u.xt, 1)
    dve.sem_inc(u.split, KH)


def pe_transpose(pe, m, u, i, rows, ntile):
    pe.wait_ge(u.xt, i + (u.first + 1))
    for j in range(ntile):
        for k in range(KC):
            last = pe.transpose(m.ps[:, TBANK, k * 2 * P + j * P:k * 2 * P + (j + 1) * P], rows(j, k), m.id32[:, :])
    last.then_inc(u.tr, 1)


def pe_hidden(pe, m, u, i, par, ntile, between):
    n = ntile * P
    i = i + u.first
    pe.wait_ge(u.xt, i + 2)
    for h in range(KH):
        pe.wait_ge(u.gelu, i * KH + (h + 1))
        for q, (w, x) in enumerate(((m.w1_hi, m.xt_hi), (m.w1_lo, m.xt_hi), (m.w1_hi, m.xt_lo))):
            for k in range(KC):
                last = pe.matmul(m.ps[:, h % UB, 0:n], w[:, k, h * P:(h + 1) * P], x[:, par, k, 0:n],
                                 start=q == 0 and k == 0, stop=q == 2 and k == KC - 1)
        last.then_inc(u.up, 1)
        if h in between:
            between[h]()


def act_xt(act, m, u, i, par, ntile):
    i = i + u.first
    act.wait_ge(u.tr, i + 1)
    act.wait_ge(u.up, i * KH + KH)
    act.activation(m.xt_hi[:, par, :, 0:ntile * P],
                   m.ps[:, TBANK, :].rearrange("p (k n) -> p k n", k=KC)[:, :, 0:ntile * P], ACT.Copy).then_inc(u.xthi, 1)


def act_hidden(act, m, u, i, par, ntile, nxt):
    n = ntile * P
    i = i + u.first

    def high(h):
        if h in DVE_HIGH:
            return
        act.wait_ge(u.gelu, i * KH + (h + 1 + UB))
        act.activation(m.h_hi[:, par, h, 0:n], m.hf[:, h, 0:n], ACT.Copy, scale=m.beta[:, h:h + 1]).then_inc(u.hi, 1)

    for h in range(KH):
        act.wait_ge(u.up, i * KH + (h + 1 + 2 * KH))
        act.wait_ge(u.split, i * KH + (h + 1))
        act.activation(m.hf[:, h, 0:n], m.ps[:, h % UB, 0:n], ACT.Gelu, bias=m.b1f[:, h:h + 1]).then_inc(u.gelu, 1)
        if h == 0:
            act.wait_ge(u.done, i + 1)
        else:
            high(h - 1)
        if h == 3 and nxt:
            act_xt(act, m, u, i + 1 - u.first, 1 - par, nxt)
    high(KH - 1)


def dve_xt(dve, m, u, i, par, ntile):
    i = i + u.first
    dve.wait_ge(u.xthi, i + 1)
    dve.tensor_tensor(m.xt_lo[:, par, :, 0:ntile * P],
                      m.ps[:, TBANK, :].rearrange("p (k n) -> p k n", k=KC)[:, :, 0:ntile * P],
                      m.xt_hi[:, par, :, 0:ntile * P].bitcast(F32), ALU.subtract).then_inc(u.xt, 1)


def dve_hidden(dve, m, u, i, par, ntile, nxt, between={}):
    n = ntile * P
    i = i + u.first
    highs = 0
    for h in range(KH):
        if h in DVE_HIGH:
            dve.wait_ge(u.gelu, i * KH + (h + 1 + UB))
            dve.tensor_scalar(m.h_hi[:, par, h, 0:n], m.hf[:, h, 0:n], m.beta[:, h:h + 1], None, ALU.mult).then_inc(u.own, 1)
            dve.wait_ge(u.own, i * len(DVE_HIGH) + (DVE_HIGH.index(h) + 1))
        else:
            highs += 1
            dve.wait_ge(u.hi, i * (KH - len(DVE_HIGH)) + highs)
        dve.scalar_tensor_tensor(m.h_lo[:, par, h, 0:n], m.hf[:, h, 0:n], m.beta[:, h:h + 1], m.h_hi[:, par, h, 0:n],
                                 ALU.mult, ALU.subtract).then_inc(u.split, 1)
        if h == 3 and nxt:
            dve_xt(dve, m, u, i + 1 - u.first, 1 - par, nxt)
        if h in between:
            between[h]()


REG = 6400
MAXT = 56
assert MAXT * P >= N + NEXP * (P - 1) - P + 1 and REG >= NP_ + P
RW = C + 1


def gate_weights(m):
    g = Names()
    g.w1_raw = m.at("fw1_raw", m.r4, [P, KC, HID], F32)
    g.wg_raw = m.at("wg_raw", m.r4 + 8192, [P, KH, NEXP], F32)
    g.wd_raw0 = m.at("wd_raw0", m.r5 - 8192 - 512, [P, NEXP, C], F32)
    g.bg = m.at("bgB", m.r5 - 512, [P, NEXP], F32)
    g.s_w1, g.s_par, g.s_wd0 = m.sem("i_w1"), m.sem("i_par"), m.sem("i_wd0")
    return g


def gate(nc, m, a):
    rows = m.rows
    w1_raw, wg_raw, bg = m.gw.w1_raw, m.gw.wg_raw, m.gw.bg
    s_w1, s_par = m.gw.s_w1, m.gw.s_par
    wd_raw = (m.gw.wd_raw0, m.at("wd_raw1", m.work, [P, NEXP, C], F32))
    assert m.work3 <= m.r5 - 8192 - 512
    take = Place(m, m.work + 8192)
    wg = take("wg", [P, KH, 2 * NEXP], F16)
    tri, ones16 = take("tri", [P, P], F16), take("ones16", [P, P], F16)
    prio, run = take("prio", [P, NEXP], F32), take("run", [P, NEXP], F32)
    lg, mx = take("lg", [P, NT + 1, NEXP], F32), take("mx", [P, 2], F32)
    now = take("now", [P, 2, NEXP], F32)
    sc, best = take("sc", [P, 2, NEXP], F32), take("best", [P, 2], F32)
    oh, ohf = take("oh", [P, 2, 2, NEXP], F16), take("ohf", [P, 2, 2, NEXP], F32)
    rk, slotf, slot = take("rk", [P, 2, NEXP], F32), take("slotf", [P, 2], F32), take("slot", [P, NT], I32)
    valid = take("valid", [P, 1], F32)
    padi, padf, prow = take("padi", [P, NEXP + 1], I32), take("padf", [P, NEXP + 1], F32), take("prow", [P, RW], F32)
    pcol = take("pcol", [P, 1], F32)
    stage = take("stage", [P, 2, 2, C], F32)
    tv, tb, nt, nti = take("tv", [1, 64], F32), take("tb", [1, NEXP + 1], F32), take("nt", [1, NEXP], F32), take("nti", [1, NEXP], I32)
    te, tr_, tq, tf = take("te", [1, 64], F32), take("tr_", [1, 64], F32), take("tq", [1, 64], F32), take("tf", [1, 64], F32)
    u = m.hidden
    S = m.sem
    (s_w1hi, s_w1lo, s_wdhi, s_wdfree, s_const, s_oh, s_rk, s_slot, s_scat,
     s_init, s_choose, s_place, s_lgfree, s_pads, s_stage, s_ex, s_prob, s_store) = (S("i_" + n) for n in (
         "w1hi", "w1lo", "wdhi", "wdfree", "const", "oh", "rk", "slot", "scat",
         "init", "choose", "place", "lgfree", "pads", "stage", "ex", "prob", "store"))
    s_wd = (m.gw.s_wd0, S("i_wd1"))
    NPAIR = NT // 2
    LB, RB = (5, 7), 6
    tiles = lambda i: 1 if i == NPAIR else 2

    def steps(eng, step):
        for i in range(4):
            step(eng, i, i % 2, i)
        with eng.Fori(2, NPAIR // 2 - 1) as k:
            step(eng, 2 * k, 0, None)
            step(eng, 2 * k + 1, 1, None)
        for i in range(NPAIR - 2, NPAIR + 1):
            step(eng, i, i % 2, i)

    with nc.Block() as block:
        @block.sync
        def _(sp):
            for k in range(1, KH):
                if k >= 2:
                    sp.wait_ge(s_wdfree, k - 1)
                sp.dma_start(wd_raw[k % 2][:, :, :], a.fwd[:, k * P:(k + 1) * P, :].rearrange("e p c -> p e c")).then_inc(s_wd[k % 2], 16)
            sp.wait_ge(s_prob, 1)
            with nc.allow_non_contiguous_dma("each token's probability behind its row of x1"):
                sp.dma_start(m.x1_dram[:, C:C + 1].rearrange("(t p) c -> p t c", p=P), m.probs[:, :].unsqueeze(2)).then_inc(s_store, 16)
            sp.wait_ge(s_store, 16)

        @block.gpsimd
        def _(pool):
            pool.iota(rows[:, :, RW - 1].bitcast(I32), [[P, NT]], base=0, channel_multiplier=1).then_inc(s_const, 1)
            pool.memset(tri[:, :], 1.0).then_inc(s_init, 1)
            pool.memset(prow[:, :], 0.0).then_inc(s_init, 1)
            pool.memset(valid[:, :], 1.0).then_inc(s_init, 1)
            pool.wait_ge(s_init, 3)
            pool.affine_select(out=tri[:, :], in_=tri[:, :], compare_op=ALU.is_ge, fill=0.0,
                               base=-1, pattern=[[1, P]], channel_multiplier=-1).then_inc(s_const, 1)
            pool.affine_select(out=valid[:, :], in_=valid[:, :], compare_op=ALU.is_ge, fill=0.0,
                               base=LAST - 1, pattern=[[0, 1]], channel_multiplier=-1).then_inc(s_const, 1)
            pool.iota(prow[:, RW - 1:RW].bitcast(I32), [[0, 1]], base=N, channel_multiplier=0).then_inc(s_const, 1)
            pool.iota(prio[:, :], [[-1, NEXP]], base=NEXP, channel_multiplier=0, allow_small_or_imprecise_dtypes=True).then_inc(s_const, 1)
            for t in (run, m.reg_base):
                pool.iota(t[:, :], [[REG, NEXP]], base=0, channel_multiplier=0, allow_small_or_imprecise_dtypes=True).then_inc(s_const, 1)
            pool.iota(padf[:, :], [[REG, NEXP + 1]], base=0, channel_multiplier=1, allow_small_or_imprecise_dtypes=True).then_inc(s_const, 1)
            pool.iota(pcol[:, :], [[0, 1]], base=0, channel_multiplier=1, allow_small_or_imprecise_dtypes=True).then_inc(s_const, 1)
            pool.iota(tv[:, :], [[1, 64]], base=0, channel_multiplier=0, allow_small_or_imprecise_dtypes=True).then_inc(s_const, 1)
            pool.wait_ge(s_const, 10)
            LATE = 6
            for i in range(NPAIR + 1 + LATE):
                if i <= NPAIR:
                    n = tiles(i)
                    if i >= 2:
                        pool.wait_ge(u.tr, i - 1)
                    pool.tensor_copy(stage[:, i % 2, 0:n, :], rows[:, 2 * i:2 * i + n, 0:C]).then_inc(s_stage, 1)
                if i >= LATE:
                    pool.wait_ge(s_slot, i - LATE + 1)
                    for t in range(2 * (i - LATE), 2 * (i - LATE) + tiles(i - LATE)):
                        n = P if t < NT - 1 else LAST
                        pool.indirect_dma_start(m.sorted_rows, bass.IndirectOffsetOnAxis(ap=slot[:n, t:t + 1], axis=0),
                                                rows[:n, t, :], None).then_inc(s_scat, 16)
            pool.wait_ge(s_pads, 1)
            for e in range(NEXP + 1):
                pool.indirect_dma_start(m.sorted_rows, bass.IndirectOffsetOnAxis(ap=padi[:, e:e + 1], axis=0),
                                        prow[:, :], None).then_inc(s_scat, 16)
            pool.wait_ge(s_scat, 16 * (NT + NEXP + 1))

        @block.tensor
        def _(pe):
            pe_ahead(pe, u)
            pe.wait_ge(s_w1lo, 1)
            pe.wait_ge(s_const, 10)

            def logits(pe, i, par, ntile):
                pe.wait_ge(u.split, i * KH + 2 * KH)
                pe.wait_ge(s_lgfree, i + 1)
                for j in range(ntile):
                    for n, h in enumerate((m.h_hi, m.h_lo)):
                        for k in range(KH):
                            last = pe.matmul(m.ps[:, LB[par], j * 16:j * 16 + 2 * NEXP], h[:, par, k, j * P:(j + 1) * P], wg[:, k, :],
                                             start=n == 0 and k == 0, stop=n == 1 and k == KH - 1)
                last.then_inc(u.done, 1)

            def ranks(pe, i, par, ntile, n):
                pe.wait_ge(s_oh, i + 1)
                if n is None or n > 3:
                    pe.wait_ge(s_slot, i)
                pe.matmul(m.ps[:, RB, 0:NEXP], tri[:, :], oh[:, par, 0, :], start=True, stop=True)
                if ntile == 2:
                    pe.matmul(m.ps[:, RB, NEXP:2 * NEXP], tri[:, :], oh[:, par, 1, :], start=True, stop=False)
                    pe.matmul(m.ps[:, RB, NEXP:2 * NEXP], ones16[:, :], oh[:, par, 0, :], start=False, stop=True)
                for j in range(ntile):
                    last = pe.matmul(m.ps[:, RB, 2 * NEXP:3 * NEXP], ones16[:, :], oh[:, par, j, :], start=j == 0, stop=j == ntile - 1)
                last.then_inc(s_rk, 1)

            def transpose(i, par, ntile):
                pe.wait_ge(s_stage, i + 1)
                pe_transpose(pe, m, u, i, lambda j, k: stage[:, par, j, k * P:(k + 1) * P], ntile)

            def step(pe, i, par, n):
                nxt = 0 if n == NPAIR else 1 if n == NPAIR - 1 else 2

                between = {}
                if nxt:
                    between[1] = lambda: transpose(i + 1, 1 - par, nxt)
                if n is None or n >= 3:
                    between[4] = lambda: ranks(pe, i - 3, 1 - par, 2, n)
                pe_hidden(pe, m, u, i, par, 1 if n == NPAIR else 2, between)
                if n is None or n >= 1:
                    logits(pe, i - 1, 1 - par, 2)

            transpose(0, 0, 2)
            steps(pe, step)
            logits(pe, NPAIR, 0, 1)
            for i in range(NPAIR - 2, NPAIR + 1):
                ranks(pe, i, i % 2, tiles(i), i)

        @block.scalar
        def _(act):
            act.sem_inc(u.gelu, UB)
            act.wait_ge(s_w1, 16)
            act.activation(m.w1_hi[:, :, :], w1_raw[:, :, :], ACT.Copy).then_inc(s_w1hi, 1)
            act.wait_ge(s_par, 48)
            act.activation(wg[:, :, 0:NEXP], wg_raw[:, :, :], ACT.Copy).then_inc(s_w1hi, 1)
            act_xt(act, m, u, 0, 0, 2)

            def step(act, i, par, n):
                nxt = 0 if n == NPAIR else 1 if n == NPAIR - 1 else 2
                act_hidden(act, m, u, i, par, 1 if n == NPAIR else 2, nxt)
                if n is not None and n < 4:
                    for k in (2 * n, 2 * n + 1):
                        act.wait_ge(s_wd[k % 2], 16 * (k // 2 + 1))
                        act.activation(m.wd_hi[:, :, k, :], wd_raw[k % 2][:, :, :], ACT.Copy, scale=m.alpha[:, k:k + 1]).then_inc(s_wdhi, 1)
            steps(act, step)
            act.wait_ge(s_oh, NPAIR + 1)
            act.activation(lg[:, 0:NT, :], lg[:, 0:NT, :], ACT.Exp).then_inc(s_ex, 1)

        @block.vector
        def _(dve):
            link = chain_on(m, dve)
            dve_ahead(dve, u)
            dve.sem_inc(s_lgfree, 2)
            link(dve.memset(ones16[:, :], 1.0))
            dve.wait_ge(s_par, 32)
            dve.tensor_tensor(wg_raw[:, :, :], wg_raw[:, :, :], m.alpha[:, :].unsqueeze(2).to_broadcast([P, KH, NEXP]),
                              ALU.mult).then_inc(s_par, 16)
            dve.wait_ge(s_w1hi, 1)
            link(dve.tensor_tensor(m.w1_lo[:, :, :], w1_raw[:, :, :], m.w1_hi[:, :, :].bitcast(F32), ALU.subtract))
            dve.wait_ge(s_w1hi, 2)
            dve.tensor_tensor(wg[:, :, NEXP:], wg_raw[:, :, :], wg[:, :, 0:NEXP], ALU.subtract).then_inc(s_w1lo, 1)
            dve.wait_ge(s_const, 10)

            def choose(dve, i, par, ntile):
                t = slice(0, ntile)

                def lk(ins, n):
                    ins.then_inc(s_choose, 1)
                    dve.wait_ge(s_choose, i * 7 + n)
                dve.wait_ge(u.done, i + 3)
                ps = m.ps[:, LB[par], 0:16 * ntile].rearrange("p (t e) -> p t e", e=16)
                l = now[:, t, :]
                lk(dve.scalar_tensor_tensor(l, ps[:, :, 0:NEXP], m.inv_g[:, 0:1], bg[:, :].unsqueeze(1).to_broadcast([P, ntile, NEXP]), ALU.mult, ALU.add), 1)
                lk(dve.scalar_tensor_tensor(l, ps[:, :, NEXP:], m.inv_g[:, 0:1], l, ALU.mult, ALU.add), 2)
                lk(dve.tensor_reduce(mx[:, t], l, AX.X, ALU.max), 3)
                lk(dve.tensor_tensor(l, l, mx[:, t].unsqueeze(2).to_broadcast([P, ntile, NEXP]), ALU.subtract), 4)
                dve.sem_inc(s_lgfree, 1)
                dve.tensor_copy(lg[:, bass.ds(2 * i, ntile), :], l)
                lk(dve.scalar_tensor_tensor(sc[:, t, :], l, 0.0, prio[:, :].unsqueeze(1).to_broadcast([P, ntile, NEXP]), ALU.is_equal, ALU.mult), 5)
                lk(dve.tensor_reduce(best[:, t], sc[:, t, :], AX.X, ALU.max), 6)
                lk(dve.tensor_tensor(ohf[:, par, t, :], sc[:, t, :], best[:, t].unsqueeze(2).to_broadcast([P, ntile, NEXP]), ALU.is_equal), 7)
                if ntile == 1:
                    link(dve.tensor_scalar(ohf[:, par, 0, :], ohf[:, par, 0, :], valid[:, 0:1], None, ALU.mult))
                dve.tensor_copy(oh[:, par, t, :], ohf[:, par, t, :]).then_inc(s_oh, 1)

            def place(dve, i, par, ntile):
                t = slice(0, ntile)

                def lk(ins, n):
                    ins.then_inc(s_place, 1)
                    dve.wait_ge(s_place, i * 4 + n)
                dve.wait_ge(s_rk, i + 1)
                lk(dve.tensor_tensor(rk[:, t, :], m.ps[:, RB, 0:NEXP * ntile].rearrange("p (t e) -> p t e", e=NEXP),
                                     run[:, :].unsqueeze(1).to_broadcast([P, ntile, NEXP]), ALU.add), 1)
                lk(dve.tensor_tensor(rk[:, t, :], rk[:, t, :], ohf[:, par, t, :], ALU.mult), 2)
                lk(dve.tensor_tensor(run[:, :], run[:, :], m.ps[:, RB, 2 * NEXP:3 * NEXP], ALU.add), 3)
                lk(dve.tensor_reduce(slotf[:, t], rk[:, t, :], AX.X, ALU.add), 4)
                dve.tensor_copy(slot[:, bass.ds(2 * i, ntile)], slotf[:, t]).then_inc(s_slot, 1)

            def step(dve, i, par, n):
                nxt = 0 if n == NPAIR else 1 if n == NPAIR - 1 else 2

                between = {}
                if n is None or n >= 4:
                    between[0] = lambda: place(dve, i - 4, par, 2)
                if n is None or n >= 2:
                    between[3] = lambda: choose(dve, i - 2, par, 2)
                dve_hidden(dve, m, u, i, par, 1 if n == NPAIR else 2, nxt, between)
                if n is not None and n < 4:
                    for k in (2 * n, 2 * n + 1):
                        dve.wait_ge(s_wdhi, k + 1)
                        dve.scalar_tensor_tensor(m.wd_lo[:, :, k, :], wd_raw[k % 2][:, :, :], m.alpha[:, k:k + 1],
                                                 m.wd_hi[:, :, k, :], ALU.mult, ALU.subtract).then_inc(s_wdfree, 1)
            dve_xt(dve, m, u, 0, 0, 2)
            steps(dve, step)
            for i in range(NPAIR - 3, NPAIR + 1):
                place(dve, i, i % 2, tiles(i))
                if i < NPAIR - 1:
                    choose(dve, i + 2, i % 2, tiles(i + 2))
            link(dve.tensor_scalar(padf[:, 0:NEXP], run[:, :], pcol[:, 0:1], None, ALU.add))
            dve.tensor_copy(padi[:, :], padf[:, :]).then_inc(s_pads, 1)
            link(dve.tensor_tensor(nt[:, :], run[0:1, :], m.reg_base[0:1, :], ALU.subtract))
            link(dve.tensor_scalar(nt[:, :], nt[:, :], float(P - 1), None, ALU.add))
            link(dve.tensor_copy(nti[:, :], nt[:, :]))
            link(dve.tensor_scalar(nti[:, :], nti[:, :], 7, None, ALU.arith_shift_right))
            link(dve.tensor_copy(nt[:, :], nti[:, :]))
            dve.memset(tb[:, :], 0.0)
            dve.memset(te[:, :], 0.0)
            link(dve.memset(tr_[:, :], 0.0))
            for e in range(NEXP):
                link(dve.tensor_tensor(tb[:, e + 1:e + 2], tb[:, e:e + 1], nt[:, e:e + 1], ALU.add))
                link(dve.tensor_scalar(tq[:, :], tv[:, :], tb[0:1, e + 1:e + 2], None, ALU.is_ge))
                dve.tensor_tensor(te[:, :], te[:, :], tq[:, :], ALU.add)
                link(dve.scalar_tensor_tensor(tr_[:, :], tq[:, :], nt[0:1, e:e + 1], tr_[:, :], ALU.mult, ALU.add))
            link(dve.tensor_tensor(tr_[:, :], tv[:, :], tr_[:, :], ALU.subtract))
            link(dve.tensor_scalar(tf[:, :], te[:, :], float(REG), None, ALU.mult))
            link(dve.scalar_tensor_tensor(tr_[:, :], tr_[:, :], float(P), tf[:, :], ALU.mult, ALU.add))
            link(dve.tensor_scalar(tr_[:, :], tr_[:, :], float(NEXP * REG), None, ALU.min))
            link(dve.tensor_copy(m.tile_row[0:1, :], tr_[:, :]))
            link(dve.tensor_scalar(te[:, :], te[:, :], float(NEXP - 1), None, ALU.min))
            link(dve.tensor_copy(m.tile_exp[0:1, :], te[:, :]))
            dve.wait_ge(s_ex, 1)
            link(dve.tensor_reduce(m.probs[:, :], lg[:, 0:NT, :], AX.X, ALU.add))
            dve.reciprocal(m.probs[:, :], m.probs[:, :]).then_inc(s_prob, 1)


def experts(nc, m, a):
    RB4 = 4
    take = Place(m, m.r1)
    r = take("in_rows", [P, RB4, 2, RW], F32)
    x1t, outt = take("x1_rows", [P, 2, 2, C + 1], F32), take("out_rows", [P, 2, 2, C], F32)
    bd = take("bdB", [P, NEXP, C], F32)
    y = take("y", [P, 2, 2, C], F32)
    assert take.next <= m.r2
    u = m.hidden
    u.first = -(-NT // 2)
    S = m.sem
    s_bd, s_y, s_out, s_used = S("j_bd"), S("j_y"), S("j_out"), S("j_used")
    s_row = [S(f"j_row{q}") for q in range(RB4)]
    s_gx = [S("j_gx0"), S("j_gx1")]
    s_st = [S("j_st0"), S("j_st1")]
    NPAIR = MAXT // 2
    DB = 5

    with nc.Block() as block:
        @block.sync
        def _(sp):
            def load(i, q):
                for j in range(2):
                    at = sp.value_load(m.tile_row[0:1, bass.ds(2 * i + j, 1)], min_val=0, max_val=NEXP * REG)
                    sp.dma_start(r[:, q, j, :], m.sorted_rows[bass.ds(at, P), :]).then_inc(s_row[q], 16)

            for i in range(RB4):
                load(i, i)
            sp.dma_start(bd[:, :, :].rearrange("p e c -> p (e c)"), bass.AP(a.fbd.tensor, 0, [[0, P], [1, NEXP * C]])).then_inc(s_bd, 16)
            with sp.Fori(1, NPAIR // RB4) as k:
                for q in range(RB4):
                    sp.wait_ge(s_used, k * RB4 + (q + 1 - RB4))
                    load(k * RB4 + q, q)
            sp.wait_ge(s_bd, 16)

        @block.gpsimd
        def _(pool):
            for i in range(NPAIR + 1):
                par, q = i % 2, i % RB4
                if i >= 2:
                    pool.wait_ge(s_st[par], 32 * (i // 2))
                    pool.sem_inc(s_used, 1)
                if i < NPAIR:
                    pool.wait_ge(s_row[q], 32 * (i // RB4 + 1))
                    for j in range(2):
                        pool.indirect_dma_start(x1t[:, par, j, :], None, m.x1_dram,
                                                bass.IndirectOffsetOnAxis(ap=r[:, q, j, RW - 1:RW].bitcast(I32), axis=0)).then_inc(s_gx[par], 16)
                if i >= 1:
                    pool.wait_ge(s_out, i)
                    for j in range(2):
                        pool.indirect_dma_start(a.out, bass.IndirectOffsetOnAxis(ap=r[:, (i - 1) % RB4, j, RW - 1:RW].bitcast(I32), axis=0),
                                                outt[:, 1 - par, j, :], None, bounds_check=N - 1, oob_is_err=False).then_inc(s_st[1 - par], 16)
            for par in range(2):
                pool.wait_ge(s_st[par], 32 * (NPAIR // 2))

        @block.tensor
        def _(pe):
            def transpose(i, par, q, uses):
                pe.wait_ge(s_row[q], uses)
                pe_transpose(pe, m, u, i, lambda j, k: r[:, q, j, k * P:(k + 1) * P], 2)

            def down(pe, i, par):
                for j in range(2):
                    e = pe.value_load(m.tile_exp[0:1, bass.ds(2 * i + j, 1)], min_val=0, max_val=NEXP - 1)
                    if j == 0:
                        pe.wait_ge(u.split, KH * i + KH * (u.first + 2))
                    pe.wait_ge(s_y, 2 * i + (j + 1))
                    for k in range(KH):
                        w_hi = m.wd_hi[:, bass.ds(e, 1), k, :].rearrange("p a c -> p (a c)")
                        w_lo = m.wd_lo[:, bass.ds(e, 1), k, :].rearrange("p a c -> p (a c)")
                        for q, (h, w) in enumerate(((m.h_hi, w_hi), (m.h_hi, w_lo), (m.h_lo, w_hi))):
                            last = pe.matmul(m.ps[:, DB + j, 0:C], h[:, par, k, j * P:(j + 1) * P], w,
                                             start=q == 0 and k == 0, stop=q == 2 and k == KH - 1)
                last.then_inc(u.done, 1)

            def step(i, q, k):
                par = q % 2
                pe_hidden(pe, m, u, i, par, 2, {1: lambda: transpose(i + 1, 1 - par, (q + 1) % RB4, k * 32 + 32 * (1 + (q + 1) // RB4))})
                down(pe, i - 1, 1 - par)

            transpose(0, 0, 0, 32)
            pe_hidden(pe, m, u, 0, 0, 2, {1: lambda: transpose(1, 1, 1, 32)})
            with pe.Fori(0, (NPAIR - 2) // RB4) as k:
                for q in range(1, RB4 + 1):
                    step(k * RB4 + q, q, k)
            last = (NPAIR - 2) // RB4
            for q in range(1, NPAIR - 1 - last * RB4):
                step(last * RB4 + q, q, last)
            pe_hidden(pe, m, u, NPAIR - 1, 1, 2, {})
            down(pe, NPAIR - 2, 0)
            down(pe, NPAIR - 1, 1)

        def steps(eng, step):
            step(0, 0, 2, True)
            with eng.Fori(0, (NPAIR - 2) // 2) as k:
                step(2 * k + 1, 1, 2, False)
                step(2 * k + 2, 0, 2, False)
            step(NPAIR - 1, 1, 0, False)

        @block.scalar
        def _(act):
            act_xt(act, m, u, 0, 0, 2)
            steps(act, lambda i, par, nxt, first: act_hidden(act, m, u, i, par, 2, nxt))

        @block.vector
        def _(dve):
            dve.sem_inc(s_y, 2)
            dve.wait_ge(s_bd, 16)

            def results(i, par, k):
                e = [dve.value_load(m.tile_exp[0:1, bass.ds(2 * i + j, 1)], min_val=0, max_val=NEXP - 1) for j in range(2)]
                dve.wait_ge(u.done, i + (u.first + 3))
                dve.wait_ge(s_gx[par], k * 32 + 32)
                for j in range(2):
                    dve.scalar_tensor_tensor(y[:, par, j, :], m.ps[:, DB + j, 0:C], m.inv_g[:, 0:1],
                                             bd[:, bass.ds(e[j], 1), :].rearrange("p a c -> p (a c)"), ALU.mult, ALU.add).then_inc(s_y, 1)
                for j in range(2):
                    dve.wait_ge(s_y, 2 * i + (j + 3))
                    last = dve.scalar_tensor_tensor(outt[:, par, j, :], y[:, par, j, :], x1t[:, par, j, C:C + 1], x1t[:, par, j, 0:C], ALU.mult, ALU.add)
                last.then_inc(s_out, 1)

            dve_xt(dve, m, u, 0, 0, 2)
            dve_hidden(dve, m, u, 0, 0, 2, 2)
            with dve.Fori(0, (NPAIR - 2) // 2) as k:
                dve_hidden(dve, m, u, 2 * k + 1, 1, 2, 2)
                results(2 * k, 0, k)
                dve_hidden(dve, m, u, 2 * k + 2, 0, 2, 2)
                results(2 * k + 1, 1, k)
            dve_hidden(dve, m, u, NPAIR - 1, 1, 2, 0)
            results(NPAIR - 2, 0, NPAIR // 2 - 1)
            results(NPAIR - 1, 1, NPAIR // 2 - 1)


def lay_out(inputs):
    import numpy as np
    named = {"x": inputs["x"], "src": inputs["src"], "dst": inputs["dst"],
             "w1t": inputs["L0_gnn_W1"].T, "g1": inputs["L0_gnn_g1"], "b1": inputs["L0_gnn_b1"],
             "w2t": inputs["L0_gnn_W2"].T, "g2": inputs["L0_gnn_g2"], "b2": inputs["L0_gnn_b2"],
             "fw1": inputs["L0_ffn_W1"], "fb1": inputs["L0_ffn_b1"], "fwg": inputs["L0_ffn_Wg"],
             "fbg": inputs["L0_ffn_bg"], "fwd": inputs["L0_ffn_Wd"], "fbd": inputs["L0_ffn_bd"]}
    return {k: np.ascontiguousarray(v) for k, v in named.items()}


def kernel(**inputs):
    import numpy as np
    import concourse.bacc as bacc
    from concourse.bass_utils import run_bass_kernel_spmd
    arrays = lay_out(inputs)
    nc = bacc.Bacc("TRN2", target_bir_lowering=False, num_devices=1)
    aps = [nc.dram_tensor(name, v.shape, mybir.dt.from_np(v.dtype), kind="ExternalInput").ap()
           for name, v in arrays.items()]
    out = nc.dram_tensor("out", (N, C), F32, kind="ExternalOutput").ap()
    gnn_ffn_kernel(nc, *aps, out)
    nc.compile()
    res = run_bass_kernel_spmd(nc, [arrays], core_ids=[0])
    return np.asarray(res.results[0]["out"])
```
